# Optimizing a Trainium2 kernel written in Bass

```python
import numpy as np
import jax
import jax.numpy as jnp

def _softmax(x, axis=-1):
    return jax.nn.softmax(x, axis=axis)

def _gelu(x):
    return jax.nn.gelu(x, approximate=True)

def _silu(x):
    return jax.nn.silu(x)

def _sigmoid(x):
    return jax.nn.sigmoid(x)

def _layernorm(x, axis=-1, eps=1e-05):
    m = jnp.mean(x, axis=axis, keepdims=True)
    v = jnp.var(x, axis=axis, keepdims=True)
    return (x - m) / jnp.sqrt(v + eps)

def _scatter_add(tgt, idx, src, axis=0):
    return tgt.at[idx].add(src)

def _segment_sum(src, seg, n):
    return jax.ops.segment_sum(src, seg, n)
kernel_name = 'mk_cond_seq_d4_seqx_r4_2608f1'

def setup_inputs(seed: int=0):
    np.random.seed(seed)
    _w = jnp.asarray

    def _rec_inputs():
        import jax
        import jax.numpy as jnp
        _rk = jax.random.key(seed)
        x = -0.0002928 + 1 * jax.random.normal(jax.random.fold_in(_rk, 1), (32, 64, 256), jnp.float32)
        _lenS = 64 - jax.random.randint(jax.random.fold_in(_rk, 7), (32,), 0, max(1, 64 // 4) + 1, jnp.int32)
        _lenS2 = 64 - jax.random.randint(jax.random.fold_in(_rk, 8), (32,), 0, max(1, 64 // 4) + 1, jnp.int32)
        cond_1024 = 0.000887014 + 1.03683 * jax.random.normal(jax.random.fold_in(_rk, 11), (32, 256), jnp.float32)
        _validS = jnp.arange(64)[None, :] < _lenS[:, None]
        _validS2 = jnp.arange(64)[None, :] < _lenS2[:, None]
        _causal = jnp.tril(jnp.ones((64, 64), dtype=bool))
        mask_BxS_bf0 = jnp.logical_not(jnp.ones((32, 64), dtype=bool))
        return (x, cond_1024, mask_BxS_bf0)
    x, cond_1024, mask_BxS_bf0 = _rec_inputs()

    def _L0_cond_setup():
        import math
        import jax, jax.numpy as jnp
        import numpy as np
        H = 256
        NH = 16
        HD = H // NH
        CD = 256
        MLP = 1024
        EPS = 1e-05

        def _layernorm(x):
            mu = jnp.mean(x, axis=-1, keepdims=True)
            var = jnp.var(x, axis=-1, keepdims=True)
            return (x - mu) * jax.lax.rsqrt(var + EPS)

        def _adaln(x, cond, W, b):
            ss = cond @ W.T + b
            scale, shift = jnp.split(ss, 2, axis=-1)
            return _layernorm(x) * (1.0 + scale[:, None, :]) + shift[:, None, :]
        key = jax.random.key(seed)
        ks = jax.random.split(key, 16)
        s = 0.02
        inp = {'x': jax.random.normal(ks[0], (2, 512, H), jnp.float32), 'cond': jax.random.normal(ks[1], (2, CD), jnp.float32), 'key_padding_mask': jnp.zeros((2, 512), dtype=bool), 'w_adaln1': jax.random.normal(ks[2], (2 * H, CD), jnp.float32) * s, 'b_adaln1': jnp.zeros((2 * H,), jnp.float32), 'w_adaln2': jax.random.normal(ks[3], (2 * H, CD), jnp.float32) * s, 'b_adaln2': jnp.zeros((2 * H,), jnp.float32), 'wq': jax.random.normal(ks[4], (H, H), jnp.float32) * s, 'bq': jnp.zeros((H,), jnp.float32), 'wk': jax.random.normal(ks[5], (H, H), jnp.float32) * s, 'bk': jnp.zeros((H,), jnp.float32), 'wv': jax.random.normal(ks[6], (H, H), jnp.float32) * s, 'bv': jnp.zeros((H,), jnp.float32), 'wo': jax.random.normal(ks[7], (H, H), jnp.float32) * s, 'bo': jnp.zeros((H,), jnp.float32), 'w1': jax.random.normal(ks[8], (MLP, H), jnp.float32) * s, 'b1': jnp.zeros((MLP,), jnp.float32), 'w2': jax.random.normal(ks[9], (H, MLP), jnp.float32) * s, 'b2': jnp.zeros((H,), jnp.float32)}
        return inp
    _L0_cond_all = _L0_cond_setup()
    _L0_cond_in = {k: v for k, v in _L0_cond_all.items() if k in ('w_adaln1', 'b_adaln1', 'w_adaln2', 'b_adaln2', 'wq', 'bq', 'wk', 'bk', 'wv', 'bv', 'wo', 'bo', 'w1', 'b1', 'w2', 'b2')}
    del _L0_cond_all

    def _L1_cond_setup():
        import jax, jax.numpy as jnp
        import numpy as np
        B, L = (2, 256)
        D_MODEL = 256
        D_STATE = 32
        D_CONV = 4
        D_INNER = 2 * D_MODEL
        DT_RANK = D_MODEL // 16
        HIDDEN = (int(2 / 3 * 2 * D_MODEL) + 63) // 64 * 64
        COND = D_MODEL

        def _silu(x):
            return x * jax.nn.sigmoid(x)

        def _ln(x, w, b):
            m = x.mean(-1, keepdims=True)
            v = ((x - m) ** 2).mean(-1, keepdims=True)
            return (x - m) / jnp.sqrt(v + 1e-05) * w + b

        def _mamba(h, in_proj_W, conv_w, conv_b, x_proj_W, dt_proj_W, dt_proj_b, A_log, Dp, out_proj_W):
            xz = h @ in_proj_W
            x, z = jnp.split(xz, 2, axis=-1)
            xc = jnp.transpose(x, (0, 2, 1))
            xc = jax.lax.conv_general_dilated(xc, conv_w, (1,), [(D_CONV - 1, 0)], feature_group_count=D_INNER, dimension_numbers=('NCH', 'OIH', 'NCH'))
            x = _silu(jnp.transpose(xc, (0, 2, 1)) + conv_b)
            xdbl = x @ x_proj_W
            dt = jax.nn.softplus(xdbl[..., :DT_RANK] @ dt_proj_W + dt_proj_b)
            Bm = xdbl[..., DT_RANK:DT_RANK + D_STATE]
            Cm = xdbl[..., DT_RANK + D_STATE:]
            A = -jnp.exp(A_log)

            def step(hst, inp):
                dt_t, B_t, C_t, x_t = inp
                dA = jnp.exp(dt_t[:, :, None] * A)
                hst = hst * dA + dt_t[:, :, None] * B_t[:, None, :] * x_t[:, :, None]
                y = jnp.einsum('bdn,bn->bd', hst, C_t)
                return (hst, y)
            h0 = jnp.zeros((h.shape[0], D_INNER, D_STATE), h.dtype)
            seq = (jnp.swapaxes(dt, 0, 1), jnp.swapaxes(Bm, 0, 1), jnp.swapaxes(Cm, 0, 1), jnp.swapaxes(x, 0, 1))
            _, ys = jax.lax.scan(step, h0, seq)
            y = jnp.swapaxes(ys, 0, 1) + Dp * x
            return y * _silu(z) @ out_proj_W
        key = jax.random.key(seed)
        ks = jax.random.split(key, 16)
        f = lambda k, s, sc=0.02: jax.random.normal(k, s, jnp.float32) * sc
        return {'x': jax.random.normal(ks[0], (B, L, D_MODEL), jnp.float32), 'cond': jax.random.normal(ks[1], (B, COND), jnp.float32), 'norm1_w': jnp.ones((D_MODEL,), jnp.float32), 'norm1_b': jnp.zeros((D_MODEL,), jnp.float32), 'norm2_w': jnp.ones((D_MODEL,), jnp.float32), 'norm2_b': jnp.zeros((D_MODEL,), jnp.float32), 'adaln1_W': f(ks[2], (COND, 3 * D_MODEL)), 'adaln1_b': jnp.zeros((3 * D_MODEL,), jnp.float32), 'adaln2_W': f(ks[3], (COND, 3 * D_MODEL)), 'adaln2_b': jnp.zeros((3 * D_MODEL,), jnp.float32), 'in_proj_W': f(ks[4], (D_MODEL, 2 * D_INNER)), 'conv_w': f(ks[5], (D_INNER, 1, D_CONV), 0.1), 'conv_b': jnp.zeros((D_INNER,), jnp.float32), 'x_proj_W': f(ks[6], (D_INNER, DT_RANK + 2 * D_STATE)), 'dt_proj_W': f(ks[7], (DT_RANK, D_INNER), 0.1), 'dt_proj_b': jnp.full((D_INNER,), float(np.log(np.expm1(0.01))), jnp.float32), 'A_log': jnp.log(jnp.tile(jnp.arange(1, D_STATE + 1, dtype=jnp.float32), (D_INNER, 1))), 'Dp': jnp.ones((D_INNER,), jnp.float32), 'out_proj_W': f(ks[8], (D_INNER, D_MODEL)), 'w1': f(ks[9], (D_MODEL, HIDDEN)), 'w2': f(ks[10], (D_MODEL, HIDDEN)), 'w3': f(ks[11], (HIDDEN, D_MODEL))}
    _L1_cond_all = _L1_cond_setup()
    _L1_cond_in = {k: v for k, v in _L1_cond_all.items() if k in ('norm1_w', 'norm1_b', 'norm2_w', 'norm2_b', 'adaln1_W', 'adaln1_b', 'adaln2_W', 'adaln2_b', 'in_proj_W', 'conv_w', 'conv_b', 'x_proj_W', 'dt_proj_W', 'dt_proj_b', 'A_log', 'Dp', 'out_proj_W', 'w1', 'w2', 'w3')}
    del _L1_cond_all

    def _L2_cond_setup():
        import jax, jax.numpy as jnp
        import numpy as np
        D = 256
        H = 16
        HD = 4 * D
        B, T = (4, 256)
        EPS = 1e-05

        def _layernorm(x, g, b):
            mu = jnp.mean(x, axis=-1, keepdims=True)
            var = jnp.mean(jnp.square(x - mu), axis=-1, keepdims=True)
            return (x - mu) * jax.lax.rsqrt(var + EPS) * g + b

        def _attention(x, Wqkv, Wproj, bproj):
            b, t, c = x.shape
            hd = c // H
            qkv = (x @ Wqkv).reshape(b, t, 3, H, hd).transpose(2, 0, 3, 1, 4)
            q, k, v = (qkv[0], qkv[1], qkv[2])
            scale = hd ** (-0.5)
            scores = jnp.einsum('bhqd,bhkd->bhqk', q, k) * scale
            causal = jnp.tril(jnp.ones((t, t), bool))
            scores = jnp.where(causal, scores, -jnp.inf)
            attn = jax.nn.softmax(scores, axis=-1)
            out = jnp.einsum('bhqk,bhkd->bhqd', attn, v)
            out = out.transpose(0, 2, 1, 3).reshape(b, t, c)
            return out @ Wproj + bproj
        key = jax.random.key(seed)
        ks = jax.random.split(key, 12)
        s = 0.02
        return {'x': jax.random.normal(ks[0], (B, T, D), jnp.float32), 'condition': jax.random.normal(ks[1], (B, D), jnp.float32), 'Wqkv': jax.random.normal(ks[2], (D, 3 * D), jnp.float32) * s, 'Wproj': jax.random.normal(ks[3], (D, D), jnp.float32) * s, 'bproj': jnp.zeros((D,), jnp.float32), 'W1': jax.random.normal(ks[4], (D, HD), jnp.float32) * s, 'b1': jnp.zeros((HD,), jnp.float32), 'W2': jax.random.normal(ks[5], (HD, D), jnp.float32) * s, 'b2': jnp.zeros((D,), jnp.float32), 'g1': jnp.ones((D,), jnp.float32), 'be1': jnp.zeros((D,), jnp.float32), 'g2': jnp.ones((D,), jnp.float32), 'be2': jnp.zeros((D,), jnp.float32), 'Wada': jax.random.normal(ks[6], (D, 6 * D), jnp.float32) * s, 'bada': jax.random.normal(ks[7], (6 * D,), jnp.float32) * s}
    _L2_cond_all = _L2_cond_setup()
    _L2_cond_in = {k: v for k, v in _L2_cond_all.items() if k in ('Wqkv', 'Wproj', 'bproj', 'W1', 'b1', 'W2', 'b2', 'g1', 'be1', 'g2', 'be2', 'Wada', 'bada')}
    del _L2_cond_all

    def _L3_cond_setup():
        import jax, jax.numpy as jnp
        import numpy as np
        B, L, D_MODEL, COND = (2, 512, 256, 256)
        D_STATE, EXPAND = (64, 2)
        D_INNER = EXPAND * D_MODEL
        MLP_H = 2 * D_MODEL
        EPS = 1e-05

        def _adaln(x, c, w, b):
            mod = (c @ w + b)[:, None, :]
            shift, scale, gate = jnp.split(mod, 3, axis=-1)
            mu = jnp.mean(x, axis=-1, keepdims=True)
            var = jnp.var(x, axis=-1, keepdims=True)
            normed = (x - mu) * jax.lax.rsqrt(var + EPS) * (1.0 + scale) + shift
            return (normed, gate)

        def _ssm(h, in_w, xproj_w, dt_bias, A_log, Dskip, out_w):
            xz = h @ in_w
            xs, z = jnp.split(xz, 2, axis=-1)
            xs = jax.nn.silu(xs)
            proj = xs @ xproj_w
            dt = jax.nn.softplus(proj[..., :D_INNER] + dt_bias)
            Bm = proj[..., D_INNER:D_INNER + D_STATE]
            Cm = proj[..., D_INNER + D_STATE:]
            A = -jnp.exp(A_log)

            def step(hst, ins):
                dt_t, B_t, C_t, x_t = ins
                dA = jnp.exp(dt_t[:, :, None] * A)
                hst = hst * dA + (dt_t * x_t)[:, :, None] * B_t[:, None, :]
                y_t = jnp.einsum('bds,bs->bd', hst, C_t)
                return (hst, y_t)
            tm = lambda a: jnp.swapaxes(a, 0, 1)
            h0 = jnp.zeros((h.shape[0], D_INNER, D_STATE), h.dtype)
            _, ys = jax.lax.scan(step, h0, (tm(dt), tm(Bm), tm(Cm), tm(xs)))
            y = jnp.swapaxes(ys, 0, 1) + xs * Dskip
            return y * jax.nn.silu(z) @ out_w
        key = jax.random.key(seed)
        ks = jax.random.split(key, 24)
        p = lambda i, shape, s=0.02: jax.random.normal(ks[i], shape, jnp.float32) * s
        inp = {'x': jax.random.normal(ks[0], (B, L, D_MODEL), jnp.float32), 'c': jax.random.normal(ks[1], (B, COND), jnp.float32), 'adaln_mamba_w': p(2, (COND, 3 * D_MODEL)), 'adaln_mamba_b': jnp.zeros((3 * D_MODEL,), jnp.float32), 'adaln_mlp_w': p(3, (COND, 3 * D_MODEL)), 'adaln_mlp_b': jnp.zeros((3 * D_MODEL,), jnp.float32), 'mlp_w1': p(4, (D_MODEL, MLP_H)), 'mlp_w2': p(5, (D_MODEL, MLP_H)), 'mlp_w3': p(6, (MLP_H, D_MODEL))}
        a_init = jnp.log(jnp.tile(jnp.arange(1, D_STATE + 1, dtype=jnp.float32), (D_INNER, 1)))
        for j, pre in enumerate(['fwd', 'bwd']):
            o = 7 + 6 * j
            inp[f'{pre}_in_w'] = p(o, (D_MODEL, 2 * D_INNER))
            inp[f'{pre}_xproj_w'] = p(o + 1, (D_INNER, D_INNER + 2 * D_STATE))
            inp[f'{pre}_dt_bias'] = jnp.zeros((D_INNER,), jnp.float32)
            inp[f'{pre}_A_log'] = a_init
            inp[f'{pre}_D'] = jnp.ones((D_INNER,), jnp.float32)
            inp[f'{pre}_out_w'] = p(o + 2, (D_INNER, D_MODEL))
        return inp
    _L3_cond_all = _L3_cond_setup()
    _L3_cond_in = {k: v for k, v in _L3_cond_all.items() if k in ('adaln_mamba_w', 'adaln_mamba_b', 'adaln_mlp_w', 'adaln_mlp_b', 'mlp_w1', 'mlp_w2', 'mlp_w3', 'fwd_in_w', 'fwd_xproj_w', 'fwd_dt_bias', 'fwd_A_log', 'fwd_D', 'fwd_out_w', 'bwd_in_w', 'bwd_xproj_w', 'bwd_dt_bias', 'bwd_A_log', 'bwd_D', 'bwd_out_w')}
    del _L3_cond_all
    return {'x': x, 'cond_1024': cond_1024, 'mask_BxS_bf0': mask_BxS_bf0, 'L0_cond_w_adaln1': _L0_cond_in['w_adaln1'], 'L0_cond_b_adaln1': _L0_cond_in['b_adaln1'], 'L0_cond_w_adaln2': _L0_cond_in['w_adaln2'], 'L0_cond_b_adaln2': _L0_cond_in['b_adaln2'], 'L0_cond_wq': _L0_cond_in['wq'], 'L0_cond_bq': _L0_cond_in['bq'], 'L0_cond_wk': _L0_cond_in['wk'], 'L0_cond_bk': _L0_cond_in['bk'], 'L0_cond_wv': _L0_cond_in['wv'], 'L0_cond_bv': _L0_cond_in['bv'], 'L0_cond_wo': _L0_cond_in['wo'], 'L0_cond_bo': _L0_cond_in['bo'], 'L0_cond_w1': _L0_cond_in['w1'], 'L0_cond_b1': _L0_cond_in['b1'], 'L0_cond_w2': _L0_cond_in['w2'], 'L0_cond_b2': _L0_cond_in['b2'], 'L1_cond_norm1_w': _L1_cond_in['norm1_w'], 'L1_cond_norm1_b': _L1_cond_in['norm1_b'], 'L1_cond_norm2_w': _L1_cond_in['norm2_w'], 'L1_cond_norm2_b': _L1_cond_in['norm2_b'], 'L1_cond_adaln1_W': _L1_cond_in['adaln1_W'], 'L1_cond_adaln1_b': _L1_cond_in['adaln1_b'], 'L1_cond_adaln2_W': _L1_cond_in['adaln2_W'], 'L1_cond_adaln2_b': _L1_cond_in['adaln2_b'], 'L1_cond_in_proj_W': _L1_cond_in['in_proj_W'], 'L1_cond_conv_w': _L1_cond_in['conv_w'], 'L1_cond_conv_b': _L1_cond_in['conv_b'], 'L1_cond_x_proj_W': _L1_cond_in['x_proj_W'], 'L1_cond_dt_proj_W': _L1_cond_in['dt_proj_W'], 'L1_cond_dt_proj_b': _L1_cond_in['dt_proj_b'], 'L1_cond_A_log': _L1_cond_in['A_log'], 'L1_cond_Dp': _L1_cond_in['Dp'], 'L1_cond_out_proj_W': _L1_cond_in['out_proj_W'], 'L1_cond_w1': _L1_cond_in['w1'], 'L1_cond_w2': _L1_cond_in['w2'], 'L1_cond_w3': _L1_cond_in['w3'], 'L2_cond_Wqkv': _L2_cond_in['Wqkv'], 'L2_cond_Wproj': _L2_cond_in['Wproj'], 'L2_cond_bproj': _L2_cond_in['bproj'], 'L2_cond_W1': _L2_cond_in['W1'], 'L2_cond_b1': _L2_cond_in['b1'], 'L2_cond_W2': _L2_cond_in['W2'], 'L2_cond_b2': _L2_cond_in['b2'], 'L2_cond_g1': _L2_cond_in['g1'], 'L2_cond_be1': _L2_cond_in['be1'], 'L2_cond_g2': _L2_cond_in['g2'], 'L2_cond_be2': _L2_cond_in['be2'], 'L2_cond_Wada': _L2_cond_in['Wada'], 'L2_cond_bada': _L2_cond_in['bada'], 'L3_cond_adaln_mamba_w': _L3_cond_in['adaln_mamba_w'], 'L3_cond_adaln_mamba_b': _L3_cond_in['adaln_mamba_b'], 'L3_cond_adaln_mlp_w': _L3_cond_in['adaln_mlp_w'], 'L3_cond_adaln_mlp_b': _L3_cond_in['adaln_mlp_b'], 'L3_cond_mlp_w1': _L3_cond_in['mlp_w1'], 'L3_cond_mlp_w2': _L3_cond_in['mlp_w2'], 'L3_cond_mlp_w3': _L3_cond_in['mlp_w3'], 'L3_cond_fwd_in_w': _L3_cond_in['fwd_in_w'], 'L3_cond_fwd_xproj_w': _L3_cond_in['fwd_xproj_w'], 'L3_cond_fwd_dt_bias': _L3_cond_in['fwd_dt_bias'], 'L3_cond_fwd_A_log': _L3_cond_in['fwd_A_log'], 'L3_cond_fwd_D': _L3_cond_in['fwd_D'], 'L3_cond_fwd_out_w': _L3_cond_in['fwd_out_w'], 'L3_cond_bwd_in_w': _L3_cond_in['bwd_in_w'], 'L3_cond_bwd_xproj_w': _L3_cond_in['bwd_xproj_w'], 'L3_cond_bwd_dt_bias': _L3_cond_in['bwd_dt_bias'], 'L3_cond_bwd_A_log': _L3_cond_in['bwd_A_log'], 'L3_cond_bwd_D': _L3_cond_in['bwd_D'], 'L3_cond_bwd_out_w': _L3_cond_in['bwd_out_w']}

def reference(x, cond_1024, mask_BxS_bf0, L0_cond_w_adaln1, L0_cond_b_adaln1, L0_cond_w_adaln2, L0_cond_b_adaln2, L0_cond_wq, L0_cond_bq, L0_cond_wk, L0_cond_bk, L0_cond_wv, L0_cond_bv, L0_cond_wo, L0_cond_bo, L0_cond_w1, L0_cond_b1, L0_cond_w2, L0_cond_b2, L1_cond_norm1_w, L1_cond_norm1_b, L1_cond_norm2_w, L1_cond_norm2_b, L1_cond_adaln1_W, L1_cond_adaln1_b, L1_cond_adaln2_W, L1_cond_adaln2_b, L1_cond_in_proj_W, L1_cond_conv_w, L1_cond_conv_b, L1_cond_x_proj_W, L1_cond_dt_proj_W, L1_cond_dt_proj_b, L1_cond_A_log, L1_cond_Dp, L1_cond_out_proj_W, L1_cond_w1, L1_cond_w2, L1_cond_w3, L2_cond_Wqkv, L2_cond_Wproj, L2_cond_bproj, L2_cond_W1, L2_cond_b1, L2_cond_W2, L2_cond_b2, L2_cond_g1, L2_cond_be1, L2_cond_g2, L2_cond_be2, L2_cond_Wada, L2_cond_bada, L3_cond_adaln_mamba_w, L3_cond_adaln_mamba_b, L3_cond_adaln_mlp_w, L3_cond_adaln_mlp_b, L3_cond_mlp_w1, L3_cond_mlp_w2, L3_cond_mlp_w3, L3_cond_fwd_in_w, L3_cond_fwd_xproj_w, L3_cond_fwd_dt_bias, L3_cond_fwd_A_log, L3_cond_fwd_D, L3_cond_fwd_out_w, L3_cond_bwd_in_w, L3_cond_bwd_xproj_w, L3_cond_bwd_dt_bias, L3_cond_bwd_A_log, L3_cond_bwd_D, L3_cond_bwd_out_w):
    import jax
    import jax.numpy as jnp

    def _L0_cond_ref(x, cond, key_padding_mask, w_adaln1, b_adaln1, w_adaln2, b_adaln2, wq, bq, wk, bk, wv, bv, wo, bo, w1, b1, w2, b2):
        import math
        import jax, jax.numpy as jnp
        import numpy as np
        H = 256
        NH = 16
        HD = H // NH
        CD = 256
        MLP = 1024
        EPS = 1e-05

        def _layernorm(x):
            mu = jnp.mean(x, axis=-1, keepdims=True)
            var = jnp.var(x, axis=-1, keepdims=True)
            return (x - mu) * jax.lax.rsqrt(var + EPS)

        def _adaln(x, cond, W, b):
            ss = cond @ W.T + b
            scale, shift = jnp.split(ss, 2, axis=-1)
            return _layernorm(x) * (1.0 + scale[:, None, :]) + shift[:, None, :]
        B, L, D = x.shape
        normed = _adaln(x, cond, w_adaln1, b_adaln1)
        q = (normed @ wq.T + bq).reshape(B, L, NH, HD)
        k = (normed @ wk.T + bk).reshape(B, L, NH, HD)
        v = (normed @ wv.T + bv).reshape(B, L, NH, HD)
        scale = math.sqrt(HD)
        scores = jnp.einsum('blhd,bmhd->bhlm', q, k) / scale
        scores = jnp.where(key_padding_mask[:, None, None, :], -jnp.inf, scores)
        attn = jax.nn.softmax(scores, axis=-1)
        attn_out = jnp.einsum('bhlm,bmhd->blhd', attn, v).reshape(B, L, D)
        x = x + attn_out @ wo.T + bo
        normed = _adaln(x, cond, w_adaln2, b_adaln2)
        h = jax.nn.gelu(normed @ w1.T + b1, approximate=False)
        x = x + h @ w2.T + b2
        return x

    def _L1_cond_ref(x, cond, norm1_w, norm1_b, norm2_w, norm2_b, adaln1_W, adaln1_b, adaln2_W, adaln2_b, in_proj_W, conv_w, conv_b, x_proj_W, dt_proj_W, dt_proj_b, A_log, Dp, out_proj_W, w1, w2, w3):
        import jax, jax.numpy as jnp
        import numpy as np
        B, L = (2, 256)
        D_MODEL = 256
        D_STATE = 32
        D_CONV = 4
        D_INNER = 2 * D_MODEL
        DT_RANK = D_MODEL // 16
        HIDDEN = (int(2 / 3 * 2 * D_MODEL) + 63) // 64 * 64
        COND = D_MODEL

        def _silu(x):
            return x * jax.nn.sigmoid(x)

        def _ln(x, w, b):
            m = x.mean(-1, keepdims=True)
            v = ((x - m) ** 2).mean(-1, keepdims=True)
            return (x - m) / jnp.sqrt(v + 1e-05) * w + b

        def _mamba(h, in_proj_W, conv_w, conv_b, x_proj_W, dt_proj_W, dt_proj_b, A_log, Dp, out_proj_W):
            xz = h @ in_proj_W
            x, z = jnp.split(xz, 2, axis=-1)
            xc = jnp.transpose(x, (0, 2, 1))
            xc = jax.lax.conv_general_dilated(xc, conv_w, (1,), [(D_CONV - 1, 0)], feature_group_count=D_INNER, dimension_numbers=('NCH', 'OIH', 'NCH'))
            x = _silu(jnp.transpose(xc, (0, 2, 1)) + conv_b)
            xdbl = x @ x_proj_W
            dt = jax.nn.softplus(xdbl[..., :DT_RANK] @ dt_proj_W + dt_proj_b)
            Bm = xdbl[..., DT_RANK:DT_RANK + D_STATE]
            Cm = xdbl[..., DT_RANK + D_STATE:]
            A = -jnp.exp(A_log)

            def step(hst, inp):
                dt_t, B_t, C_t, x_t = inp
                dA = jnp.exp(dt_t[:, :, None] * A)
                hst = hst * dA + dt_t[:, :, None] * B_t[:, None, :] * x_t[:, :, None]
                y = jnp.einsum('bdn,bn->bd', hst, C_t)
                return (hst, y)
            h0 = jnp.zeros((h.shape[0], D_INNER, D_STATE), h.dtype)
            seq = (jnp.swapaxes(dt, 0, 1), jnp.swapaxes(Bm, 0, 1), jnp.swapaxes(Cm, 0, 1), jnp.swapaxes(x, 0, 1))
            _, ys = jax.lax.scan(step, h0, seq)
            y = jnp.swapaxes(ys, 0, 1) + Dp * x
            return y * _silu(z) @ out_proj_W
        sc = _silu(cond)
        sh1, s1, g1 = jnp.split(sc @ adaln1_W + adaln1_b, 3, axis=-1)
        sh2, s2, g2 = jnp.split(sc @ adaln2_W + adaln2_b, 3, axis=-1)
        mp = (in_proj_W, conv_w, conv_b, x_proj_W, dt_proj_W, dt_proj_b, A_log, Dp, out_proj_W)
        h = _ln(x, norm1_w, norm1_b)
        h = h * (1.0 + s1[:, None, :]) + sh1[:, None, :]
        fwd = _mamba(h, *mp)
        bwd = jnp.flip(_mamba(jnp.flip(h, 1), *mp), 1)
        x = x + g1[:, None, :] * (fwd + bwd)
        h = _ln(x, norm2_w, norm2_b)
        h = h * (1.0 + s2[:, None, :]) + sh2[:, None, :]
        mlp = _silu(h @ w1) * (h @ w2) @ w3
        return x + g2[:, None, :] * mlp

    def _L2_cond_ref(x, condition, Wqkv, Wproj, bproj, W1, b1, W2, b2, g1, be1, g2, be2, Wada, bada):
        import jax, jax.numpy as jnp
        import numpy as np
        D = 256
        H = 16
        HD = 4 * D
        B, T = (4, 256)
        EPS = 1e-05

        def _layernorm(x, g, b):
            mu = jnp.mean(x, axis=-1, keepdims=True)
            var = jnp.mean(jnp.square(x - mu), axis=-1, keepdims=True)
            return (x - mu) * jax.lax.rsqrt(var + EPS) * g + b

        def _attention(x, Wqkv, Wproj, bproj):
            b, t, c = x.shape
            hd = c // H
            qkv = (x @ Wqkv).reshape(b, t, 3, H, hd).transpose(2, 0, 3, 1, 4)
            q, k, v = (qkv[0], qkv[1], qkv[2])
            scale = hd ** (-0.5)
            scores = jnp.einsum('bhqd,bhkd->bhqk', q, k) * scale
            causal = jnp.tril(jnp.ones((t, t), bool))
            scores = jnp.where(causal, scores, -jnp.inf)
            attn = jax.nn.softmax(scores, axis=-1)
            out = jnp.einsum('bhqk,bhkd->bhqd', attn, v)
            out = out.transpose(0, 2, 1, 3).reshape(b, t, c)
            return out @ Wproj + bproj
        mod = jax.nn.silu(condition) @ Wada + bada
        sh_a, sc_a, gt_a, sh_m, sc_m, gt_m = jnp.split(mod, 6, axis=1)
        xn = _layernorm(x, g1, be1)
        xm = xn * (1.0 + sc_a[:, None, :]) + sh_a[:, None, :]
        x = x + gt_a[:, None, :] * _attention(xm, Wqkv, Wproj, bproj)
        xn = _layernorm(x, g2, be2)
        xm = xn * (1.0 + sc_m[:, None, :]) + sh_m[:, None, :]
        h = jax.nn.gelu(xm @ W1 + b1, approximate=False)
        x = x + gt_m[:, None, :] * (h @ W2 + b2)
        return x

    def _L3_cond_ref(x, c, adaln_mamba_w, adaln_mamba_b, adaln_mlp_w, adaln_mlp_b, mlp_w1, mlp_w2, mlp_w3, fwd_in_w, fwd_xproj_w, fwd_dt_bias, fwd_A_log, fwd_D, fwd_out_w, bwd_in_w, bwd_xproj_w, bwd_dt_bias, bwd_A_log, bwd_D, bwd_out_w):
        import jax, jax.numpy as jnp
        import numpy as np
        B, L, D_MODEL, COND = (2, 512, 256, 256)
        D_STATE, EXPAND = (64, 2)
        D_INNER = EXPAND * D_MODEL
        MLP_H = 2 * D_MODEL
        EPS = 1e-05

        def _adaln(x, c, w, b):
            mod = (c @ w + b)[:, None, :]
            shift, scale, gate = jnp.split(mod, 3, axis=-1)
            mu = jnp.mean(x, axis=-1, keepdims=True)
            var = jnp.var(x, axis=-1, keepdims=True)
            normed = (x - mu) * jax.lax.rsqrt(var + EPS) * (1.0 + scale) + shift
            return (normed, gate)

        def _ssm(h, in_w, xproj_w, dt_bias, A_log, Dskip, out_w):
            xz = h @ in_w
            xs, z = jnp.split(xz, 2, axis=-1)
            xs = jax.nn.silu(xs)
            proj = xs @ xproj_w
            dt = jax.nn.softplus(proj[..., :D_INNER] + dt_bias)
            Bm = proj[..., D_INNER:D_INNER + D_STATE]
            Cm = proj[..., D_INNER + D_STATE:]
            A = -jnp.exp(A_log)

            def step(hst, ins):
                dt_t, B_t, C_t, x_t = ins
                dA = jnp.exp(dt_t[:, :, None] * A)
                hst = hst * dA + (dt_t * x_t)[:, :, None] * B_t[:, None, :]
                y_t = jnp.einsum('bds,bs->bd', hst, C_t)
                return (hst, y_t)
            tm = lambda a: jnp.swapaxes(a, 0, 1)
            h0 = jnp.zeros((h.shape[0], D_INNER, D_STATE), h.dtype)
            _, ys = jax.lax.scan(step, h0, (tm(dt), tm(Bm), tm(Cm), tm(xs)))
            y = jnp.swapaxes(ys, 0, 1) + xs * Dskip
            return y * jax.nn.silu(z) @ out_w
        h, gate = _adaln(x, c, adaln_mamba_w, adaln_mamba_b)
        h_fwd = _ssm(h, fwd_in_w, fwd_xproj_w, fwd_dt_bias, fwd_A_log, fwd_D, fwd_out_w)
        h_bwd = jnp.flip(_ssm(jnp.flip(h, 1), bwd_in_w, bwd_xproj_w, bwd_dt_bias, bwd_A_log, bwd_D, bwd_out_w), 1)
        x = x + gate * (h_fwd + h_bwd)
        h, gate = _adaln(x, c, adaln_mlp_w, adaln_mlp_b)
        mlp_out = jax.nn.silu(h @ mlp_w1) * (h @ mlp_w2) @ mlp_w3
        return x + gate * mlp_out
    x = _L0_cond_ref(x, cond_1024, mask_BxS_bf0, L0_cond_w_adaln1, L0_cond_b_adaln1, L0_cond_w_adaln2, L0_cond_b_adaln2, L0_cond_wq, L0_cond_bq, L0_cond_wk, L0_cond_bk, L0_cond_wv, L0_cond_bv, L0_cond_wo, L0_cond_bo, L0_cond_w1, L0_cond_b1, L0_cond_w2, L0_cond_b2)
    x = _L1_cond_ref(x, cond_1024, L1_cond_norm1_w, L1_cond_norm1_b, L1_cond_norm2_w, L1_cond_norm2_b, L1_cond_adaln1_W, L1_cond_adaln1_b, L1_cond_adaln2_W, L1_cond_adaln2_b, L1_cond_in_proj_W, L1_cond_conv_w, L1_cond_conv_b, L1_cond_x_proj_W, L1_cond_dt_proj_W, L1_cond_dt_proj_b, L1_cond_A_log, L1_cond_Dp, L1_cond_out_proj_W, L1_cond_w1, L1_cond_w2, L1_cond_w3)
    x = _L2_cond_ref(x, cond_1024, L2_cond_Wqkv, L2_cond_Wproj, L2_cond_bproj, L2_cond_W1, L2_cond_b1, L2_cond_W2, L2_cond_b2, L2_cond_g1, L2_cond_be1, L2_cond_g2, L2_cond_be2, L2_cond_Wada, L2_cond_bada)
    x = _L3_cond_ref(x, cond_1024, L3_cond_adaln_mamba_w, L3_cond_adaln_mamba_b, L3_cond_adaln_mlp_w, L3_cond_adaln_mlp_b, L3_cond_mlp_w1, L3_cond_mlp_w2, L3_cond_mlp_w3, L3_cond_fwd_in_w, L3_cond_fwd_xproj_w, L3_cond_fwd_dt_bias, L3_cond_fwd_A_log, L3_cond_fwd_D, L3_cond_fwd_out_w, L3_cond_bwd_in_w, L3_cond_bwd_xproj_w, L3_cond_bwd_dt_bias, L3_cond_bwd_A_log, L3_cond_bwd_D, L3_cond_bwd_out_w)
    return x

_drawn_inputs = setup_inputs


def setup_inputs(seed=0):
    import zlib

    import numpy as np

    out = dict(_drawn_inputs(seed))
    spreads = {'L0_cond_b_adaln1': (0.0, 0.1),
     'L0_cond_b_adaln2': (0.0, 0.1),
     'L0_cond_bq': (0.0, 0.1),
     'L0_cond_bk': (0.0, 0.1),
     'L0_cond_bv': (0.0, 0.1),
     'L0_cond_bo': (0.0, 0.1),
     'L0_cond_b1': (0.0, 0.1),
     'L0_cond_b2': (0.0, 0.1),
     'L1_cond_norm1_w': (1.0, 0.2),
     'L1_cond_norm1_b': (0.0, 0.1),
     'L1_cond_norm2_w': (1.0, 0.2),
     'L1_cond_norm2_b': (0.0, 0.1),
     'L1_cond_adaln1_b': (0.0, 0.1),
     'L1_cond_adaln2_b': (0.0, 0.1),
     'L1_cond_conv_b': (0.0, 0.1),
     'L1_cond_dt_proj_b': (-4.600165843963623, 0.2),
     'L1_cond_Dp': (1.0, 0.2),
     'L2_cond_bproj': (0.0, 0.1),
     'L2_cond_b1': (0.0, 0.1),
     'L2_cond_b2': (0.0, 0.1),
     'L2_cond_g1': (1.0, 0.2),
     'L2_cond_be1': (0.0, 0.1),
     'L2_cond_g2': (1.0, 0.2),
     'L2_cond_be2': (0.0, 0.1),
     'L3_cond_adaln_mamba_b': (0.0, 0.1),
     'L3_cond_adaln_mlp_b': (0.0, 0.1),
     'L3_cond_fwd_dt_bias': (0.0, 0.1),
     'L3_cond_fwd_D': (1.0, 0.2),
     'L3_cond_bwd_dt_bias': (0.0, 0.1),
     'L3_cond_bwd_D': (1.0, 0.2)}
    factors = {}
    for name, (base, spread) in spreads.items():
        noise = np.random.default_rng([zlib.crc32(name.encode()), seed]).standard_normal(out[name].shape)
        drawn = base * np.exp(spread * noise) if base else spread * noise
        out[name] = jnp.asarray(drawn.astype(out[name].dtype))
    for name, factor in factors.items():
        out[name] = (out[name] * factor).astype(out[name].dtype)
    return out
```

```python
from contextlib import ExitStack

import numpy as np

import concourse.bass as bass
from concourse import mybir

P = 128
D = 256
KC = D // P
BATCH, SEQ = 32, 64
TOKENS = BATCH * SEQ
T = 512
NBLK = TOKENS // T
BB = T // SEQ
PAIRS = BB // 2
TT = T // P
HEADS, HD = 16, 16
HPC = P // HD
MLP = 1024
DI = 512
DC = DI // P
UN = 4
CREDIT = 16
EPS = 1e-5

VECTORS = [
    ("L0_cond_b_adaln1", 4), ("L0_cond_b_adaln2", 4), ("L0_cond_bq", 2), ("L0_cond_bk", 2),
    ("L0_cond_bv", 2), ("L0_cond_bo", 2), ("L0_cond_b1", 8), ("L0_cond_b2", 2),
    ("L1_cond_norm1_w", 2), ("L1_cond_norm1_b", 2), ("L1_cond_norm2_w", 2), ("L1_cond_norm2_b", 2),
    ("L1_cond_adaln1_b", 6), ("L1_cond_adaln2_b", 6), ("L1_cond_conv_b", 4),
    ("L1_cond_dt_proj_b", 4), ("L1_cond_Dp", 4),
    ("L2_cond_bproj", 2), ("L2_cond_b1", 8), ("L2_cond_b2", 2), ("L2_cond_g1", 2),
    ("L2_cond_be1", 2), ("L2_cond_g2", 2), ("L2_cond_be2", 2), ("L2_cond_bada", 12),
    ("L3_cond_adaln_mamba_b", 6), ("L3_cond_adaln_mlp_b", 6),
    ("L3_cond_fwd_dt_bias", 4), ("L3_cond_bwd_dt_bias", 4), ("L3_cond_fwd_D", 4), ("L3_cond_bwd_D", 4),
]
VCOL, _at = {}, 0
for _name, _n in VECTORS:
    VCOL[_name] = _at
    _at += _n
VCONV = _at
NVEC = _at + 16

SITES = [
    dict(w="L0_cond_w_adaln1", at=0, b="L0_cond_b_adaln1", scale=0, shift=2, gate=None, norm=None, silu=False),
    dict(w="L0_cond_w_adaln2", at=0, b="L0_cond_b_adaln2", scale=0, shift=2, gate=None, norm=None, silu=False),
    dict(w="L1_cond_adaln1_W", at=0, b="L1_cond_adaln1_b", scale=2, shift=0, gate=4,
         norm=("L1_cond_norm1_w", "L1_cond_norm1_b"), silu=True),
    dict(w="L1_cond_adaln2_W", at=0, b="L1_cond_adaln2_b", scale=2, shift=0, gate=4,
         norm=("L1_cond_norm2_w", "L1_cond_norm2_b"), silu=True),
    dict(w="L2_cond_Wada", at=0, b="L2_cond_bada", scale=2, shift=0, gate=4,
         norm=("L2_cond_g1", "L2_cond_be1"), silu=True),
    dict(w="L2_cond_Wada", at=6, b="L2_cond_bada", scale=8, shift=6, gate=10,
         norm=("L2_cond_g2", "L2_cond_be2"), silu=True),
    dict(w="L3_cond_adaln_mamba_w", at=0, b="L3_cond_adaln_mamba_b", scale=2, shift=0, gate=4, norm=None, silu=False),
    dict(w="L3_cond_adaln_mlp_w", at=0, b="L3_cond_adaln_mlp_b", scale=2, shift=0, gate=4, norm=None, silu=False),
]
SCALE, SHIFT, GATE = range(3)

ATTN = {
    0: dict(bq="L0_cond_bq", bk="L0_cond_bk", bv="L0_cond_bv", bo="L0_cond_bo",
            b1="L0_cond_b1", b2="L0_cond_b2", gated=False),
    2: dict(bq=None, bk=None, bv=None, bo="L2_cond_bproj", b1="L2_cond_b1", b2="L2_cond_b2", gated=True),
}
MAMBA = {
    1: dict(states=32, conv=True, hidden=3, dirs=("", ""), rank=16),
    3: dict(states=64, conv=False, hidden=4, dirs=("fwd_", "bwd_"), rank=None),
}


class Steps:

    def __init__(self, semaphore, names):
        self.semaphore, self.names, self.next = semaphore, names, 0
        self.place = {n: i + 1 for i, n in enumerate(names)}
        assert len(self.place) == len(names)

    def sem(self, name):
        assert self.names[self.next] == name, (self.names[self.next], name)
        self.next += 1
        return self.semaphore

    def count(self, block, name):
        return block * len(self.names) + (1 + self.place[name])

    def before(self, block):
        return block * len(self.names) + 1


def attention_steps():
    pe, act, dve, pool = [], [], [], []
    for name in ("ln1",):
        pe += [f"{name}_mean", f"{name}_var"]
        dve += [f"{name}_centred", f"{name}_h"]
        act += [f"{name}_square", f"{name}_rstd"]
    pe += ["q0", "q1", "k0", "k1", "v0", "v1", "score0", "score1"]
    act += ["q0", "q1", "k0", "k1", "v0", "v1", "exp0"]
    dve += ["sub0"]
    for p in range(PAIRS):
        pool += [f"kbd{p}"]
        pe += [f"tr{p}", f"av{p}"] + ([f"score{p + 2}"] if p + 2 < PAIRS else [])
        act += ([f"exp{p + 1}"] if p + 1 < PAIRS else []) + [f"pt{p}", f"o{p}"]
        dve += ([f"sub{p + 1}"] if p + 1 < PAIRS else []) + [f"norm{p}"]
    pe += ["proj0", "proj1", "ln2_mean", "ln2_var"]
    dve += ["x0", "x1", "ln2_centred", "ln2_h"]
    act += ["ln2_square", "ln2_rstd"]
    pe += [f"up{j}" for j in range(MLP // P)] + ["down0", "down1"]
    act += [f"gelu{j}" for j in range(MLP // P)]
    dve += ["end0", "end1"]
    return pe, act, dve, pool


def mamba_steps(cfg):
    pe, act, dve = ["ln1_mean", "ln1_var"], ["ln1_square", "ln1_rstd"], ["ln1_centred", "ln1_h"]
    for d in range(2):
        if d == 0 or not cfg["conv"]:
            pe += [f"in{d}_{j}" for j in range(2 * DC)]
            act += [f"in{d}_{j}" for j in range(2 * DC)]
        if cfg["conv"]:
            dve += [f"conv{d}"]
            act += [f"xs{d}"]
            pe += [f"rank{d}"]
            act += [f"rank{d}"]
        pe += [f"dt{d}_{j}" for j in range(DC)] + [f"B{d}", f"C{d}"]
        act += [f"B{d}", f"soft{d}"]
        dve += [f"C{d}", f"dt{d}"]
        pe += [f"dtx{d}_{t}" for t in range(TT)]
        act += [f"dtx{d}_{t}" for t in range(TT)]
        dve += [f"y{d}"]
        if d == 1 or not cfg["conv"]:
            pe += [f"out{d}_{j}" for j in range(KC)]
            dve += [f"x{d}_{j}" for j in range(KC)]
    pe += ["ln2_mean", "ln2_var"]
    act += ["ln2_square", "ln2_rstd"]
    dve += ["ln2_centred", "ln2_h"]
    for j in range(cfg["hidden"]):
        pe += [f"gate{j}", f"up{j}"]
        act += [f"silu{j}"]
        dve += [f"glu{j}"]
    pe += ["down0", "down1"]
    dve += ["end0", "end1"]
    return pe, act, dve, []


def build(nc, a, out):
    f32, bf16, u8 = mybir.dt.float32, mybir.dt.bfloat16, mybir.dt.uint8
    ALU, ACT, AX = mybir.AluOpType, mybir.ActivationFunctionType, mybir.AxisListType
    ds = bass.ds
    ctx = ExitStack()
    with ctx:
        def sb(name, shape, dt=f32):
            return ctx.enter_context(nc.sbuf_tensor(name, shape, dt))

        def sem(name):
            return ctx.enter_context(nc.semaphore(name))

        X = sb("x_stream", [P, KC, TOKENS])
        MOD = sb("modulation", [P, len(SITES), 3, KC, BATCH])
        VEC = sb("vectors", [P, NVEC])
        ZERO = sb("zero_col", [P, 1])
        EPSC = sb("eps_col", [P, 1])
        ONEC = sb("one_col", [P, 1])
        COND = sb("cond", [P, KC, BATCH])
        CSILU = sb("cond_silu", [P, KC, BATCH])
        IDENT = sb("ident", [P, P])
        MEAN = sb("mean_weights", [P, P])
        HMASK = sb("head_mask", [P, HPC])
        CAUSAL = sb("causal_add", [P, SEQ])
        KEYADD = sb("key_mask_add", [P, BATCH // 2, SEQ])
        KEYU8 = sb("key_mask", [P, BATCH // 2, SEQ], u8)
        SEL = sb("row_selector", [96, 32], bf16)
        SELF = sb("row_selector_f", [96, 32])
        ZROW = sb("zero_block", [P, T], bf16)
        IDB = sb("ident_bf", [P, P], bf16)
        A1 = sb("decay1", [P, DC, 32])
        A3 = sb("decay3", [P, 2, DC, 64])
        WA = sb("weights_a", [P, 6144])
        WC = sb("weights_c", [P, 15360])
        WORK = sb("work", [P, 21504])
        PS = ctx.enter_context(nc.psum_tensor("psum", [P, 8, T], f32))

        def region(base, at, *dims):
            n = int(np.prod(dims))
            v = base[:, at:at + n]
            if len(dims) == 1:
                return v
            names = "abcd"[:len(dims)]
            return v.rearrange(f"p ({' '.join(names)}) -> p {' '.join(names)}",
                               **{k: s for k, s in zip(names[1:], dims[1:])})

        H = region(WORK, 0, KC, T)
        Q = region(WORK, 1024, KC, T)
        KF = region(WORK, 2048, KC, T)
        KBD = region(WORK, 3072, 2, KC, 2, HPC * SEQ)
        VBD = WORK[:, 7168:9216].rearrange("p (b h r d) -> p b h r d", b=BB, h=HEADS // 2, r=2)
        S = region(WORK, 9216, 2, HEADS, SEQ)
        PT = region(WORK, 11264, 2, HEADS // 2, P)
        AO = region(WORK, 13312, KC, T)
        G = region(WORK, 14336, MLP // P, T)
        XC_A = region(WORK, 18432, KC, T)
        SQ_A = region(WORK, 19456, KC, T)
        RSTD_A = region(WORK, 20480, T)
        TMP_A = region(WORK, 20992, T)
        Z = region(WORK, 1024, DC, T)
        XS = region(WORK, 3072, DC, T)
        DT = region(WORK, 5120, DC, T)
        DTXT = region(WORK, 7168, TT, DI)
        UT = region(WORK, 9216, 2, TT, DI)
        DA = region(WORK, 13312, DC, T)
        HB = region(WORK, 15360, DC, T)
        PR = region(WORK, 17408, DC, T)
        CB = region(WORK, 19456, 2, T)
        BT = region(WORK, 20480, TT, 64)
        C3 = WORK[0:96, 20736:21248].bitcast(bf16).rearrange("p (g t) -> p g t", g=2)
        R1 = PR[0:96, 0, :]
        TMPB = PR[0:96, 1, 0:256].bitcast(bf16)
        XC_M, SQ_M = region(WORK, 9216, KC, T), region(WORK, 10240, KC, T)
        RSTD_M, TMP_M = region(WORK, 11264, T), region(WORK, 11776, T)
        SOFT = PR
        SG = region(WORK, 13312, 4, T)
        GLU = region(WORK, 15360, 4, T)
        XPRE = region(WC, 6656, DC, T)
        YS = region(WC, 8704, DC, T)
        DTR = region(WC, 10752, T)

        mx = sb("row_max", [P, HEADS])
        sm = sb("row_sum", [P, HEADS])
        mx2 = sb("row_max2", [P, HEADS])

        WQKVO = region(WA, 0, KC, 4 * D)
        W1A, W2A = region(WA, 2048, KC, MLP), region(WA, 4096, MLP // P, D)
        W1 = dict(inp=region(WC, 0, KC, 2 * DI), rank=region(WC, 2048, DC, 16), B=region(WC, 2112, DC, 32),
                  C=WC[:, 2240:2624].rearrange("p (k g c) -> p k g c", k=DC, g=1),
                  dt=WC[0:16, 2624:3136], out=region(WC, 3136, DC, D))
        WM1 = dict(w1=region(WC, 4160, KC, 384), w2=region(WC, 4928, KC, 384), w3=region(WC, 5696, 3, D))
        W3 = [dict(inp=region(WC, o, KC, 2 * DI), dt=region(WC, o + 2048, DC, DI), B=region(WC, o + 4096, DC, 64),
                   C=WC[:, o + 4352:o + 5120].rearrange("p (k g c) -> p k g c", k=DC, g=2),
                   out=region(WC, o + 5120, DC, D)) for o in (0, 6144)]
        WM3 = dict(w1=region(WC, 12288, KC, 512), w2=region(WC, 13312, KC, 512), w3=region(WC, 14336, 4, D))
        ADA, at = {}, 0
        for s in SITES:
            if s["w"] not in ADA:
                n = a[s["w"]].shape[1]
                ADA[s["w"]] = region(WC, at, KC, n)
                at += KC * n
        NADA = len(ADA)

        def vec(name, c):
            return ZERO[:, 0:1] if name is None else VEC[:, VCOL[name] + c:VCOL[name] + c + 1]

        dma_small, dma_ada, dma_x, dma_out = sem("dma_small"), sem("dma_ada"), sem("dma_x"), sem("dma_out")
        dma_w = [sem(f"dma_weights{l}") for l in range(4)]
        const_ready = sem("const_ready")
        cond_silu_ready = sem("cond_silu_ready")
        mods_psum = sem("mods_psum")
        mods_ready = sem("mods_ready")
        decay_exp = sem("decay_exp")
        vbd_zeroed = sem("vbd_zeroed")
        steps = []
        for l in range(4):
            lists = attention_steps() if l in ATTN else mamba_steps(MAMBA[l])
            steps.append({e: Steps(sem(f"{e}_steps{l}"), n)
                          for e, n in zip(("pe", "act", "dve", "pool"), lists)})
        scan_sems = {l: {n: sem(f"{n}{l}") for n in (
            "scaled_act",
            "scaled_dve",
            "input_ready",
            "decay_ready",
            "state_ready",
            "c_psum",
            "c_ready",
            "prod_ready",
            "sum_done",
        )} for l in MAMBA}
        NSMALL = 10

        block = ctx.enter_context(nc.Block())

        @block.sync
        def _(sp):
            def load(dst, src, s):
                sp.dma_start(dst, src).then_inc(s, 16)

            kp = "(k p) n -> p k n"
            load(COND[:, :, :], a["cond_t"].rearrange(kp, p=P), dma_small)
            load(VEC[:, :], a["vectors"], dma_small)
            for name, w in ADA.items():
                load(w, a[name].rearrange(kp, p=P), dma_ada)
            load(IDENT[:, :], a["ident"], dma_small)
            load(HMASK[:, :], a["head_mask"], dma_small)
            load(SELF[:, :], a["selector"], dma_small)
            mask = a["mask"].rearrange("(p r) m -> r p m", r=2)
            for r in range(2):
                load(KEYU8[64 * r:64 * r + 64, :, :],
                     mask[r].unsqueeze(0).broadcast_to([64, BATCH // 2, SEQ]), dma_small)
            load(A1[:, :, :], a["L1_cond_A_log"].rearrange(kp, p=P), dma_small)
            for d, pre in enumerate(("fwd_", "bwd_")):
                load(A3[:, d, :, :], a[f"L3_cond_{pre}A_log"].rearrange(kp, p=P), dma_small)
            for b in range(NBLK):
                load(X[:, :, b * T:(b + 1) * T], a["x_t"].rearrange(kp, p=P)[:, :, b * T:(b + 1) * T], dma_x)
            for i, n in enumerate(("wq", "wk", "wv", "wo")):
                load(WQKVO[:, :, i * D:(i + 1) * D], a[f"L0_cond_{n}"].rearrange(kp, p=P), dma_w[0])
            load(W1A, a["L0_cond_w1"].rearrange(kp, p=P), dma_w[0])
            load(W2A, a["L0_cond_w2"].rearrange(kp, p=P), dma_w[0])

            sp.wait_ge(mods_psum, 1)
            xp = a["L1_cond_x_proj_W"].rearrange(kp, p=P)
            load(W1["inp"], a["L1_cond_in_proj_W"].rearrange(kp, p=P), dma_w[1])
            load(W1["rank"], xp[:, :, 0:16], dma_w[1])
            load(W1["B"], xp[:, :, 16:48], dma_w[1])
            for c in range(3):
                load(W1["C"][:, :, 0, 32 * c:32 * c + 32], xp[:, :, 48:80], dma_w[1])
            load(W1["dt"], a["L1_cond_dt_proj_W"], dma_w[1])
            load(W1["out"], a["L1_cond_out_proj_W"].rearrange(kp, p=P), dma_w[1])
            for n in ("w1", "w2", "w3"):
                load(WM1[n], a[f"L1_cond_{n}"].rearrange(kp, p=P), dma_w[1])

            sp.wait_ge(steps[0]["dve"].semaphore, steps[0]["dve"].before(NBLK))
            load(WQKVO[:, :, 0:3 * D], a["L2_cond_Wqkv"].rearrange(kp, p=P), dma_w[2])
            load(WQKVO[:, :, 3 * D:4 * D], a["L2_cond_Wproj"].rearrange(kp, p=P), dma_w[2])
            load(W1A, a["L2_cond_W1"].rearrange(kp, p=P), dma_w[2])
            load(W2A, a["L2_cond_W2"].rearrange(kp, p=P), dma_w[2])

            sp.wait_ge(steps[1]["dve"].semaphore, steps[1]["dve"].before(NBLK))
            for w, pre in zip(W3, ("fwd_", "bwd_")):
                xp = a[f"L3_cond_{pre}xproj_w"].rearrange(kp, p=P)
                load(w["inp"], a[f"L3_cond_{pre}in_w"].rearrange(kp, p=P), dma_w[3])
                load(w["dt"], xp[:, :, 0:DI], dma_w[3])
                load(w["B"], xp[:, :, DI:DI + 64], dma_w[3])
                for g in range(2):
                    for c in range(3):
                        load(w["C"][:, :, g, 32 * c:32 * c + 32],
                             xp[:, :, DI + 64 + 32 * g:DI + 96 + 32 * g], dma_w[3])
                load(w["out"], a[f"L3_cond_{pre}out_w"].rearrange(kp, p=P), dma_w[3])
            for n in ("w1", "w2", "w3"):
                load(WM3[n], a[f"L3_cond_mlp_{n}"].rearrange(kp, p=P), dma_w[3])

            for b in range(NBLK):
                sp.wait_ge(steps[3]["dve"].semaphore, steps[3]["dve"].count(b, "end1"))
                sp.dma_start(out.rearrange(kp, p=P)[:, :, b * T:(b + 1) * T],
                             X[:, :, b * T:(b + 1) * T]).then_inc(dma_out, 16)
            sp.wait_ge(dma_out, 16 * NBLK)

        NW = [6, 11, 4, 2 * 10 + 3]

        @block.tensor
        def _(pe):
            pe.wait_ge(dma_small, 16 * NSMALL)
            pe.wait_ge(dma_ada, 16 * NADA)
            pe.wait_ge(cond_silu_ready, 1)
            flat = PS[:, 0:3, :].rearrange("p b n -> p (b n)")
            for i, s in enumerate(SITES):
                for kind, first in enumerate((s["scale"], s["shift"], s["gate"])):
                    if first is None:
                        continue
                    for c in range(KC):
                        o = ((i * 3 + kind) * KC + c) * BATCH
                        for k in range(KC):
                            last = nc.tensor.matmul(
                                flat[:, o:o + BATCH], ADA[s["w"]][:, k, (first + c) * P:(first + c + 1) * P],
                                (CSILU if s["silu"] else COND)[:, k, :], start=(k == 0), stop=(k == KC - 1))
            last.then_inc(mods_psum, 1)
            pe.wait_ge(const_ready, 3)
            pe.wait_ge(dma_x, 16 * NBLK)

            for l in range(4):
                st = steps[l]
                mine = st["pe"]
                pe.sem_inc(mine.semaphore, 1)
                if l in MAMBA:
                    for n in ("input_ready", "c_psum", "sum_done"):
                        pe.sem_inc(scan_sems[l][n], CREDIT)
                pe.wait_ge(dma_w[l], 16 * NW[l])
                if l == 0:
                    pe.wait_ge(mods_ready, 1)
                else:
                    pe.wait_ge(steps[l - 1]["dve"].semaphore, steps[l - 1]["dve"].before(NBLK))

                with pe.Fori(0, NBLK) as b:
                    def after(engine, name):
                        pe.wait_ge(st[engine].semaphore, st[engine].count(b, name))

                    pe.wait_ge(st["dve"].semaphore, st["dve"].before(b))

                    def norm(n, bank_mean, bank_var, sq, ready):
                        if ready is not None:
                            after("dve", ready)
                        for k in range(KC):
                            last = nc.tensor.matmul(PS[:, bank_mean, :], MEAN[:, :], X[:, k, ds(b * T, T)],
                                                    start=(k == 0), stop=(k == KC - 1))
                        last.then_inc(mine.sem(f"{n}_mean"), 1)
                        after("act", f"{n}_square")
                        for k in range(KC):
                            last = nc.tensor.matmul(PS[:, bank_var, :], MEAN[:, :], sq[:, k, :],
                                                    start=(k == 0), stop=(k == KC - 1))
                        last.then_inc(mine.sem(f"{n}_var"), 1)

                    def linear(name, psum, weights, moving, chunks):
                        for k in range(chunks):
                            last = nc.tensor.matmul(psum, weights[k], moving[k],
                                                    start=(k == 0), stop=(k == chunks - 1))
                        last.then_inc(mine.sem(name), 1)

                    if l in ATTN:
                        norm("ln1", 0, 1, SQ_A, None)
                        after("dve", "ln1_h")
                        hs = [H[:, k, :] for k in range(KC)]
                        for i, n in enumerate("qk"):
                            for c in range(KC):
                                o = i * D + c * P
                                linear(f"{n}{c}", PS[:, 2 + 2 * i + c, :],
                                       [WQKVO[:, k, o:o + P] for k in range(KC)], hs, KC)
                        wv = WQKVO[:, :, 2 * D:3 * D].rearrange("p k (h r d) -> p k h r d", r=2, d=HD)
                        for half in range(2):
                            for j in range(BB // 2):
                                o = (half * BB // 2 + j) * SEQ
                                for r in range(2):
                                    for k in range(KC):
                                        last = nc.tensor.matmul(
                                            PS[64 * r:64 * r + 64, 6 + half, j * P:(j + 1) * P],
                                            H[:, k, o:o + SEQ], wv[:, k, :, r, :],
                                            start=(k == 0), stop=(k == KC - 1))
                            last.then_inc(mine.sem(f"v{half}"), 1)

                        def score(p):
                            after("pool", f"kbd{p}")
                            if p >= 2:
                                after("dve", f"sub{p - 2}")
                            for c in range(KC):
                                for r in range(2):
                                    o = (2 * p + r) * SEQ
                                    last = nc.tensor.matmul(
                                        PS[64 * r:64 * r + 64, 2 * (p % 2) + c, :], Q[:, c, o:o + SEQ],
                                        KBD[:, p % 2, c, r, :], start=True, stop=True)
                            last.then_inc(mine.sem(f"score{p}"), 1)

                        after("act", "q1")
                        score(0)
                        score(1)
                        for p in range(PAIRS):
                            after("dve", f"norm{p}")
                            if p == 0:
                                after("act", "k1")
                            else:
                                after("act", f"pt{p - 1}")
                            for h in range(HEADS // 2):
                                last = nc.tensor.transpose(
                                    PS[:, 4 + h // 4, (h % 4) * P:(h % 4 + 1) * P],
                                    S[:, p % 2, 2 * h:2 * h + 2, :].rearrange("p h m -> p (h m)"), IDENT[:, :])
                            last.then_inc(mine.sem(f"tr{p}"), 1)
                            after("act", f"pt{p}")
                            if p >= 2:
                                after("act", f"o{p - 2}")
                            else:
                                after("act", f"v{p}")
                                after("act", "v1")
                            for h in range(HEADS // 2):
                                q4 = 32 * (h % 4)
                                for r in range(2):
                                    o = (h // 4) * P + r * SEQ
                                    last = nc.tensor.matmul(
                                        PS[q4:q4 + 32, 6 + p % 2, o:o + SEQ],
                                        VBD[:, 2 * p + r, h, :, :].rearrange("p r d -> p (r d)"),
                                        PT[:, p % 2, h, r * SEQ:(r + 1) * SEQ], start=True, stop=True,
                                        tile_position=(0, q4))
                            last.then_inc(mine.sem(f"av{p}"), 1)
                            if p + 2 < PAIRS:
                                score(p + 2)
                        after("act", f"o{PAIRS - 1}")
                        after("dve", f"sub{PAIRS - 1}")
                        for c in range(KC):
                            o = 3 * D + c * P
                            linear(f"proj{c}", PS[:, c, :], [WQKVO[:, k, o:o + P] for k in range(KC)],
                                   [AO[:, k, :] for k in range(KC)], KC)
                        norm("ln2", 2, 3, SQ_A, "x1")
                        after("dve", "ln2_h")
                        for j in range(MLP // P):
                            linear(f"up{j}", PS[:, (4 + j) % 8, :],
                                   [W1A[:, k, j * P:(j + 1) * P] for k in range(KC)], hs, KC)
                        for c in range(KC):
                            after("act", f"gelu{MLP // P - 1}")
                            linear(f"down{c}", PS[:, 4 + c, :],
                                   [W2A[:, k, c * P:(c + 1) * P] for k in range(MLP // P)],
                                   [G[:, k, :] for k in range(MLP // P)], MLP // P)
                        continue

                    cfg, ss = MAMBA[l], scan_sems[l]
                    N = cfg["states"]
                    norm("ln1", 0, 1, SQ_M, None)
                    after("dve", "ln1_h")
                    hs = [H[:, k, :] for k in range(KC)]
                    for d in range(2):
                        w = W1 if l == 1 else W3[d]
                        if d == 0 or not cfg["conv"]:
                            if d == 1:
                                after("dve", "y0")
                                after("dve", "x0_1")
                            for j in range(2 * DC):
                                linear(f"in{d}_{j}", PS[:, (4 + j) % 8, :],
                                       [w["inp"][:, k, j * P:(j + 1) * P] for k in range(KC)], hs, KC)
                        xs = [XS[:, k, :] for k in range(DC)]
                        if cfg["conv"]:
                            after("act", f"xs{d}")
                            if d == 0:
                                after("act", f"in{d}_{2 * DC - 1}")
                            else:
                                after("dve", "y0")
                            linear(f"rank{d}", PS[0:16, 3, :], [w["rank"][:, k, :] for k in range(DC)], xs, DC)
                            after("act", f"rank{d}")
                            for j in range(DC):
                                nc.tensor.matmul(PS[:, 4 + j, :], w["dt"][:, j * P:(j + 1) * P], DTR[0:16, :],
                                                 start=True, stop=True).then_inc(mine.sem(f"dt{d}_{j}"), 1)
                        else:
                            after("act", f"in{d}_{2 * DC - 1}")
                            for j in range(DC):
                                linear(f"dt{d}_{j}", PS[:, 4 + j, :],
                                       [w["dt"][:, k, j * P:(j + 1) * P] for k in range(DC)], xs, DC)
                        for t in range(TT):
                            for k in range(DC):
                                last = nc.tensor.matmul(PS[:, 0, t * N:(t + 1) * N],
                                                        XS[:, k, t * P:(t + 1) * P], w["B"][:, k, :],
                                                        start=(k == 0), stop=(k == DC - 1))
                        last.then_inc(mine.sem(f"B{d}"), 1)
                        for g in range(N // 32):
                            for k in range(DC):
                                last = nc.tensor.matmul(PS[0:96, 1 + g, :], w["C"][:, k, g, :], XS[:, k, :],
                                                        start=(k == 0), stop=(k == DC - 1))
                        last.then_inc(mine.sem(f"C{d}"), 1)
                        after("dve", f"dt{d}")
                        for t in range(TT):
                            for j in range(DC):
                                last = nc.tensor.transpose(PS[:, 4 + t, j * P:(j + 1) * P],
                                                           HB[:, j, t * P:(t + 1) * P], IDENT[:, :])
                            last.then_inc(mine.sem(f"dtx{d}_{t}"), 1)

                        run = (b * 2 + d) * N + CREDIT
                        runc = (b * 2 + d) * (N * DC) + CREDIT
                        run2 = (b * 2 + d) * (N * 2) + CREDIT
                        after("act", f"dtx{d}_{TT - 1}")
                        after("act", f"B{d}")
                        after("dve", f"C{d}")
                        for j in range(DC):
                            nc.tensor.matmul(PS[:, j, :], IDB[:, :], ZROW[:, :], start=True, stop=False)

                        def spread_c(n):
                            pe.wait_ge(ss["c_ready"], run + n - 1)
                            nc.tensor.matmul(PS[:, 6 + spread_c.parity, :],
                                             SEL[:, ds(n % 32, 1)].broadcast_to([96, P]),
                                             C3[:, ds(n // 32, 1), :].rearrange("p g t -> p (g t)"),
                                             start=True, stop=True).then_inc(ss["c_psum"], 1)

                        def transpose_input(n, j, parity):
                            if j == 0:
                                pe.wait_ge(ss["scaled_act"], run2 + (n + 1) * 2)
                                pe.wait_ge(ss["scaled_dve"], run2 + (n + 1) * 2)
                            pe.wait_ge(ss["state_ready"], runc + n * DC + (j - 1))
                            for t in range(TT):
                                last = nc.tensor.transpose(PS[:, 4 + j % 2, t * P:(t + 1) * P],
                                                           UT[:, parity, t, j * P:(j + 1) * P], IDENT[:, :])
                            last.then_inc(ss["input_ready"], 1)

                        def add_up(n, j, final):
                            pe.wait_ge(ss["prod_ready"], runc + n * DC + (j + 1))
                            nc.tensor.matmul(PS[:, j, :], IDENT[:, :], PR[:, j, :], start=False,
                                             stop=final).then_inc(ss["sum_done"], 1)

                        spread_c.parity = 0
                        spread_c(0)
                        for j in range(DC):
                            transpose_input(0, j, 0)

                        def states(first, final):
                            for k in range(UN):
                                n = first + k
                                more = not (final and k == UN - 1)
                                if more:
                                    spread_c.parity = (k + 1) % 2
                                    spread_c(n + 1)
                                for j in range(DC):
                                    if more:
                                        transpose_input(n + 1, j, (k + 1) % 2)
                                    add_up(n, j, final and k == UN - 1)

                        with pe.Fori(0, N // UN - 1) as i:
                            states(i * UN, False)
                        states(N - UN, True)

                        if d == 1 or not cfg["conv"]:
                            after("dve", f"y{d}")
                            for c in range(KC):
                                linear(f"out{d}_{c}", PS[:, 4 + c, :],
                                       [w["out"][:, k, c * P:(c + 1) * P] for k in range(DC)],
                                       [HB[:, k, :] for k in range(DC)], DC)

                    m = WM1 if l == 1 else WM3
                    norm("ln2", 0, 1, SQ_M, "x1_1")
                    after("dve", "ln2_h")
                    for j in range(cfg["hidden"]):
                        for n, key, o in (("gate", "w1", 0), ("up", "w2", 1)):
                            linear(f"{n}{j}", PS[:, 2 * j + o, :],
                                   [m[key][:, k, j * P:(j + 1) * P] for k in range(KC)], hs, KC)
                    after("dve", f"glu{cfg['hidden'] - 1}")
                    for c in range(KC):
                        linear(f"down{c}", PS[:, c, :],
                               [m["w3"][:, k, c * P:(c + 1) * P] for k in range(cfg["hidden"])],
                               [GLU[:, k, :] for k in range(cfg["hidden"])], cfg["hidden"])

        @block.scalar
        def _(act):
            f = nc.scalar.activation
            act.wait_ge(dma_small, 16 * NSMALL)
            act.wait_ge(const_ready, 3)
            f(CSILU[:, :, :], COND[:, :, :], ACT.Silu).then_inc(cond_silu_ready, 1)
            f(A1[:, :, :], A1[:, :, :], ACT.Exp)
            f(A3[:, :, :, :], A3[:, :, :, :], ACT.Exp).then_inc(decay_exp, 1)
            act.wait_ge(mods_ready, 1)

            for l in range(4):
                st = steps[l]
                mine = st["act"]
                act.sem_inc(mine.semaphore, 1)
                if l in MAMBA:
                    ss = scan_sems[l]
                    for n in ("scaled_act", "decay_ready", "c_ready"):
                        act.sem_inc(ss[n], CREDIT)
                with act.Fori(0, NBLK) as b:
                    def after(engine, name):
                        act.wait_ge(st[engine].semaphore, st[engine].count(b, name))

                    def norm(n, bank_var, xc, sq, rstd):
                        after("dve", f"{n}_centred")
                        f(sq, xc, ACT.Square).then_inc(mine.sem(f"{n}_square"), 1)
                        after("pe", f"{n}_var")
                        f(rstd, PS[:, bank_var, :], ACT.Ln, bias=EPSC[:, 0:1])
                        act.drain()
                        f(rstd, rstd, ACT.Exp, scale=-0.5).then_inc(mine.sem(f"{n}_rstd"), 1)

                    if l in ATTN:
                        cfg = ATTN[l]
                        norm("ln1", 1, XC_A, SQ_A, RSTD_A)
                        for i, (n, dst) in enumerate((("q", Q), ("k", KF))):
                            for c in range(KC):
                                after("pe", f"{n}{c}")
                                f(dst[:, c, :], PS[:, 2 + 2 * i + c, :], ACT.Identity,
                                  bias=vec(cfg["b" + n], c)).then_inc(mine.sem(f"{n}{c}"), 1)
                        act.wait_ge(vbd_zeroed, 1 + l // 2)
                        for half in range(2):
                            after("pe", f"v{half}")
                            for r in range(2):
                                last = f(VBD[64 * r:64 * r + 64, half * 4:half * 4 + 4, :, r, :],
                                         PS[64 * r:64 * r + 64, 6 + half, :].rearrange(
                                             "p (b h d) -> p b h d", b=4, h=HEADS // 2), ACT.Copy)
                            last.then_inc(mine.sem(f"v{half}"), 1)

                        def exps(p):
                            after("dve", f"sub{p}")
                            f(S[:, p % 2, :, :], S[:, p % 2, :, :], ACT.Exp).then_inc(mine.sem(f"exp{p}"), 1)

                        exps(0)
                        for p in range(PAIRS):
                            if p + 1 < PAIRS:
                                exps(p + 1)
                            after("pe", f"tr{p}")
                            if p >= 2:
                                after("pe", f"av{p - 2}")
                            f(PT[:, p % 2, :, :], PS[:, 4:6, :].rearrange("p a (h n) -> p (a h) n", n=P),
                              ACT.Copy).then_inc(mine.sem(f"pt{p}"), 1)
                            after("pe", f"av{p}")
                            for c in range(KC):
                                last = f(AO[:, c, p * P:(p + 1) * P], PS[:, 6 + p % 2, c * P:(c + 1) * P],
                                         ACT.Identity, bias=vec(cfg["bv"], c))
                            last.then_inc(mine.sem(f"o{p}"), 1)
                        norm("ln2", 3, XC_A, SQ_A, RSTD_A)
                        for j in range(MLP // P):
                            after("pe", f"up{j}")
                            f(G[:, j, :], PS[:, (4 + j) % 8, :], ACT.Gelu,
                              bias=vec(cfg["b1"], j)).then_inc(mine.sem(f"gelu{j}"), 1)
                        continue

                    cfg, ss = MAMBA[l], scan_sems[l]
                    N = cfg["states"]
                    norm("ln1", 1, XC_M, SQ_M, RSTD_M)
                    for d in range(2):
                        decay = A1 if l == 1 else A3[:, d, :, :]
                        dt_bias = "L1_cond_dt_proj_b" if l == 1 else f"L3_cond_{cfg['dirs'][d]}dt_bias"
                        if d == 0 or not cfg["conv"]:
                            for j in range(2 * DC):
                                after("pe", f"in{d}_{j}")
                                if j >= DC:
                                    f(Z[:, j - DC, :], PS[:, j - DC, :], ACT.Silu).then_inc(mine.sem(f"in{d}_{j}"), 1)
                                elif cfg["conv"]:
                                    f(XPRE[:, j, :], PS[:, 4 + j, :], ACT.Copy).then_inc(mine.sem(f"in{d}_{j}"), 1)
                                else:
                                    f(XS[:, j, :], PS[:, 4 + j, :], ACT.Silu).then_inc(mine.sem(f"in{d}_{j}"), 1)
                        if cfg["conv"]:
                            after("dve", f"conv{d}")
                            for j in range(DC):
                                last = f(XS[:, j, :], HB[:, j, :], ACT.Silu, bias=vec("L1_cond_conv_b", j))
                            last.then_inc(mine.sem(f"xs{d}"), 1)
                            after("pe", f"rank{d}")
                            f(DTR[0:16, :], PS[0:16, 3, :], ACT.Copy).then_inc(mine.sem(f"rank{d}"), 1)
                        after("pe", f"B{d}")
                        f(BT[:, :, 0:N], PS[:, 0, 0:TT * N].rearrange("p (t n) -> p t n", t=TT),
                          ACT.Copy).then_inc(mine.sem(f"B{d}"), 1)
                        after("dve", f"C{d}")
                        for j in range(DC):
                            f(SOFT[:, j, :], PS[:, 4 + j, :], ACT.Abs, bias=vec(dt_bias, j))
                        act.drain()
                        f(SOFT, SOFT, ACT.Exp, scale=-1.0)
                        act.drain()
                        f(SOFT, SOFT, ACT.Ln, bias=ONEC[:, 0:1]).then_inc(mine.sem(f"soft{d}"), 1)
                        for t in range(TT):
                            after("pe", f"dtx{d}_{t}")
                            f(DTXT[:, t, :], PS[:, 4 + t, :], ACT.Copy).then_inc(mine.sem(f"dtx{d}_{t}"), 1)

                        run = (b * 2 + d) * N + CREDIT
                        runc = (b * 2 + d) * (N * DC) + CREDIT
                        act.drain()
                        after("dve", f"dt{d}")
                        lo = 1 - d
                        with act.Fori(0, N // UN) as i:
                            for k in range(UN):
                                n = i * UN + k
                                act.wait_ge(ss["input_ready"], runc + n * DC - DC)
                                for t in range(2):
                                    f(UT[:, k % 2, t, :], DTXT[:, t, :], ACT.Copy,
                                      scale=BT[:, t, ds(n, 1)]).then_inc(ss["scaled_act"], 1)
                                for j in range(DC):
                                    act.wait_ge(ss["state_ready"], runc + n * DC + (j + 1 - DC))
                                    seqs = DA[:, j, :].rearrange("p (b s) -> p b s", s=SEQ)
                                    dts = DT[:, j, :].rearrange("p (b s) -> p b s", s=SEQ)
                                    f(seqs[:, :, lo:lo + SEQ - 1], dts[:, :, lo:lo + SEQ - 1], ACT.Exp,
                                      scale=decay[:, j, ds(n, 1)]).then_inc(ss["decay_ready"], 1)
                                    if j == 0:
                                        act.wait_ge(ss["c_psum"], run + n + 1)
                                        act.wait_ge(ss["prod_ready"], runc + n * DC - DC)
                                        f(CB[:, k % 2, :], PS[:, 6 + k % 2, :], ACT.Copy).then_inc(ss["c_ready"], 1)
                    norm("ln2", 1, XC_M, SQ_M, RSTD_M)
                    for j in range(cfg["hidden"]):
                        after("pe", f"gate{j}")
                        f(SG[:, j, :], PS[:, 2 * j, :], ACT.Silu).then_inc(mine.sem(f"silu{j}"), 1)

        @block.vector
        def _(dve):
            v = nc.vector
            v.memset(ZERO[:, :], 0.0)
            v.memset(EPSC[:, :], EPS)
            v.memset(ONEC[:, :], 1.0)
            v.memset(MEAN[:, :], 1.0 / D)
            v.memset(ZROW[:, :], 0.0).then_inc(const_ready, 1)
            dve.wait_ge(dma_small, 16 * NSMALL)
            v.tensor_copy(IDB[:, :], IDENT[:, :])
            v.tensor_copy(SEL[:, :], SELF[:, :])
            v.tensor_scalar(KEYADD[:, :, :], KEYU8[:, :, :], -3e38, 10.0, ALU.mult, ALU.mult).then_inc(const_ready, 1)
            dve.wait_ge(decay_exp, 1)
            v.tensor_scalar(A1[:, :, :], A1[:, :, :], -1.0, None, ALU.mult)
            v.tensor_scalar(A3[:, :, :, :], A3[:, :, :, :], -1.0, None, ALU.mult)
            dve.wait_ge(mods_psum, 1)
            flat = PS[:, 0:3, :].rearrange("p b n -> p (b n)")
            for i, s in enumerate(SITES):
                for kind, first in enumerate((s["scale"], s["shift"], s["gate"])):
                    if first is not None:
                        o = (i * 3 + kind) * KC * BATCH
                        c = VCOL[s["b"]] + first
                        v.tensor_tensor(MOD[:, i, kind, :, :],
                                        flat[:, o:o + KC * BATCH].rearrange("p (c n) -> p c n", c=KC),
                                        VEC[:, c:c + KC].unsqueeze(2).broadcast_to([P, KC, BATCH]), ALU.add)
            dve.drain()
            for i in range(len(SITES)):
                v.tensor_scalar(MOD[:, i, SCALE, :, :], MOD[:, i, SCALE, :, :], 1.0, None, ALU.add)
            dve.drain()
            for i, s in enumerate(SITES):
                if s["norm"]:
                    wcol, bcol = (VEC[:, VCOL[n]:VCOL[n] + KC].unsqueeze(2).broadcast_to([P, KC, BATCH])
                                  for n in s["norm"])
                    v.tensor_tensor(TMP_A[:, 0:KC * BATCH].rearrange("p (c n) -> p c n", c=KC),
                                    MOD[:, i, SCALE, :, :], bcol, ALU.mult)
                    dve.drain()
                    v.tensor_tensor(MOD[:, i, SHIFT, :, :], MOD[:, i, SHIFT, :, :],
                                    TMP_A[:, 0:KC * BATCH].rearrange("p (c n) -> p c n", c=KC), ALU.add)
                    v.tensor_tensor(MOD[:, i, SCALE, :, :], MOD[:, i, SCALE, :, :], wcol, ALU.mult)
                    dve.drain()
            v.tensor_copy(ZERO[:, :], ZERO[:, :]).then_inc(mods_ready, 1)

            for l in range(4):
                st = steps[l]
                mine = st["dve"]
                dve.drain()
                dve.sem_inc(mine.semaphore, 1)
                if l in MAMBA:
                    for n in ("scaled_dve", "state_ready"):
                        dve.sem_inc(scan_sems[l][n], CREDIT)
                if l == 0:
                    dve.wait_ge(dma_x, 16 * NBLK)
                with dve.Fori(0, NBLK) as b:
                    def after(engine, name):
                        dve.wait_ge(st[engine].semaphore, st[engine].count(b, name))

                    def xblk(c):
                        return X[:, c, ds(b * T, T)]

                    def mod(site, kind, c):
                        return MOD[:, site, kind, c, ds(b * BB, BB)].unsqueeze(2).broadcast_to([P, BB, SEQ])

                    def seqs(ap):
                        return ap.rearrange("p (b s) -> p b s", s=SEQ)

                    def norm(n, site, bank_mean, xc, rstd):
                        after("pe", f"{n}_mean")
                        for c in range(KC):
                            last = v.tensor_tensor(xc[:, c, :], xblk(c), PS[:, bank_mean, :], ALU.subtract)
                        last.then_inc(mine.sem(f"{n}_centred"), 1)
                        after("act", f"{n}_rstd")
                        for c in range(KC):
                            v.tensor_tensor(xc[:, c, :], xc[:, c, :], rstd, ALU.mult)
                        dve.drain()
                        for c in range(KC):
                            v.tensor_tensor(seqs(xc[:, c, :]), seqs(xc[:, c, :]), mod(site, SCALE, c), ALU.mult)
                        dve.drain()
                        for c in range(KC):
                            last = v.tensor_tensor(seqs(H[:, c, :]), seqs(xc[:, c, :]), mod(site, SHIFT, c), ALU.add)
                        last.then_inc(mine.sem(f"{n}_h"), 1)

                    def residual(name, c, bank, bias, site, tmp):
                        if site is None:
                            v.scalar_tensor_tensor(out=xblk(c), in0=PS[:, bank, :], scalar=bias, in1=xblk(c),
                                                   op0=ALU.add, op1=ALU.add).then_inc(mine.sem(name), 1)
                            return
                        v.scalar_tensor_tensor(out=seqs(tmp), in0=seqs(PS[:, bank, :]), scalar=bias,
                                               in1=mod(site, GATE, c), op0=ALU.add, op1=ALU.mult)
                        dve.drain()
                        v.tensor_tensor(xblk(c), xblk(c), tmp, ALU.add).then_inc(mine.sem(name), 1)
                        dve.drain()

                    if l in ATTN:
                        cfg = ATTN[l]
                        site = lambda i: 2 * l + i if cfg["gated"] else None
                        norm("ln1", 2 * l, 0, XC_A, RSTD_A)

                        def sub(p):
                            after("pe", f"score{p}")
                            if p >= 2:
                                after("pe", f"tr{p - 2}")
                            add = KEYADD[:, ds(b * PAIRS + p, 1), :] if l == 0 else CAUSAL[:, :].unsqueeze(1)
                            s = S[:, p % 2, :, :]
                            v.scalar_tensor_tensor(
                                out=s, in0=PS[:, 2 * (p % 2):2 * (p % 2) + 2, :].rearrange("p c (h m) -> p (c h) m", m=SEQ),
                                scalar=float(HD) ** -0.5, in1=add.broadcast_to([P, HEADS, SEQ]),
                                op0=ALU.mult, op1=ALU.add)
                            dve.drain()
                            v.reduce_max(mx[:, :], s, AX.X)
                            dve.drain()
                            v.tensor_tensor(s, s, mx[:, :].unsqueeze(2).broadcast_to([P, HEADS, SEQ]),
                                            ALU.subtract).then_inc(mine.sem(f"sub{p}"), 1)

                        def normalise(p):
                            s = S[:, p % 2, :, :]
                            after("act", f"exp{p}")
                            v.reduce_sum(sm[:, :], s, AX.X)
                            dve.drain()
                            v.reciprocal(mx2[:, :], sm[:, :])
                            dve.drain()
                            v.tensor_tensor(s, s, mx2[:, :].unsqueeze(2).broadcast_to([P, HEADS, SEQ]),
                                            ALU.mult).then_inc(mine.sem(f"norm{p}"), 1)
                            dve.drain()

                        dve.drain()
                        sub(0)
                        for p in range(PAIRS):
                            if p + 1 < PAIRS:
                                sub(p + 1)
                            normalise(p)
                        for c in range(KC):
                            after("pe", f"proj{c}")
                            residual(f"x{c}", c, c, vec(cfg["bo"], c), site(0), TMP_A)
                        norm("ln2", 2 * l + 1, 2, XC_A, RSTD_A)
                        for c in range(KC):
                            after("pe", f"down{c}")
                            residual(f"end{c}", c, 4 + c, vec(cfg["b2"], c), site(1), TMP_A)
                        dve.drain()
                        continue

                    cfg, ss = MAMBA[l], scan_sems[l]
                    N = cfg["states"]
                    norm("ln1", 2 * l, 0, XC_M, RSTD_M)
                    for d in range(2):
                        pre = cfg["dirs"][d]
                        dt_bias = "L1_cond_dt_proj_b" if l == 1 else f"L3_cond_{pre}dt_bias"
                        skip = "L1_cond_Dp" if l == 1 else f"L3_cond_{pre}D"
                        if cfg["conv"]:
                            if d == 1:
                                dve.drain()
                            after("act", f"in0_{DC - 1}")
                            for tap in range(3, -1, -1):
                                shift = 3 - tap
                                for j in range(DC):
                                    col = VCONV + j * 4 + tap
                                    wt = VEC[:, col:col + 1]
                                    src, dst = seqs(XPRE[:, j, :]), seqs(HB[:, j, :])
                                    if shift == 0:
                                        last = v.tensor_scalar(HB[:, j, :], XPRE[:, j, :], wt, None, ALU.mult)
                                        continue
                                    to, fr = (slice(shift, SEQ), slice(0, SEQ - shift))
                                    if d == 1:
                                        to, fr = fr, to
                                    last = v.scalar_tensor_tensor(out=dst[:, :, to], in0=src[:, :, fr], scalar=wt,
                                                                  in1=dst[:, :, to], op0=ALU.mult, op1=ALU.add)
                                if shift < 3:
                                    dve.drain()
                            last.then_inc(mine.sem(f"conv{d}"), 1)
                        after("pe", f"C{d}")
                        for g in range(N // 32):
                            c = PS[0:96, 1 + g, :]
                            v.tensor_copy(C3[0:32, g, :], c[0:32, :])
                            v.tensor_copy(TMPB, c)
                            dve.drain()
                            v.tensor_tensor(R1, c, TMPB, ALU.subtract)
                            dve.drain()
                            v.tensor_copy(C3[32:64, g, :], R1[32:64, :])
                            v.tensor_copy(TMPB[64:96, :], R1[64:96, :])
                            dve.drain()
                            last = v.tensor_tensor(C3[64:96, g, :], R1[64:96, :], TMPB[64:96, :], ALU.subtract)
                            dve.drain()
                        for j in range(DC):
                            last = v.tensor_scalar(DT[:, j, :], PS[:, 4 + j, :], vec(dt_bias, j), 0.0,
                                                   ALU.add, ALU.max)
                        last.then_inc(mine.sem(f"C{d}"), 1)
                        dve.drain()
                        after("act", f"soft{d}")
                        v.tensor_tensor(DT, DT, SOFT, ALU.add)
                        dve.drain()
                        v.tensor_tensor(HB, DT, XS, ALU.mult)
                        first = 0 if d == 0 else SEQ - 1
                        v.memset(DA.rearrange("p j (b s) -> p (j b) s", s=SEQ)[:, :, first:first + 1], 0.0)\
                            .then_inc(mine.sem(f"dt{d}"), 1)
                        dve.drain()
                        after("act", f"dtx{d}_{TT - 1}")

                        runc = (b * 2 + d) * (N * DC) + CREDIT

                        def scale_input(n, parity):
                            dve.wait_ge(ss["input_ready"], runc + n * DC - DC)
                            for t in range(2, TT):
                                v.tensor_scalar(UT[:, parity, t, :], DTXT[:, t, :], BT[:, t, ds(n, 1)], None,
                                                ALU.mult).then_inc(ss["scaled_dve"], 1)

                        def states(start, final):
                            for k in range(UN):
                                n = start + k
                                for j in range(DC):
                                    dve.wait_ge(ss["input_ready"], runc + n * DC + (j + 1))
                                    dve.wait_ge(ss["decay_ready"], runc + n * DC + (j + 1))
                                    dve.wait_ge(ss["prod_ready"], runc + n * DC + (j + 1 - DC))
                                    step = slice(None, None, -1) if d else slice(None)
                                    v.tensor_tensor_scan(HB[:, j, step], DA[:, j, step], PS[:, 4 + j % 2, step],
                                                         0.0, ALU.mult, ALU.add).then_inc(ss["state_ready"], 1)
                                    if j == 0 and not (final and k == UN - 1):
                                        scale_input(n + 1, (k + 1) % 2)

                        scale_input(0, 0)
                        with dve.Fori(0, N // UN - 1) as i:
                            states(i * UN, False)
                        states(N - UN, True)

                        dve.drain()
                        dve.wait_ge(ss["sum_done"], runc + N * DC)
                        if l == 1 and d == 0:
                            for j in range(DC):
                                last = v.scalar_tensor_tensor(out=YS[:, j, :], in0=XS[:, j, :], scalar=vec(skip, j),
                                                              in1=PS[:, j, :], op0=ALU.mult, op1=ALU.add)
                            last.then_inc(mine.sem(f"y{d}"), 1)
                            dve.drain()
                            continue
                        for j in range(DC):
                            v.scalar_tensor_tensor(out=HB[:, j, :], in0=XS[:, j, :], scalar=vec(skip, j),
                                                   in1=PS[:, j, :], op0=ALU.mult, op1=ALU.add)
                        dve.drain()
                        if l == 1:
                            v.tensor_tensor(HB, HB, YS, ALU.add)
                            dve.drain()
                        v.tensor_tensor(HB, HB, Z, ALU.mult).then_inc(mine.sem(f"y{d}"), 1)
                        for c in range(KC):
                            after("pe", f"out{d}_{c}")
                            residual(f"x{d}_{c}", c, 4 + c, ZERO[:, 0:1], 2 * l, TMP_M)
                    norm("ln2", 2 * l + 1, 0, XC_M, RSTD_M)
                    for j in range(cfg["hidden"]):
                        after("pe", f"up{j}")
                        after("act", f"silu{j}")
                        v.tensor_tensor(GLU[:, j, :], SG[:, j, :], PS[:, 2 * j + 1, :],
                                        ALU.mult).then_inc(mine.sem(f"glu{j}"), 1)
                    for c in range(KC):
                        after("pe", f"down{c}")
                        residual(f"end{c}", c, c, ZERO[:, 0:1], 2 * l + 1, TMP_M)
                    dve.drain()

        @block.gpsimd
        def _(pool):
            g = nc.gpsimd
            g.memset(CAUSAL[:, :], 0.0)
            pool.drain()
            for r in range(2):
                g.affine_select(out=CAUSAL[64 * r:64 * r + 64, :], in_=CAUSAL[64 * r:64 * r + 64, :],
                                compare_op=ALU.is_ge, fill=-1e30, base=0, pattern=[[-1, SEQ]], channel_multiplier=1)
            pool.drain()
            g.memset(VBD, 0.0).then_inc(vbd_zeroed, 1)
            pool.sem_inc(const_ready, 1)

            for l in range(4):
                st = steps[l]
                mine = st["pool"]
                pool.sem_inc(mine.semaphore, 1)
                if l == 2:
                    pool.wait_ge(steps[1]["dve"].semaphore, steps[1]["dve"].before(NBLK))
                    g.memset(VBD, 0.0).then_inc(vbd_zeroed, 1)
                if l in MAMBA:
                    pool.sem_inc(scan_sems[l]["prod_ready"], CREDIT)
                with pool.Fori(0, NBLK) as b:
                    if l in ATTN:
                        pool.wait_ge(st["act"].semaphore, st["act"].count(b, "k1"))
                        for p in range(PAIRS):
                            if p >= 2:
                                pool.wait_ge(st["pe"].semaphore, st["pe"].count(b, f"score{p - 2}"))
                            for c in range(KC):
                                for r in range(2):
                                    o = (2 * p + r) * SEQ
                                    last = g.tensor_tensor(
                                        KBD[:, p % 2, c, r, :].rearrange("p (h m) -> p h m", m=SEQ),
                                        KF[:, c, o:o + SEQ].unsqueeze(1).broadcast_to([P, HPC, SEQ]),
                                        HMASK[:, :].unsqueeze(2).broadcast_to([P, HPC, SEQ]), ALU.mult)
                            last.then_inc(mine.sem(f"kbd{p}"), 1)
                        continue
                    cfg, ss = MAMBA[l], scan_sems[l]
                    N = cfg["states"]
                    for d in range(2):
                        run = (b * 2 + d) * N + CREDIT
                        runc = (b * 2 + d) * (N * DC) + CREDIT
                        with pool.Fori(0, N // UN) as i:
                            for k in range(UN):
                                n = i * UN + k
                                pool.wait_ge(ss["c_ready"], run + n + 1)
                                for j in range(DC):
                                    pool.wait_ge(ss["state_ready"], runc + n * DC + (j + 1))
                                    pool.wait_ge(ss["sum_done"], runc + n * DC + (j + 1 - DC))
                                    g.tensor_tensor(PR[:, j, :], HB[:, j, :], CB[:, k % 2, :],
                                                    ALU.mult).then_inc(ss["prod_ready"], 1)


_TRANSPOSED = ("L0_cond_w_adaln1", "L0_cond_w_adaln2", "L0_cond_wq", "L0_cond_wk", "L0_cond_wv",
               "L0_cond_wo", "L0_cond_w1", "L0_cond_w2")
_PLAIN = ("L1_cond_adaln1_W", "L1_cond_adaln2_W", "L1_cond_in_proj_W", "L1_cond_x_proj_W", "L1_cond_dt_proj_W",
          "L1_cond_A_log", "L1_cond_out_proj_W", "L1_cond_w1", "L1_cond_w2", "L1_cond_w3", "L2_cond_Wqkv",
          "L2_cond_Wproj", "L2_cond_W1", "L2_cond_W2", "L2_cond_Wada", "L3_cond_adaln_mamba_w",
          "L3_cond_adaln_mlp_w", "L3_cond_mlp_w1", "L3_cond_mlp_w2", "L3_cond_mlp_w3", "L3_cond_fwd_in_w",
          "L3_cond_fwd_xproj_w", "L3_cond_fwd_A_log", "L3_cond_fwd_out_w", "L3_cond_bwd_in_w",
          "L3_cond_bwd_xproj_w", "L3_cond_bwd_A_log", "L3_cond_bwd_out_w")


def kernel(**inputs):
    import concourse.bacc as bacc
    from concourse.bass_utils import run_bass_kernel_spmd

    arrays = {k: np.asarray(v) for k, v in inputs.items()}
    laid = {k: arrays[k].T for k in _TRANSPOSED}
    laid |= {k: arrays[k] for k in _PLAIN}
    laid["x_t"] = arrays["x"].reshape(TOKENS, D).T
    laid["cond_t"] = arrays["cond_1024"].T
    laid["mask"] = arrays["mask_BxS_bf0"]
    columns = [arrays[n].reshape(c, P).T for n, c in VECTORS]
    columns.append(arrays["L1_cond_conv_w"].reshape(DC, P, 4).transpose(1, 0, 2).reshape(P, DC * 4))
    laid["vectors"] = np.concatenate(columns, axis=1)
    laid["ident"] = np.eye(P, dtype=np.float32)
    laid["head_mask"] = np.kron(np.eye(HPC), np.ones((HD, 1))).astype(np.float32)
    laid["selector"] = np.tile(np.eye(32), (3, 1)).astype(np.float32)

    nc = bacc.Bacc("TRN2", target_bir_lowering=False, num_devices=1)
    feeds, aps = {}, {}
    for name, value in laid.items():
        value = np.ascontiguousarray(value)
        feeds[f"in_{name}"] = value
        aps[name] = nc.dram_tensor(f"in_{name}", value.shape, mybir.dt.from_np(value.dtype), kind="ExternalInput").ap()
    out = nc.dram_tensor("out_t", (D, TOKENS), mybir.dt.float32, kind="ExternalOutput").ap()
    build(nc, aps, out)
    r = run_bass_kernel_spmd(nc, [feeds], core_ids=[0])
    return np.ascontiguousarray(r.results[0]["out_t"].T).reshape(BATCH, SEQ, D)
```

```python
from contextlib import ExitStack

import numpy as np

import concourse.bass as bass
from concourse import mybir

P = 128
D = 256
KC = D // P
BATCH, SEQ = 32, 64
TOKENS = BATCH * SEQ
T = 512
NBLK = TOKENS // T
BB = T // SEQ
PAIRS = BB // 2
TT = T // P
HEADS, HD = 16, 16
HPC = P // HD
MLP = 1024
DI = 512
DC = DI // P
UN = 4
PAIRED = 2
SINGLE = DC - PAIRED
VECTOR_PRODUCTS = 1
Y_ORDER = [*range(PAIRED, DC), *range(PAIRED)]
ACT_TILES = 3
BASE = 8
CREDIT = 16
EPS = 1e-5

VECTORS = [
    ("L0_cond_b_adaln1", 4), ("L0_cond_b_adaln2", 4), ("L0_cond_bq", 2), ("L0_cond_bk", 2),
    ("L0_cond_bv", 2), ("L0_cond_bo", 2), ("L0_cond_b1", 8), ("L0_cond_b2", 2),
    ("L1_cond_norm1_w", 2), ("L1_cond_norm1_b", 2), ("L1_cond_norm2_w", 2), ("L1_cond_norm2_b", 2),
    ("L1_cond_adaln1_b", 6), ("L1_cond_adaln2_b", 6), ("L1_cond_conv_b", 4),
    ("L1_cond_dt_proj_b", 4), ("L1_cond_Dp", 4),
    ("L2_cond_bproj", 2), ("L2_cond_b1", 8), ("L2_cond_b2", 2), ("L2_cond_g1", 2),
    ("L2_cond_be1", 2), ("L2_cond_g2", 2), ("L2_cond_be2", 2), ("L2_cond_bada", 12),
    ("L3_cond_adaln_mamba_b", 6), ("L3_cond_adaln_mlp_b", 6),
    ("L3_cond_fwd_dt_bias", 4), ("L3_cond_bwd_dt_bias", 4), ("L3_cond_fwd_D", 4), ("L3_cond_bwd_D", 4),
]
VCOL, _at = {}, 0
for _name, _n in VECTORS:
    VCOL[_name] = _at
    _at += _n
VCONV = _at
NVEC = _at + 16

SITES = [
    dict(w="L0_cond_w_adaln1", at=0, b="L0_cond_b_adaln1", scale=0, shift=2, gate=None, norm=None, silu=False),
    dict(w="L0_cond_w_adaln2", at=0, b="L0_cond_b_adaln2", scale=0, shift=2, gate=None, norm=None, silu=False),
    dict(w="L1_cond_adaln1_W", at=0, b="L1_cond_adaln1_b", scale=2, shift=0, gate=4,
         norm=("L1_cond_norm1_w", "L1_cond_norm1_b"), silu=True),
    dict(w="L1_cond_adaln2_W", at=0, b="L1_cond_adaln2_b", scale=2, shift=0, gate=4,
         norm=("L1_cond_norm2_w", "L1_cond_norm2_b"), silu=True),
    dict(w="L2_cond_Wada", at=0, b="L2_cond_bada", scale=2, shift=0, gate=4,
         norm=("L2_cond_g1", "L2_cond_be1"), silu=True),
    dict(w="L2_cond_Wada", at=6, b="L2_cond_bada", scale=8, shift=6, gate=10,
         norm=("L2_cond_g2", "L2_cond_be2"), silu=True),
    dict(w="L3_cond_adaln_mamba_w", at=0, b="L3_cond_adaln_mamba_b", scale=2, shift=0, gate=4, norm=None, silu=False),
    dict(w="L3_cond_adaln_mlp_w", at=0, b="L3_cond_adaln_mlp_b", scale=2, shift=0, gate=4, norm=None, silu=False),
]
SCALE, SHIFT, GATE = range(3)

ATTN = {
    0: dict(bq="L0_cond_bq", bk="L0_cond_bk", bv="L0_cond_bv", bo="L0_cond_bo",
            b1="L0_cond_b1", b2="L0_cond_b2", gated=False),
    2: dict(bq=None, bk=None, bv=None, bo="L2_cond_bproj", b1="L2_cond_b1", b2="L2_cond_b2", gated=True),
}
MAMBA = {
    1: dict(states=32, conv=True, hidden=3, dirs=("", ""), rank=16),
    3: dict(states=64, conv=False, hidden=4, dirs=("fwd_", "bwd_"), rank=None),
}


class Steps:

    def __init__(self, semaphore, names):
        self.semaphore, self.names, self.next = semaphore, names, 0
        self.place = {n: i + 1 for i, n in enumerate(names)}
        assert len(self.place) == len(names)

    def sem(self, name):
        assert self.names[self.next] == name, (self.names[self.next], name)
        self.next += 1
        return self.semaphore

    def count(self, block, name):
        return block * len(self.names) + (BASE + self.place[name])

    def previous(self, block, name):
        ahead = len(self.names) - self.place[name]
        assert ahead < BASE
        return block * len(self.names) + (BASE - ahead)

    def lead(self, name):
        return self.place[name]

    def before(self, block):
        return block * len(self.names) + BASE


def norm_steps(name):
    return [[f"{name}_mean", f"{name}_var"], [f"{name}_square", f"{name}_rstd"], [f"{name}_centred", f"{name}_h"]]


ACT_NORMS = ["next_square", "next_rstd", "ln2_square", "ln2_rstd"]
DVE_NORMS = ["ln2_centred", "next_h", "ln2_h"]


def attention_steps():
    pe = ["k0", "k1", "q0", "q1", "v0", "v1"] + [f"score{p}" for p in range(PAIRS)]
    act = ["k0", "k1", "q0", "q1", "v0", "v1", "exp0"]
    dve, pool = ["sub0"], []
    for p in range(PAIRS):
        pool += [f"kbd{p}"]
        pe += [f"tr{p}"] + (["next_mean"] if p == PAIRS - 1 else []) + [f"av{p}"]
        act += ([f"exp{p + 1}"] if p + 1 < PAIRS else []) + [f"pt{p}", f"o{p}"]
        dve += ([f"sub{p + 1}"] if p + 1 < PAIRS else []) + [f"norm{p}"]
    pe += ["proj0", "proj1", "next_var", "ln2_mean", "ln2_var"]
    dve += ["next_centred", "x0", "x1"] + DVE_NORMS
    act += ACT_NORMS
    pe += [f"up{j}" for j in range(MLP // P)] + ["down0", "down1"]
    act += [f"gelu{j}" for j in range(MLP // P)]
    dve += ["end0", "end1"]
    return pe, act, dve, pool


def mamba_steps(cfg):
    pe, act, dve = [], [], []
    for d in range(2):
        if d == 0:
            pe += [f"in{d}_{j}" for j in range(2 * DC)]
        elif not cfg["conv"]:
            pe += [f"in{d}_{j}" for j in range(DC, 2 * DC)]
        if d == 0 or not cfg["conv"]:
            act += [f"in{d}_{j}" for j in range(2 * DC)]
        if cfg["conv"]:
            dve += [f"conv{d}_{j}" for j in range(DC)]
            act += [f"xs{d}"]
            pe += [f"rank{d}"]
            act += [f"rank{d}"]
        pe += [f"dt{d}_{j}" for j in range(DC)] + [f"C{d}", f"B{d}", f"dtx{d}"]
        act += [f"soft{d}_0", f"soft{d}_1", f"B{d}", f"dtx{d}"]
        dve += [f"relu{d}_{j}" for j in range(DC)] + [f"C{d}", f"dtx{d}_0", f"dtx{d}_1", f"dtxt{d}"]
        dve += [f"y{d}_{j}" for j in Y_ORDER]
        if d == 0 and not cfg["conv"]:
            pe += [f"in1_{j}" for j in range(DC)]
        if d == 1:
            pe += ["next_mean"]
            dve += ["next_centred"]
        if d == 1 or not cfg["conv"]:
            pe += [f"out{d}_{j}" for j in range(KC)]
            dve += [f"x{d}_{j}" for j in range(KC)]
    pe += ["next_var", "ln2_mean", "ln2_var"]
    act += ACT_NORMS
    dve += DVE_NORMS
    for j in range(cfg["hidden"]):
        pe += [f"gate{j}", f"up{j}"]
        act += [f"silu{j}"]
        dve += [f"glu{j}"]
    pe += ["down0", "down1"]
    dve += ["end0", "end1"]
    return pe, act, dve, []


def products(states, run, group, k, j):
    per_pair = 2 * DC - VECTOR_PRODUCTS
    assert k % 2 == 0 or j < 0 or j >= VECTOR_PRODUCTS
    return ((run * (states // 2) + group * (UN // 2)) * per_pair
            + (k // 2 * per_pair + (k % 2) * (DC - VECTOR_PRODUCTS) + (j + 1) + CREDIT))


def build(nc, a, out, c_rows):
    f32, bf16, u8 = mybir.dt.float32, mybir.dt.bfloat16, mybir.dt.uint8
    ALU, ACT, AX = mybir.AluOpType, mybir.ActivationFunctionType, mybir.AxisListType
    ds = bass.ds
    ctx = ExitStack()
    with ctx:
        def sb(name, shape, dt=f32):
            return ctx.enter_context(nc.sbuf_tensor(name, shape, dt))

        def sem(name):
            return ctx.enter_context(nc.semaphore(name))

        X = sb("x_stream", [P, KC, TOKENS])
        MOD = sb("modulation", [P, len(SITES), 3, KC, BATCH])
        VEC = sb("vectors", [P, NVEC])
        ZERO = sb("zero_col", [P, 1])
        EPSC = sb("eps_col", [P, 1])
        ONEC = sb("one_col", [P, 1])
        COND = sb("cond", [P, KC, BATCH])
        CSILU = sb("cond_silu", [P, KC, BATCH])
        IDENT = sb("ident", [P, P])
        MEAN = sb("mean_weights", [P, P])
        HMASK = sb("head_mask", [P, HPC])
        CAUSAL = sb("causal_add", [P, SEQ])
        KEYADD = sb("key_mask_add", [P, BATCH // 2, SEQ])
        KEYU8 = sb("key_mask", [P, BATCH // 2, SEQ], u8)
        ZROW = sb("zero_block", [P, T], bf16)
        IDB = sb("ident_bf", [P, P], bf16)
        A1 = sb("decay1", [P, DC, 32])
        A3 = sb("decay3", [P, 2, DC, 64])
        WA = sb("weights_a", [P, 6144])
        WC = sb("weights_c", [P, 15360])
        WORK = sb("work", [P, 21504])
        PS = ctx.enter_context(nc.psum_tensor("psum", [P, 8, T], f32))

        def region(base, at, *dims):
            n = int(np.prod(dims))
            v = base[:, at:at + n]
            if len(dims) == 1:
                return v
            names = "abcd"[:len(dims)]
            return v.rearrange(f"p ({' '.join(names)}) -> p {' '.join(names)}",
                               **{k: s for k, s in zip(names[1:], dims[1:])})

        H = H1 = sb("normed1", [P, KC, T])
        H2 = region(WORK, 0, KC, T)
        Q = region(WORK, 1024, KC, T)
        KF = region(WORK, 2048, KC, T)
        KBD = region(WORK, 3072, 2, KC, 2, HPC * SEQ)
        VBD = WORK[:, 7168:9216].rearrange("p (b h r d) -> p b h r d", b=BB, h=HEADS // 2, r=2)
        S = region(WORK, 14336, PAIRS, HEADS, SEQ)
        PT = region(WORK, 11264, 2, HEADS // 2, P)
        AO = region(WORK, 13312, KC, T)
        G = region(WORK, 14336, MLP // P, T)
        XC_A = region(WORK, 18432, KC, T)
        SQ_A = region(WORK, 19456, KC, T)
        RSTD_A = region(WORK, 20480, T)
        LN_A = (XC_A, SQ_A, RSTD_A)
        NEXT_A = (region(WORK, 3072, KC, T), region(WORK, 4096, KC, T), region(WORK, 5120, T))
        TMP_A = region(WORK, 20992, T)
        Z = region(WORK, 1024, DC, T)
        XS = region(WORK, 3072, DC, T)
        DT = region(WORK, 5120, DC, T)
        DTXT = region(WORK, 7168, TT, DI)
        UT = region(WORK, 9216, 2, TT, DI)
        DA = region(WORK, 13312, DC, T)
        HB = region(WORK, 15360, DC, T)
        PR = region(WORK, 17408, DC, T)
        BT = region(WORK, 19456, TT, 64)
        CROW = WORK[0:64, 19712:20224]
        CB = {1: region(WC, 11264 + PAIRED * T, 2, 2, T), 3: region(WA, PAIRED * T, 2, 2, T)}
        XC_M, SQ_M = region(WORK, 9216, KC, T), region(WORK, 10240, KC, T)
        RSTD_M, TMP_M = region(WORK, 11264, T), region(WORK, 11776, T)
        LN_M = (XC_M, SQ_M, RSTD_M)
        NEXT_M = (region(WORK, 7168, KC, T), region(WORK, 8192, KC, T), region(WORK, 12288, T))
        PR2 = {1: region(WC, 11264, PAIRED, T), 3: region(WA, 0, PAIRED, T)}
        SOFT = PR
        SG = region(WORK, 13312, 4, T)
        GLU = region(WORK, 15360, 4, T)
        XPRE = region(WC, 6656, DC, T)
        YS = region(WC, 8704, DC, T)
        DTR = region(WC, 10752, T)

        mx = sb("row_max", [P, HEADS])
        sm = sb("row_sum", [P, HEADS])
        mx2 = sb("row_max2", [P, HEADS])

        WQKVO = region(WA, 0, KC, 4 * D)
        W1A, W2A = region(WA, 2048, KC, MLP), region(WA, 4096, MLP // P, D)
        W1 = dict(inp=region(WC, 0, KC, 2 * DI), rank=region(WC, 2048, DC, 16), B=region(WC, 2112, DC, 32),
                  C=region(WC, 2240, DC, 32),
                  dt=region(WC, 2624, 1, 512), out=region(WC, 3136, DC, D))
        WM1 = dict(w1=region(WC, 4160, KC, 384), w2=region(WC, 4928, KC, 384), w3=region(WC, 5696, 3, D))
        W3 = [dict(inp=region(WC, o, KC, 2 * DI), dt=region(WC, o + 2048, DC, DI), B=region(WC, o + 4096, DC, 64),
                   C=region(WC, o + 4352, DC, 64),
                   out=region(WC, o + 5120, DC, D)) for o in (0, 6144)]
        WM3 = dict(w1=region(WC, 12288, KC, 512), w2=region(WC, 13312, KC, 512), w3=region(WC, 14336, 4, D))
        ADA, at = {}, 0
        for s in SITES:
            if s["w"] not in ADA:
                n = a[s["w"]].shape[1]
                ADA[s["w"]] = region(WC, at, KC, n)
                at += KC * n
        NADA = len(ADA)

        def vec(name, c):
            return ZERO[:, 0:1] if name is None else VEC[:, VCOL[name] + c:VCOL[name] + c + 1]

        dma_small, dma_ada, dma_x, dma_out = sem("dma_small"), sem("dma_ada"), sem("dma_x"), sem("dma_out")
        dma_w = [sem(f"dma_weights{l}") for l in range(4)]
        const_ready = sem("const_ready")
        cond_silu_ready = sem("cond_silu_ready")
        mods_psum = sem("mods_psum")
        mods_ready = sem("mods_ready")
        decay_exp = sem("decay_exp")
        vbd_zeroed = sem("vbd_zeroed")
        rank_zeroed = sem("rank_zeroed")
        lead = [{e: Steps(sem(f"{e}_lead{l}"), n) for e, n in zip(("pe", "act", "dve"), norm_steps("lead"))}
                for l in range(4)]
        steps = []
        for l in range(4):
            lists = attention_steps() if l in ATTN else mamba_steps(MAMBA[l])
            steps.append({e: Steps(sem(f"{e}_steps{l}"), n)
                          for e, n in zip(("pe", "act", "dve", "pool"), lists)})
        crow_out = {l: sem(f"crow_out{l}") for l in MAMBA}
        c_loaded = {l: [sem(f"c_loaded{l}_slot{s}") for s in range(2)] for l in MAMBA}
        scan_sems = {l: {n: sem(f"{n}{l}") for n in (
            "scaled_act",
            "scaled_dve",
            "input_ready",
            "decay_ready",
            "state_ready",
            "prod_ready",
            "prod_vector",
            "sum_done",
            "pair_added",
            "pair_summed",
        )} for l in MAMBA}
        NSMALL = 9

        block = ctx.enter_context(nc.Block())

        @block.sync
        def _(sp):
            def load(dst, src, s):
                sp.dma_start(dst, src).then_inc(s, 16)

            kp = "(k p) n -> p k n"
            load(COND[:, :, :], a["cond_t"].rearrange(kp, p=P), dma_small)
            load(VEC[:, :], a["vectors"], dma_small)
            for name, w in ADA.items():
                load(w, a[name].rearrange(kp, p=P), dma_ada)
            load(IDENT[:, :], a["ident"], dma_small)
            load(HMASK[:, :], a["head_mask"], dma_small)
            mask = a["mask"].rearrange("(p r) m -> r p m", r=2)
            for r in range(2):
                load(KEYU8[64 * r:64 * r + 64, :, :],
                     mask[r].unsqueeze(0).broadcast_to([64, BATCH // 2, SEQ]), dma_small)
            load(A1[:, :, :], a["L1_cond_A_log"].rearrange(kp, p=P), dma_small)
            for d, pre in enumerate(("fwd_", "bwd_")):
                load(A3[:, d, :, :], a[f"L3_cond_{pre}A_log"].rearrange(kp, p=P), dma_small)
            for b in range(NBLK):
                load(X[:, :, b * T:(b + 1) * T], a["x_t"].rearrange(kp, p=P)[:, :, b * T:(b + 1) * T], dma_x)
            for i, n in enumerate(("wq", "wk", "wv", "wo")):
                load(WQKVO[:, :, i * D:(i + 1) * D], a[f"L0_cond_{n}"].rearrange(kp, p=P), dma_w[0])
            load(W1A, a["L0_cond_w1"].rearrange(kp, p=P), dma_w[0])
            load(W2A, a["L0_cond_w2"].rearrange(kp, p=P), dma_w[0])

            sp.wait_ge(rank_zeroed, 1)
            xp = a["L1_cond_x_proj_W"].rearrange(kp, p=P)
            load(W1["inp"], a["L1_cond_in_proj_W"].rearrange(kp, p=P), dma_w[1])
            load(W1["rank"], xp[:, :, 0:16], dma_w[1])
            load(W1["B"], xp[:, :, 16:48], dma_w[1])
            load(W1["C"], xp[:, :, 48:80], dma_w[1])
            load(W1["dt"][0:16, 0, :], a["L1_cond_dt_proj_W"], dma_w[1])
            load(W1["out"], a["L1_cond_out_proj_W"].rearrange(kp, p=P), dma_w[1])
            for n in ("w1", "w2", "w3"):
                load(WM1[n], a[f"L1_cond_{n}"].rearrange(kp, p=P), dma_w[1])

            sp.wait_ge(steps[0]["dve"].semaphore, steps[0]["dve"].before(NBLK))
            load(WQKVO[:, :, 0:3 * D], a["L2_cond_Wqkv"].rearrange(kp, p=P), dma_w[2])
            load(WQKVO[:, :, 3 * D:4 * D], a["L2_cond_Wproj"].rearrange(kp, p=P), dma_w[2])
            load(W1A, a["L2_cond_W1"].rearrange(kp, p=P), dma_w[2])
            load(W2A, a["L2_cond_W2"].rearrange(kp, p=P), dma_w[2])

            def spread_c(l, b, d):
                N, ss = MAMBA[l]["states"], scan_sems[l]
                r = b * 2 + d
                sp.wait_ge(steps[l]["dve"].semaphore, steps[l]["dve"].count(b, f"C{d}"))
                sp.dma_start(c_rows[d, 0:N, :], CROW[0:N, :]).then_inc(crow_out[l], 16)
                with sp.Fori(0, N // UN) as i:
                    sp.wait_ge(crow_out[l], r * 16 + 16)
                    for s in range(2):
                        sp.wait_ge(ss["pair_summed"], (r * (N // 2) + i * (UN // 2) + s - 1) * PAIRED + CREDIT)
                        sp.dma_start(CB[l][:, s, :, :],
                                     c_rows[d, ds(i * UN + 2 * s, 2), :].unsqueeze(0).broadcast_to([P, 2, T])
                                     ).then_inc(c_loaded[l][s], 16)

            with sp.Fori(0, NBLK) as b:
                for d in range(2):
                    spread_c(1, b, d)

            sp.wait_ge(steps[1]["dve"].semaphore, steps[1]["dve"].before(NBLK))
            for w, pre in zip(W3, ("fwd_", "bwd_")):
                xp = a[f"L3_cond_{pre}xproj_w"].rearrange(kp, p=P)
                load(w["inp"], a[f"L3_cond_{pre}in_w"].rearrange(kp, p=P), dma_w[3])
                load(w["dt"], xp[:, :, 0:DI], dma_w[3])
                load(w["B"], xp[:, :, DI:DI + 64], dma_w[3])
                load(w["C"], xp[:, :, DI + 64:DI + 128], dma_w[3])
                load(w["out"], a[f"L3_cond_{pre}out_w"].rearrange(kp, p=P), dma_w[3])
            for n in ("w1", "w2", "w3"):
                load(WM3[n], a[f"L3_cond_mlp_{n}"].rearrange(kp, p=P), dma_w[3])

            with sp.Fori(0, NBLK) as b:
                for d in range(2):
                    spread_c(3, b, d)
                sp.wait_ge(steps[3]["dve"].semaphore, steps[3]["dve"].count(b, "end1"))
                sp.dma_start(out.rearrange(kp, p=P)[:, :, ds(b * T, T)], X[:, :, ds(b * T, T)]).then_inc(dma_out, 16)
            sp.wait_ge(dma_out, 16 * NBLK)

        NW = [6, 9, 4, 2 * 5 + 3]

        @block.tensor
        def _(pe):
            pe.wait_ge(dma_small, 16 * NSMALL)
            pe.wait_ge(dma_ada, 16 * NADA)
            pe.wait_ge(cond_silu_ready, 1)
            flat = PS[:, 0:3, :].rearrange("p b n -> p (b n)")
            for i, s in enumerate(SITES):
                for kind, first in enumerate((s["scale"], s["shift"], s["gate"])):
                    if first is None:
                        continue
                    for c in range(KC):
                        o = ((i * 3 + kind) * KC + c) * BATCH
                        for k in range(KC):
                            last = nc.tensor.matmul(
                                flat[:, o:o + BATCH], ADA[s["w"]][:, k, (first + c) * P:(first + c + 1) * P],
                                (CSILU if s["silu"] else COND)[:, k, :], start=(k == 0), stop=(k == KC - 1))
            last.then_inc(mods_psum, 1)
            pe.wait_ge(const_ready, 3)
            pe.wait_ge(dma_x, 16 * NBLK)

            for l in range(4):
                st = steps[l]
                mine = st["pe"]
                pe.sem_inc(mine.semaphore, BASE)
                if l in MAMBA:
                    for n in ("input_ready", "sum_done", "pair_summed"):
                        pe.sem_inc(scan_sems[l][n], CREDIT)
                pe.wait_ge(dma_w[l], 16 * NW[l])
                if l == 0:
                    pe.wait_ge(mods_ready, 1)
                else:
                    pe.wait_ge(steps[l - 1]["dve"].semaphore, steps[l - 1]["dve"].before(NBLK))

                def average(bank, moving, done):
                    for k in range(KC):
                        last = nc.tensor.matmul(PS[:, bank, :], MEAN[:, :], moving[k],
                                                start=(k == 0), stop=(k == KC - 1))
                    last.then_inc(done, 1)

                LN, NEXT = (LN_A, NEXT_A) if l in ATTN else (LN_M, NEXT_M)
                ld = lead[l]
                average(0, [X[:, k, 0:T] for k in range(KC)], ld["pe"].sem("lead_mean"))
                pe.wait_ge(ld["act"].semaphore, ld["act"].lead("lead_square"))
                average(1, [LN[1][:, k, :] for k in range(KC)], ld["pe"].sem("lead_var"))

                with pe.Fori(0, NBLK) as b:
                    def after(engine, name):
                        pe.wait_ge(st[engine].semaphore, st[engine].count(b, name))

                    pe.wait_ge(st["dve"].semaphore, st["dve"].previous(b, "next_h"))

                    def next_mean(bank):
                        nxt = ((b + 1) % NBLK) * T
                        average(bank, [X[:, k, ds(nxt, T)] for k in range(KC)], mine.sem("next_mean"))

                    def norms(bank, next_bank, ready):
                        after("act", "next_square")
                        average(next_bank + 1, [NEXT[1][:, k, :] for k in range(KC)], mine.sem("next_var"))
                        after("dve", ready)
                        average(bank, [X[:, k, ds(b * T, T)] for k in range(KC)], mine.sem("ln2_mean"))
                        after("act", "ln2_square")
                        average(bank + 1, [LN[1][:, k, :] for k in range(KC)], mine.sem("ln2_var"))

                    def linear(name, psum, weights, moving, chunks):
                        for k in range(chunks):
                            last = nc.tensor.matmul(psum, weights[k], moving[k],
                                                    start=(k == 0), stop=(k == chunks - 1))
                        last.then_inc(mine.sem(name), 1)

                    if l in ATTN:
                        hs = [H1[:, k, :] for k in range(KC)]
                        h2 = [H2[:, k, :] for k in range(KC)]
                        for i, n, bank in ((1, "k", 2), (0, "q", 4)):
                            if n == "q":
                                pe.wait_ge(st["dve"].semaphore, st["dve"].before(b))
                            for c in range(KC):
                                o = i * D + c * P
                                linear(f"{n}{c}", PS[:, bank + c, :],
                                       [WQKVO[:, k, o:o + P] for k in range(KC)], hs, KC)
                        wv = WQKVO[:, :, 2 * D:3 * D].rearrange("p k (h r d) -> p k h r d", r=2, d=HD)
                        for half in range(2):
                            for j in range(BB // 2):
                                o = (half * BB // 2 + j) * SEQ
                                for r in range(2):
                                    for k in range(KC):
                                        last = nc.tensor.matmul(
                                            PS[64 * r:64 * r + 64, 6 + half, j * P:(j + 1) * P],
                                            H[:, k, o:o + SEQ], wv[:, k, :, r, :],
                                            start=(k == 0), stop=(k == KC - 1))
                            last.then_inc(mine.sem(f"v{half}"), 1)

                        def score(p):
                            after("pool", f"kbd{p}")
                            if p >= 2:
                                after("dve", f"sub{p - 2}")
                            for c in range(KC):
                                for r in range(2):
                                    o = (2 * p + r) * SEQ
                                    last = nc.tensor.matmul(
                                        PS[64 * r:64 * r + 64, 2 * (p % 2) + c, :], Q[:, c, o:o + SEQ],
                                        KBD[:, p % 2, c, r, :], start=True, stop=True)
                            last.then_inc(mine.sem(f"score{p}"), 1)

                        after("act", "q1")
                        for p in range(PAIRS):
                            score(p)
                        for p in range(PAIRS):
                            after("dve", f"norm{p}")
                            if p > 0:
                                after("act", f"pt{p - 1}")
                            for h in range(HEADS // 2):
                                last = nc.tensor.transpose(
                                    PS[:, 4 + h // 4, (h % 4) * P:(h % 4 + 1) * P],
                                    S[:, p, 2 * h:2 * h + 2, :].rearrange("p h m -> p (h m)"), IDENT[:, :])
                            last.then_inc(mine.sem(f"tr{p}"), 1)
                            if p == PAIRS - 1:
                                next_mean(2)
                            after("act", f"pt{p}")
                            if p >= 2:
                                after("act", f"o{p - 2}")
                            else:
                                after("act", f"v{p}")
                                after("act", "v1")
                            for h in range(HEADS // 2):
                                q4 = 32 * (h % 4)
                                for r in range(2):
                                    o = (h // 4) * P + r * SEQ
                                    last = nc.tensor.matmul(
                                        PS[q4:q4 + 32, 6 + p % 2, o:o + SEQ],
                                        VBD[:, 2 * p + r, h, :, :].rearrange("p r d -> p (r d)"),
                                        PT[:, p % 2, h, r * SEQ:(r + 1) * SEQ], start=True, stop=True,
                                        tile_position=(0, q4))
                            last.then_inc(mine.sem(f"av{p}"), 1)
                        after("act", f"o{PAIRS - 1}")
                        for c in range(KC):
                            o = 3 * D + c * P
                            linear(f"proj{c}", PS[:, c, :], [WQKVO[:, k, o:o + P] for k in range(KC)],
                                   [AO[:, k, :] for k in range(KC)], KC)
                        norms(6, 2, "x1")
                        after("dve", "ln2_h")
                        for j in range(MLP // P):
                            linear(f"up{j}", PS[:, (4 + j) % 8, :],
                                   [W1A[:, k, j * P:(j + 1) * P] for k in range(KC)], h2, KC)
                        last = [None] * KC
                        for k in range(MLP // P):
                            after("act", f"gelu{k}")
                            for c in range(KC):
                                last[c] = nc.tensor.matmul(PS[:, 4 + c, :], W2A[:, k, c * P:(c + 1) * P], G[:, k, :],
                                                           start=(k == 0), stop=(k == MLP // P - 1))
                                if k == 0 and c == 0:
                                    after("act", "gelu1")
                        for c in range(KC):
                            last[c].then_inc(mine.sem(f"down{c}"), 1)
                        continue

                    cfg, ss = MAMBA[l], scan_sems[l]
                    N = cfg["states"]
                    hs = [H1[:, k, :] for k in range(KC)]
                    h2 = [H2[:, k, :] for k in range(KC)]

                    def project_in(d, chunks):
                        for j in chunks:
                            linear(f"in{d}_{j}", PS[:, (4 + j) % 8, :],
                                   [(W1 if l == 1 else W3[d])["inp"][:, k, j * P:(j + 1) * P] for k in range(KC)],
                                   hs, KC)

                    for d in range(2):
                        w = W1 if l == 1 else W3[d]
                        if d == 0:
                            project_in(0, range(DC))
                            pe.wait_ge(st["dve"].semaphore, st["dve"].before(b))
                            project_in(0, range(DC, 2 * DC))
                        elif not cfg["conv"]:
                            project_in(1, (DC, DC + 1))
                            after("dve", "x0_1")
                            project_in(1, (DC + 2, DC + 3))
                        xs = [XS[:, k, :] for k in range(DC)]
                        if cfg["conv"]:
                            after("act", f"xs{d}")
                            if d == 0:
                                after("act", f"in{d}_{2 * DC - 1}")
                            else:
                                after("dve", f"y0_{Y_ORDER[-1]}")
                            linear(f"rank{d}", PS[0:16, 3, :], [w["rank"][:, k, :] for k in range(DC)], xs, DC)
                            after("act", f"rank{d}")
                            for j in range(DC):
                                nc.tensor.matmul(PS[:, 4 + j, :], w["dt"][:, 0, j * P:(j + 1) * P], DTR,
                                                 start=True, stop=True).then_inc(mine.sem(f"dt{d}_{j}"), 1)
                        else:
                            after("act", f"in{d}_{DC - 1}")
                            for j in range(DC):
                                linear(f"dt{d}_{j}", PS[:, 4 + j, :],
                                       [w["dt"][:, k, j * P:(j + 1) * P] for k in range(DC)], xs, DC)
                            after("act", f"in{d}_{2 * DC - 1}")
                        linear(f"C{d}", PS[0:N, 1, :], [w["C"][:, k, :] for k in range(DC)], xs, DC)
                        for t in range(TT):
                            for k in range(DC):
                                last = nc.tensor.matmul(PS[:, 0, t * N:(t + 1) * N],
                                                        XS[:, k, t * P:(t + 1) * P], w["B"][:, k, :],
                                                        start=(k == 0), stop=(k == DC - 1))
                        last.then_inc(mine.sem(f"B{d}"), 1)
                        for j in range(DC):
                            if j % 2 == 0:
                                after("dve", f"dtx{d}_{j // 2}")
                            for t in range(TT):
                                last = nc.tensor.transpose(PS[:, 4 + t, j * P:(j + 1) * P],
                                                           HB[:, j, t * P:(t + 1) * P], IDENT[:, :])
                        last.then_inc(mine.sem(f"dtx{d}"), 1)

                        runc = (b * 2 + d) * (N * DC) + CREDIT
                        run_act = (b * 2 + d) * (N * ACT_TILES) + CREDIT
                        run_dve = (b * 2 + d) * (N * (TT - ACT_TILES)) + CREDIT
                        run_pair = (b * 2 + d) * (N // 2 * PAIRED) + CREDIT
                        after("act", f"dtx{d}")
                        after("dve", f"dtxt{d}")
                        for j in range(DC):
                            nc.tensor.matmul(PS[:, j, :], IDB[:, :], ZROW[:, :], start=True, stop=False)

                        def transpose_input(n, j, parity):
                            if j == 0:
                                pe.wait_ge(ss["scaled_act"], run_act + (n + 1) * ACT_TILES)
                                pe.wait_ge(ss["scaled_dve"], run_dve + (n + 1) * (TT - ACT_TILES))
                            pe.wait_ge(ss["state_ready"], runc + n * DC + (j + 1 - DC))
                            for t in range(TT):
                                last = nc.tensor.transpose(PS[:, 4 + j, t * P:(t + 1) * P],
                                                           UT[:, parity, t, j * P:(j + 1) * P], IDENT[:, :])
                            last.then_inc(ss["input_ready"], 1)

                        def add_up(i, k, j, final):
                            pe.wait_ge(ss["prod_ready"], products(N, b * 2 + d, i, k, j))
                            nc.tensor.matmul(PS[:, j, :], IDENT[:, :], PR[:, j, :], start=False,
                                             stop=final).then_inc(ss["sum_done"], 1)

                        def add_up_pair(pair, j, final):
                            pe.wait_ge(ss["pair_added"], run_pair + pair * PAIRED + (j + 1))
                            nc.tensor.matmul(PS[:, j, :], IDENT[:, :], PR2[l][:, j, :], start=False,
                                             stop=final).then_inc(ss["pair_summed"], 1)

                        for j in range(DC):
                            transpose_input(0, j, 0)

                        def states(i, final):
                            for k in range(UN):
                                n = i * UN + k
                                more = not (final and k == UN - 1)
                                for j in range(DC):
                                    if more:
                                        transpose_input(n + 1, j, (k + 1) % 2)
                                    if j >= PAIRED:
                                        add_up(i, k, j, not more)
                                if k % 2:
                                    for j in range(PAIRED):
                                        add_up_pair(i * (UN // 2) + k // 2, j, not more)

                        with pe.Fori(0, N // UN - 1) as i:
                            states(i, False)
                        states(N // UN - 1, True)

                        pe.wait_ge(ss["state_ready"], runc + N * DC)
                        if d == 1:
                            next_mean(6)
                        elif not cfg["conv"]:
                            project_in(1, range(DC))
                        if d == 1 or not cfg["conv"]:
                            last = [None] * KC
                            for k in Y_ORDER:
                                after("dve", f"y{d}_{k}")
                                for c in range(KC):
                                    last[c] = nc.tensor.matmul(PS[:, 2 + 2 * d + c, :], w["out"][:, k, c * P:(c + 1) * P],
                                                               HB[:, k, :], start=(k == Y_ORDER[0]),
                                                               stop=(k == Y_ORDER[-1]))
                            for c in range(KC):
                                last[c].then_inc(mine.sem(f"out{d}_{c}"), 1)

                    m = WM1 if l == 1 else WM3
                    norms(0, 6, "x1_1")
                    after("dve", "ln2_h")
                    for j in range(cfg["hidden"]):
                        if j == 3:
                            after("act", "next_rstd")
                        for n, key, o in (("gate", "w1", 0), ("up", "w2", 1)):
                            linear(f"{n}{j}", PS[:, 2 * j + o, :],
                                   [m[key][:, k, j * P:(j + 1) * P] for k in range(KC)], h2, KC)
                    after("dve", f"glu{cfg['hidden'] - 1}")
                    for c in range(KC):
                        linear(f"down{c}", PS[:, c, :],
                               [m["w3"][:, k, c * P:(c + 1) * P] for k in range(cfg["hidden"])],
                               [GLU[:, k, :] for k in range(cfg["hidden"])], cfg["hidden"])

        @block.scalar
        def _(act):
            f = nc.scalar.activation
            EXP_LN, GELU, SILU = 6, 10, 18

            def tables(which):
                act.add_instruction(mybir.InstLoadActFuncSet(
                    name=nc.get_next_instruction_name(), engine=act.engine, act_func_set_id=which, ins=[], outs=[]))

            act.wait_ge(dma_small, 16 * NSMALL)
            act.wait_ge(const_ready, 3)
            f(CSILU[:, :, :], COND[:, :, :], ACT.Silu).then_inc(cond_silu_ready, 1)
            tables(EXP_LN)
            f(A1[:, :, :], A1[:, :, :], ACT.Exp)
            f(A3[:, :, :, :], A3[:, :, :, :], ACT.Exp).then_inc(decay_exp, 1)
            act.wait_ge(mods_ready, 1)

            for l in range(4):
                st = steps[l]
                mine = st["act"]
                act.sem_inc(mine.semaphore, BASE)
                if l in MAMBA:
                    ss = scan_sems[l]
                    for n in ("scaled_act", "decay_ready"):
                        act.sem_inc(ss[n], CREDIT)
                def square(xc, sq, done):
                    f(sq, xc, ACT.Square).then_inc(done, 1)

                def rsqrt(bank, rstd, done):
                    f(rstd, PS[:, bank, :], ACT.Ln, bias=EPSC[:, 0:1])
                    act.drain()
                    f(rstd, rstd, ACT.Exp, scale=-0.5).then_inc(done, 1)

                LN, NEXT = (LN_A, NEXT_A) if l in ATTN else (LN_M, NEXT_M)
                ld = lead[l]
                tables(EXP_LN)
                act.wait_ge(ld["dve"].semaphore, ld["dve"].lead("lead_centred"))
                square(LN[0], LN[1], ld["act"].sem("lead_square"))
                act.wait_ge(ld["pe"].semaphore, ld["pe"].lead("lead_var"))
                rsqrt(1, LN[2], ld["act"].sem("lead_rstd"))
                if l in MAMBA:
                    tables(SILU)

                with act.Fori(0, NBLK) as b:
                    def after(engine, name):
                        act.wait_ge(st[engine].semaphore, st[engine].count(b, name))

                    def norms(bank, next_bank):
                        after("dve", "next_centred")
                        square(NEXT[0], NEXT[1], mine.sem("next_square"))
                        after("pe", "next_var")
                        rsqrt(next_bank + 1, NEXT[2], mine.sem("next_rstd"))
                        after("dve", "ln2_centred")
                        square(LN[0], LN[1], mine.sem("ln2_square"))
                        after("pe", "ln2_var")
                        rsqrt(bank + 1, LN[2], mine.sem("ln2_rstd"))

                    if l in ATTN:
                        cfg = ATTN[l]
                        tables(EXP_LN)
                        for n, dst, bank in (("k", KF, 2), ("q", Q, 4)):
                            for c in range(KC):
                                after("pe", f"{n}{c}")
                                f(dst[:, c, :], PS[:, bank + c, :], ACT.Identity,
                                  bias=vec(cfg["b" + n], c)).then_inc(mine.sem(f"{n}{c}"), 1)
                        act.wait_ge(vbd_zeroed, 1 + l // 2)
                        for half in range(2):
                            after("pe", f"v{half}")
                            for r in range(2):
                                last = f(VBD[64 * r:64 * r + 64, half * 4:half * 4 + 4, :, r, :],
                                         PS[64 * r:64 * r + 64, 6 + half, :].rearrange(
                                             "p (b h d) -> p b h d", b=4, h=HEADS // 2), ACT.Copy)
                            last.then_inc(mine.sem(f"v{half}"), 1)

                        def exps(p):
                            after("dve", f"sub{p}")
                            f(S[:, p, :, :], S[:, p, :, :], ACT.Exp).then_inc(mine.sem(f"exp{p}"), 1)

                        exps(0)
                        for p in range(PAIRS):
                            if p + 1 < PAIRS:
                                exps(p + 1)
                            after("pe", f"tr{p}")
                            if p >= 2:
                                after("pe", f"av{p - 2}")
                            f(PT[:, p % 2, :, :], PS[:, 4:6, :].rearrange("p a (h n) -> p (a h) n", n=P),
                              ACT.Copy).then_inc(mine.sem(f"pt{p}"), 1)
                            after("pe", f"av{p}")
                            for c in range(KC):
                                last = f(AO[:, c, p * P:(p + 1) * P], PS[:, 6 + p % 2, c * P:(c + 1) * P],
                                         ACT.Identity, bias=vec(cfg["bv"], c))
                            last.then_inc(mine.sem(f"o{p}"), 1)
                        norms(6, 2)
                        tables(GELU)
                        for j in range(MLP // P):
                            after("pe", f"up{j}")
                            f(G[:, j, :], PS[:, (4 + j) % 8, :], ACT.Gelu,
                              bias=vec(cfg["b1"], j)).then_inc(mine.sem(f"gelu{j}"), 1)
                        continue

                    cfg, ss = MAMBA[l], scan_sems[l]
                    N = cfg["states"]
                    for d in range(2):
                        if d == 1:
                            tables(SILU)
                        decay = A1 if l == 1 else A3[:, d, :, :]
                        dt_bias = "L1_cond_dt_proj_b" if l == 1 else f"L3_cond_{cfg['dirs'][d]}dt_bias"
                        if d == 0 or not cfg["conv"]:
                            if d == 1:
                                after("dve", f"y0_{Y_ORDER[-1]}")
                            for j in range(2 * DC):
                                after("pe", f"in{d}_{j}")
                                if j >= DC:
                                    f(Z[:, j - DC, :], PS[:, j - DC, :], ACT.Silu).then_inc(mine.sem(f"in{d}_{j}"), 1)
                                elif cfg["conv"]:
                                    f(XPRE[:, j, :], PS[:, 4 + j, :], ACT.Copy).then_inc(mine.sem(f"in{d}_{j}"), 1)
                                else:
                                    f(XS[:, j, :], PS[:, 4 + j, :], ACT.Silu).then_inc(mine.sem(f"in{d}_{j}"), 1)
                        if cfg["conv"]:
                            for j in range(DC):
                                after("dve", f"conv{d}_{j}")
                                last = f(XS[:, j, :], HB[:, j, :], ACT.Silu, bias=vec("L1_cond_conv_b", j))
                            last.then_inc(mine.sem(f"xs{d}"), 1)
                            after("pe", f"rank{d}")
                            f(DTR[0:16, :], PS[0:16, 3, :], ACT.Copy).then_inc(mine.sem(f"rank{d}"), 1)
                        tables(EXP_LN)
                        for j in range(DC):
                            after("dve", f"relu{d}_{j}")
                            f(SOFT[:, j, :], PS[:, 4 + j, :], ACT.Abs, bias=vec(dt_bias, j))
                        act.drain()
                        f(SOFT, SOFT, ACT.Exp, scale=-1.0)
                        act.drain()
                        for h in range(2):
                            f(SOFT[:, 2 * h:2 * h + 2, :], SOFT[:, 2 * h:2 * h + 2, :], ACT.Ln,
                              bias=ONEC[:, 0:1]).then_inc(mine.sem(f"soft{d}_{h}"), 1)
                        after("pe", f"B{d}")
                        f(BT[:, :, 0:N], PS[:, 0, 0:TT * N].rearrange("p (t n) -> p t n", t=TT),
                          ACT.Copy).then_inc(mine.sem(f"B{d}"), 1)
                        after("pe", f"dtx{d}")
                        for t in range(ACT_TILES):
                            last = f(DTXT[:, t, :], PS[:, 4 + t, :], ACT.Copy)
                        last.then_inc(mine.sem(f"dtx{d}"), 1)

                        runc = (b * 2 + d) * (N * DC) + CREDIT
                        act.drain()
                        after("dve", f"dtx{d}_1")
                        lo = 1 - d
                        with act.Fori(0, N // UN) as i:
                            for k in range(UN):
                                n = i * UN + k
                                act.wait_ge(ss["input_ready"], runc + n * DC - DC)
                                for t in range(ACT_TILES):
                                    f(UT[:, k % 2, t, :], DTXT[:, t, :], ACT.Copy,
                                      scale=BT[:, t, ds(n, 1)]).then_inc(ss["scaled_act"], 1)
                                for j in range(DC):
                                    act.wait_ge(ss["state_ready"], runc + n * DC + (j + 1 - DC))
                                    seqs = DA[:, j, :].rearrange("p (b s) -> p b s", s=SEQ)
                                    dts = DT[:, j, :].rearrange("p (b s) -> p b s", s=SEQ)
                                    f(seqs[:, :, lo:lo + SEQ - 1], dts[:, :, lo:lo + SEQ - 1], ACT.Exp,
                                      scale=decay[:, j, ds(n, 1)]).then_inc(ss["decay_ready"], 1)
                    norms(0, 6)
                    tables(SILU)
                    for j in range(cfg["hidden"]):
                        after("pe", f"gate{j}")
                        f(SG[:, j, :], PS[:, 2 * j, :], ACT.Silu).then_inc(mine.sem(f"silu{j}"), 1)

        @block.vector
        def _(dve):
            v = nc.vector
            v.memset(ZERO[:, :], 0.0)
            v.memset(EPSC[:, :], EPS)
            v.memset(ONEC[:, :], 1.0)
            v.memset(MEAN[:, :], 1.0 / D)
            v.memset(ZROW[:, :], 0.0).then_inc(const_ready, 1)
            dve.wait_ge(dma_small, 16 * NSMALL)
            v.tensor_copy(IDB[:, :], IDENT[:, :])
            v.tensor_scalar(KEYADD[:, :, :], KEYU8[:, :, :], -3e38, 10.0, ALU.mult, ALU.mult).then_inc(const_ready, 1)
            dve.wait_ge(decay_exp, 1)
            v.tensor_scalar(A1[:, :, :], A1[:, :, :], -1.0, None, ALU.mult)
            v.tensor_scalar(A3[:, :, :, :], A3[:, :, :, :], -1.0, None, ALU.mult)
            dve.wait_ge(mods_psum, 1)
            flat = PS[:, 0:3, :].rearrange("p b n -> p (b n)")
            for i, s in enumerate(SITES):
                for kind, first in enumerate((s["scale"], s["shift"], s["gate"])):
                    if first is not None:
                        o = (i * 3 + kind) * KC * BATCH
                        c = VCOL[s["b"]] + first
                        v.tensor_tensor(MOD[:, i, kind, :, :],
                                        flat[:, o:o + KC * BATCH].rearrange("p (c n) -> p c n", c=KC),
                                        VEC[:, c:c + KC].unsqueeze(2).broadcast_to([P, KC, BATCH]), ALU.add)
            dve.drain()
            for i in range(len(SITES)):
                v.tensor_scalar(MOD[:, i, SCALE, :, :], MOD[:, i, SCALE, :, :], 1.0, None, ALU.add)
            dve.drain()
            for i, s in enumerate(SITES):
                if s["norm"]:
                    wcol, bcol = (VEC[:, VCOL[n]:VCOL[n] + KC].unsqueeze(2).broadcast_to([P, KC, BATCH])
                                  for n in s["norm"])
                    v.tensor_tensor(TMP_A[:, 0:KC * BATCH].rearrange("p (c n) -> p c n", c=KC),
                                    MOD[:, i, SCALE, :, :], bcol, ALU.mult)
                    dve.drain()
                    v.tensor_tensor(MOD[:, i, SHIFT, :, :], MOD[:, i, SHIFT, :, :],
                                    TMP_A[:, 0:KC * BATCH].rearrange("p (c n) -> p c n", c=KC), ALU.add)
                    v.tensor_tensor(MOD[:, i, SCALE, :, :], MOD[:, i, SCALE, :, :], wcol, ALU.mult)
                    dve.drain()
            v.tensor_copy(ZERO[:, :], ZERO[:, :]).then_inc(mods_ready, 1)

            for l in range(4):
                st = steps[l]
                mine = st["dve"]
                if l in MAMBA:
                    for n in ("scaled_dve", "state_ready", "prod_vector", "pair_added"):
                        dve.sem_inc(scan_sems[l][n], CREDIT)
                if l == 0:
                    dve.wait_ge(dma_x, 16 * NBLK)

                def seqs(ap):
                    return ap.rearrange("p (b s) -> p b s", s=SEQ)

                def modulation(site, kind, c, b):
                    return MOD[:, site, kind, c, ds(b * BB, BB)].unsqueeze(2).broadcast_to([P, BB, SEQ])

                def centre(bank, xc, b, done):
                    for c in range(KC):
                        last = v.tensor_tensor(xc[:, c, :], X[:, c, ds(b * T, T)], PS[:, bank, :], ALU.subtract)
                    last.then_inc(done, 1)

                def scale_norm(site, xc, h, b):
                    for c in range(KC):
                        v.tensor_tensor(seqs(h[:, c, :]), seqs(xc[:, c, :]), modulation(site, SCALE, c, b), ALU.mult)

                def modulate(site, rstd, h, b, done):
                    for c in range(KC):
                        v.tensor_tensor(h[:, c, :], h[:, c, :], rstd, ALU.mult)
                    dve.drain()
                    for c in range(KC):
                        last = v.tensor_tensor(seqs(h[:, c, :]), seqs(h[:, c, :]), modulation(site, SHIFT, c, b),
                                               ALU.add)
                    last.then_inc(done, 1)

                LN, NEXT = (LN_A, NEXT_A) if l in ATTN else (LN_M, NEXT_M)
                ld = lead[l]
                dve.drain()
                dve.wait_ge(ld["pe"].semaphore, ld["pe"].lead("lead_mean"))
                centre(0, LN[0], 0, ld["dve"].sem("lead_centred"))
                dve.drain()
                scale_norm(2 * l, LN[0], H1, 0)
                dve.drain()
                dve.wait_ge(ld["act"].semaphore, ld["act"].lead("lead_rstd"))
                modulate(2 * l, LN[2], H1, 0, ld["dve"].sem("lead_h"))
                dve.drain()
                dve.sem_inc(mine.semaphore, BASE)
                with dve.Fori(0, NBLK) as b:
                    def after(engine, name):
                        dve.wait_ge(st[engine].semaphore, st[engine].count(b, name))

                    def xblk(c):
                        return X[:, c, ds(b * T, T)]

                    def mod(site, kind, c):
                        return modulation(site, kind, c, b)

                    nxt = (b + 1) % NBLK

                    def next_centre(bank):
                        after("pe", "next_mean")
                        centre(bank, NEXT[0], nxt, mine.sem("next_centred"))
                        dve.drain()
                        scale_norm(2 * l, NEXT[0], H1, nxt)

                    def norms(bank):
                        after("pe", "ln2_mean")
                        centre(bank, LN[0], b, mine.sem("ln2_centred"))
                        dve.drain()
                        scale_norm(2 * l + 1, LN[0], H2, b)
                        after("act", "next_rstd")
                        modulate(2 * l, NEXT[2], H1, nxt, mine.sem("next_h"))
                        after("act", "ln2_rstd")
                        modulate(2 * l + 1, LN[2], H2, b, mine.sem("ln2_h"))

                    def residual(name, c, bank, bias, site, tmp):
                        if site is None:
                            v.scalar_tensor_tensor(out=xblk(c), in0=PS[:, bank, :], scalar=bias, in1=xblk(c),
                                                   op0=ALU.add, op1=ALU.add).then_inc(mine.sem(name), 1)
                            return
                        v.scalar_tensor_tensor(out=seqs(tmp), in0=seqs(PS[:, bank, :]), scalar=bias,
                                               in1=mod(site, GATE, c), op0=ALU.add, op1=ALU.mult)
                        dve.drain()
                        v.tensor_tensor(xblk(c), xblk(c), tmp, ALU.add).then_inc(mine.sem(name), 1)
                        dve.drain()

                    if l in ATTN:
                        cfg = ATTN[l]
                        site = lambda i: 2 * l + i if cfg["gated"] else None
                        def sub(p):
                            after("pe", f"score{p}")
                            add = KEYADD[:, ds(b * PAIRS + p, 1), :] if l == 0 else CAUSAL[:, :].unsqueeze(1)
                            s = S[:, p, :, :]
                            v.scalar_tensor_tensor(
                                out=s, in0=PS[:, 2 * (p % 2):2 * (p % 2) + 2, :].rearrange("p c (h m) -> p (c h) m", m=SEQ),
                                scalar=float(HD) ** -0.5, in1=add.broadcast_to([P, HEADS, SEQ]),
                                op0=ALU.mult, op1=ALU.add)
                            dve.drain()
                            v.reduce_max(mx[:, :], s, AX.X)
                            dve.drain()
                            v.tensor_tensor(s, s, mx[:, :].unsqueeze(2).broadcast_to([P, HEADS, SEQ]),
                                            ALU.subtract).then_inc(mine.sem(f"sub{p}"), 1)

                        def normalise(p):
                            s = S[:, p, :, :]
                            after("act", f"exp{p}")
                            v.reduce_sum(sm[:, :], s, AX.X)
                            dve.drain()
                            v.reciprocal(mx2[:, :], sm[:, :])
                            dve.drain()
                            v.tensor_tensor(s, s, mx2[:, :].unsqueeze(2).broadcast_to([P, HEADS, SEQ]),
                                            ALU.mult).then_inc(mine.sem(f"norm{p}"), 1)
                            dve.drain()

                        dve.drain()
                        sub(0)
                        for p in range(PAIRS):
                            if p + 1 < PAIRS:
                                sub(p + 1)
                            normalise(p)
                        next_centre(2)
                        for c in range(KC):
                            after("pe", f"proj{c}")
                            residual(f"x{c}", c, c, vec(cfg["bo"], c), site(0), TMP_A)
                        norms(6)
                        for c in range(KC):
                            after("pe", f"down{c}")
                            residual(f"end{c}", c, 4 + c, vec(cfg["b2"], c), site(1), TMP_A)
                        dve.drain()
                        continue

                    cfg, ss = MAMBA[l], scan_sems[l]
                    N = cfg["states"]
                    for d in range(2):
                        pre = cfg["dirs"][d]
                        dt_bias = "L1_cond_dt_proj_b" if l == 1 else f"L3_cond_{pre}dt_bias"
                        skip = "L1_cond_Dp" if l == 1 else f"L3_cond_{pre}D"
                        if cfg["conv"]:
                            if d == 1:
                                dve.drain()
                            for tap in range(3, -1, -1):
                                shift = 3 - tap
                                for j in range(DC):
                                    if shift == 0:
                                        after("act", f"in0_{j}")
                                    col = VCONV + j * 4 + tap
                                    wt = VEC[:, col:col + 1]
                                    src, dst = seqs(XPRE[:, j, :]), seqs(HB[:, j, :])
                                    if shift == 0:
                                        last = v.tensor_scalar(HB[:, j, :], XPRE[:, j, :], wt, None, ALU.mult)
                                        continue
                                    to, fr = (slice(shift, SEQ), slice(0, SEQ - shift))
                                    if d == 1:
                                        to, fr = fr, to
                                    last = v.scalar_tensor_tensor(out=dst[:, :, to], in0=src[:, :, fr], scalar=wt,
                                                                  in1=dst[:, :, to], op0=ALU.mult, op1=ALU.add)
                                    if shift == 3:
                                        last.then_inc(mine.sem(f"conv{d}_{j}"), 1)
                                if shift < 3:
                                    dve.drain()
                        for j in range(DC):
                            after("pe", f"dt{d}_{j}")
                            v.tensor_scalar(DT[:, j, :], PS[:, 4 + j, :], vec(dt_bias, j), 0.0,
                                            ALU.add, ALU.max).then_inc(mine.sem(f"relu{d}_{j}"), 1)
                        after("pe", f"C{d}")
                        v.tensor_copy(CROW[0:N, :], PS[0:N, 1, :]).then_inc(mine.sem(f"C{d}"), 1)
                        for h in range(2):
                            two = slice(2 * h, 2 * h + 2)
                            after("act", f"soft{d}_{h}")
                            v.tensor_tensor(DT[:, two, :], DT[:, two, :], SOFT[:, two, :], ALU.add)
                            dve.drain()
                            v.tensor_tensor(HB[:, two, :], DT[:, two, :], XS[:, two, :],
                                            ALU.mult).then_inc(mine.sem(f"dtx{d}_{h}"), 1)
                        first = 0 if d == 0 else SEQ - 1
                        v.memset(DA.rearrange("p j (b s) -> p (j b) s", s=SEQ)[:, :, first:first + 1], 0.0)
                        dve.drain()
                        after("pe", f"dtx{d}")
                        for t in range(ACT_TILES, TT):
                            last = v.tensor_copy(DTXT[:, t, :], PS[:, 4 + t, :])
                        last.then_inc(mine.sem(f"dtxt{d}"), 1)
                        dve.drain()
                        after("act", f"B{d}")

                        runc = (b * 2 + d) * (N * DC) + CREDIT

                        run_vector = (b * 2 + d) * (N // 2 * VECTOR_PRODUCTS) + CREDIT

                        def scale_input(n, parity):
                            dve.wait_ge(ss["input_ready"], runc + n * DC - DC)
                            for t in range(ACT_TILES, TT):
                                v.tensor_scalar(UT[:, parity, t, :], DTXT[:, t, :], BT[:, t, ds(n, 1)], None,
                                                ALU.mult).then_inc(ss["scaled_dve"], 1)

                        def states(i, final):
                            for k in range(UN):
                                n = i * UN + k
                                for j in range(DC):
                                    dve.wait_ge(ss["input_ready"], runc + n * DC + (j + 1))
                                    dve.wait_ge(ss["decay_ready"], runc + n * DC + (j + 1))
                                    if k % 2 or j >= VECTOR_PRODUCTS:
                                        dve.wait_ge(ss["prod_ready"], products(N, b * 2 + d, i, k - 1, j))
                                    else:
                                        dve.wait_ge(ss["prod_vector"], run_vector
                                                    + (i * (UN // 2) + k // 2) * VECTOR_PRODUCTS
                                                    + (j + 1 - VECTOR_PRODUCTS))
                                    step = slice(None, None, -1) if d else slice(None)
                                    v.tensor_tensor_scan(HB[:, j, step], DA[:, j, step], PS[:, 4 + j, step],
                                                         0.0, ALU.mult, ALU.add).then_inc(ss["state_ready"], 1)
                                    if j == 0 and not (final and k == UN - 1):
                                        scale_input(n + 1, (k + 1) % 2)
                                    if k % 2 and j == max(VECTOR_PRODUCTS, 1):
                                        for c in range(VECTOR_PRODUCTS):
                                            multiply_odd(i, k, c)
                                    if k % 2 and 0 <= j - (DC - PAIRED) < PAIRED:
                                        add_pair(i, k, j - (DC - PAIRED))

                        def multiply_odd(i, k, j):
                            dve.wait_ge(ss["state_ready"], runc + (i * UN + k) * DC + (j + 1))
                            dve.wait_ge(c_loaded[l][k // 2], (b * 2 + d) * (N // UN * 16) + i * 16 + 16)
                            dve.wait_ge(ss["pair_summed"], (b * 2 + d) * (N // 2 * PAIRED)
                                        + (i * (UN // 2) + k // 2) * PAIRED + (CREDIT + j + 1 - PAIRED))
                            v.tensor_tensor(PR2[l][:, j, :], HB[:, j, :], CB[l][:, k // 2, 1, :],
                                            ALU.mult).then_inc(ss["prod_vector"], 1)

                        def add_pair(i, k, j):
                            q = k
                            if j < VECTOR_PRODUCTS:
                                q = k - 1
                                dve.wait_ge(ss["prod_vector"], run_vector
                                            + (i * (UN // 2) + k // 2) * VECTOR_PRODUCTS + (j + 1))
                            dve.wait_ge(ss["prod_ready"], products(N, b * 2 + d, i, q, j))
                            v.tensor_tensor(PR2[l][:, j, :], PR2[l][:, j, :], PR[:, j, :],
                                            ALU.add).then_inc(ss["pair_added"], 1)

                        scale_input(0, 0)
                        with dve.Fori(0, N // UN - 1) as i:
                            states(i, False)
                        states(N // UN - 1, True)

                        into = YS if l == 1 and d == 0 else HB
                        dve.drain()
                        for j in Y_ORDER:
                            if j == PAIRED:
                                dve.wait_ge(ss["sum_done"], (b * 2 + d) * (N * SINGLE) + (CREDIT + N * SINGLE))
                            elif j == 0:
                                dve.wait_ge(ss["pair_summed"],
                                            (b * 2 + d) * (N // 2 * PAIRED) + (CREDIT + N // 2 * PAIRED))
                            last = v.scalar_tensor_tensor(out=into[:, j, :], in0=XS[:, j, :], scalar=vec(skip, j),
                                                          in1=PS[:, j, :], op0=ALU.mult, op1=ALU.add)
                            if l == 1 and d == 0:
                                last.then_inc(mine.sem(f"y{d}_{j}"), 1)
                        dve.drain()
                        if l == 1 and d == 0:
                            continue
                        if l == 1:
                            for j in range(DC):
                                v.tensor_tensor(HB[:, j, :], HB[:, j, :], YS[:, j, :], ALU.add)
                            dve.drain()
                        for j in Y_ORDER:
                            v.tensor_tensor(HB[:, j, :], HB[:, j, :], Z[:, j, :],
                                            ALU.mult).then_inc(mine.sem(f"y{d}_{j}"), 1)
                        if d == 1:
                            next_centre(6)
                        for c in range(KC):
                            after("pe", f"out{d}_{c}")
                            residual(f"x{d}_{c}", c, 2 + 2 * d + c, ZERO[:, 0:1], 2 * l, TMP_M)
                    norms(0)
                    for j in range(cfg["hidden"]):
                        after("pe", f"up{j}")
                        after("act", f"silu{j}")
                        v.tensor_tensor(GLU[:, j, :], SG[:, j, :], PS[:, 2 * j + 1, :],
                                        ALU.mult).then_inc(mine.sem(f"glu{j}"), 1)
                    for c in range(KC):
                        after("pe", f"down{c}")
                        residual(f"end{c}", c, c, ZERO[:, 0:1], 2 * l + 1, TMP_M)
                    dve.drain()

        @block.gpsimd
        def _(pool):
            g = nc.gpsimd
            g.memset(CAUSAL[:, :], 0.0)
            pool.drain()
            for r in range(2):
                g.affine_select(out=CAUSAL[64 * r:64 * r + 64, :], in_=CAUSAL[64 * r:64 * r + 64, :],
                                compare_op=ALU.is_ge, fill=-1e30, base=0, pattern=[[-1, SEQ]], channel_multiplier=1)
            pool.drain()
            g.memset(VBD, 0.0).then_inc(vbd_zeroed, 1)
            pool.sem_inc(const_ready, 1)

            pool.wait_ge(mods_psum, 1)
            g.memset(W1["dt"], 0.0)
            g.memset(DTR, 0.0)
            pool.drain()
            pool.sem_inc(rank_zeroed, 1)

            for l in range(4):
                st = steps[l]
                mine = st["pool"]
                pool.sem_inc(mine.semaphore, BASE)
                if l == 2:
                    pool.wait_ge(steps[1]["dve"].semaphore, steps[1]["dve"].before(NBLK))
                    g.memset(VBD, 0.0).then_inc(vbd_zeroed, 1)
                if l in MAMBA:
                    pool.sem_inc(scan_sems[l]["prod_ready"], CREDIT)
                with pool.Fori(0, NBLK) as b:
                    if l in ATTN:
                        pool.wait_ge(st["act"].semaphore, st["act"].count(b, "k1"))
                        for p in range(PAIRS):
                            if p >= 2:
                                pool.wait_ge(st["pe"].semaphore, st["pe"].count(b, f"score{p - 2}"))
                            for c in range(KC):
                                for r in range(2):
                                    o = (2 * p + r) * SEQ
                                    last = g.tensor_tensor(
                                        KBD[:, p % 2, c, r, :].rearrange("p (h m) -> p h m", m=SEQ),
                                        KF[:, c, o:o + SEQ].unsqueeze(1).broadcast_to([P, HPC, SEQ]),
                                        HMASK[:, :].unsqueeze(2).broadcast_to([P, HPC, SEQ]), ALU.mult)
                            last.then_inc(mine.sem(f"kbd{p}"), 1)
                        continue
                    cfg, ss = MAMBA[l], scan_sems[l]
                    N = cfg["states"]
                    for d in range(2):
                        run_c = (b * 2 + d) * (N // UN * 16) + 16
                        runc = (b * 2 + d) * (N * DC) + CREDIT
                        run_single = (b * 2 + d) * (N * SINGLE) + CREDIT
                        run_pair = (b * 2 + d) * (N // 2 * PAIRED) + CREDIT
                        with pool.Fori(0, N // UN) as i:
                            for k in range(UN):
                                n = i * UN + k
                                if k % 2 == 0:
                                    pool.wait_ge(c_loaded[l][k // 2], run_c + i * 16)
                                for j in range(DC):
                                    pool.wait_ge(ss["state_ready"], runc + n * DC + (j + 1))
                                    if k % 2 and j < VECTOR_PRODUCTS:
                                        continue
                                    into = PR[:, j, :]
                                    if j >= PAIRED:
                                        pool.wait_ge(ss["sum_done"], run_single + n * SINGLE + (j + 1 - DC))
                                    elif k % 2 == 0:
                                        pool.wait_ge(ss["pair_added"],
                                                     run_pair + (i * (UN // 2) + k // 2) * PAIRED + (j + 1 - PAIRED))
                                    else:
                                        pool.wait_ge(ss["pair_summed"],
                                                     run_pair + (i * (UN // 2) + k // 2) * PAIRED + (j + 1 - PAIRED))
                                        into = PR2[l][:, j, :]
                                    g.tensor_tensor(into, HB[:, j, :], CB[l][:, k // 2, k % 2, :],
                                                    ALU.mult).then_inc(ss["prod_ready"], 1)


_TRANSPOSED = ("L0_cond_w_adaln1", "L0_cond_w_adaln2", "L0_cond_wq", "L0_cond_wk", "L0_cond_wv",
               "L0_cond_wo", "L0_cond_w1", "L0_cond_w2")
_PLAIN = ("L1_cond_adaln1_W", "L1_cond_adaln2_W", "L1_cond_in_proj_W", "L1_cond_x_proj_W", "L1_cond_dt_proj_W",
          "L1_cond_A_log", "L1_cond_out_proj_W", "L1_cond_w1", "L1_cond_w2", "L1_cond_w3", "L2_cond_Wqkv",
          "L2_cond_Wproj", "L2_cond_W1", "L2_cond_W2", "L2_cond_Wada", "L3_cond_adaln_mamba_w",
          "L3_cond_adaln_mlp_w", "L3_cond_mlp_w1", "L3_cond_mlp_w2", "L3_cond_mlp_w3", "L3_cond_fwd_in_w",
          "L3_cond_fwd_xproj_w", "L3_cond_fwd_A_log", "L3_cond_fwd_out_w", "L3_cond_bwd_in_w",
          "L3_cond_bwd_xproj_w", "L3_cond_bwd_A_log", "L3_cond_bwd_out_w")


def kernel(**inputs):
    import concourse.bacc as bacc
    from concourse.bass_utils import run_bass_kernel_spmd

    arrays = {k: np.asarray(v) for k, v in inputs.items()}
    laid = {k: arrays[k].T for k in _TRANSPOSED}
    laid |= {k: arrays[k] for k in _PLAIN}
    laid["x_t"] = arrays["x"].reshape(TOKENS, D).T
    laid["cond_t"] = arrays["cond_1024"].T
    laid["mask"] = arrays["mask_BxS_bf0"]
    columns = [arrays[n].reshape(c, P).T for n, c in VECTORS]
    columns.append(arrays["L1_cond_conv_w"].reshape(DC, P, 4).transpose(1, 0, 2).reshape(P, DC * 4))
    laid["vectors"] = np.concatenate(columns, axis=1)
    laid["ident"] = np.eye(P, dtype=np.float32)
    laid["head_mask"] = np.kron(np.eye(HPC), np.ones((HD, 1))).astype(np.float32)

    nc = bacc.Bacc("TRN2", target_bir_lowering=False, num_devices=1)
    feeds, aps = {}, {}
    for name, value in laid.items():
        value = np.ascontiguousarray(value)
        feeds[f"in_{name}"] = value
        aps[name] = nc.dram_tensor(f"in_{name}", value.shape, mybir.dt.from_np(value.dtype), kind="ExternalInput").ap()
    out = nc.dram_tensor("out_t", (D, TOKENS), mybir.dt.float32, kind="ExternalOutput").ap()
    c_rows = nc.dram_tensor("c_rows", (2, 64, T), mybir.dt.float32, kind="Internal").ap()
    build(nc, aps, out, c_rows)
    r = run_bass_kernel_spmd(nc, [feeds], core_ids=[0])
    return np.ascontiguousarray(r.results[0]["out_t"].T).reshape(BATCH, SEQ, D)
```

```python
from contextlib import ExitStack

import numpy as np

import concourse.bass as bass
from concourse import mybir

P = 128
D = 256
KC = D // P
BATCH, SEQ = 32, 64
TOKENS = BATCH * SEQ
T = 512
NBLK = TOKENS // T
BB = T // SEQ
PAIRS = BB // 2
TT = T // P
HEADS, HD = 16, 16
HPC = P // HD
MLP = 1024
DI = 512
DC = DI // P
UN = 4
PAIRED = 2
SINGLE = DC - PAIRED
VECTOR_PRODUCTS = 1
Y_ORDER = [*range(PAIRED, DC), *range(PAIRED)]
ACT_TILES = 3
BASE = 12
CREDIT = 16
EPS = 1e-5

VECTORS = [
    ("L0_cond_b_adaln1", 4), ("L0_cond_b_adaln2", 4), ("L0_cond_bq", 2), ("L0_cond_bk", 2),
    ("L0_cond_bv", 2), ("L0_cond_bo", 2), ("L0_cond_b1", 8), ("L0_cond_b2", 2),
    ("L1_cond_norm1_w", 2), ("L1_cond_norm1_b", 2), ("L1_cond_norm2_w", 2), ("L1_cond_norm2_b", 2),
    ("L1_cond_adaln1_b", 6), ("L1_cond_adaln2_b", 6), ("L1_cond_conv_b", 4),
    ("L1_cond_dt_proj_b", 4), ("L1_cond_Dp", 4),
    ("L2_cond_bproj", 2), ("L2_cond_b1", 8), ("L2_cond_b2", 2), ("L2_cond_g1", 2),
    ("L2_cond_be1", 2), ("L2_cond_g2", 2), ("L2_cond_be2", 2), ("L2_cond_bada", 12),
    ("L3_cond_adaln_mamba_b", 6), ("L3_cond_adaln_mlp_b", 6),
    ("L3_cond_fwd_dt_bias", 4), ("L3_cond_bwd_dt_bias", 4), ("L3_cond_fwd_D", 4), ("L3_cond_bwd_D", 4),
]
VCOL, _at = {}, 0
for _name, _n in VECTORS:
    VCOL[_name] = _at
    _at += _n
VCONV = _at
NVEC = _at + 16

SITES = [
    dict(w="L0_cond_w_adaln1", at=0, b="L0_cond_b_adaln1", scale=0, shift=2, gate=None, norm=None, silu=False),
    dict(w="L0_cond_w_adaln2", at=0, b="L0_cond_b_adaln2", scale=0, shift=2, gate=None, norm=None, silu=False),
    dict(w="L1_cond_adaln1_W", at=0, b="L1_cond_adaln1_b", scale=2, shift=0, gate=4,
         norm=("L1_cond_norm1_w", "L1_cond_norm1_b"), silu=True),
    dict(w="L1_cond_adaln2_W", at=0, b="L1_cond_adaln2_b", scale=2, shift=0, gate=4,
         norm=("L1_cond_norm2_w", "L1_cond_norm2_b"), silu=True),
    dict(w="L2_cond_Wada", at=0, b="L2_cond_bada", scale=2, shift=0, gate=4,
         norm=("L2_cond_g1", "L2_cond_be1"), silu=True),
    dict(w="L2_cond_Wada", at=6, b="L2_cond_bada", scale=8, shift=6, gate=10,
         norm=("L2_cond_g2", "L2_cond_be2"), silu=True),
    dict(w="L3_cond_adaln_mamba_w", at=0, b="L3_cond_adaln_mamba_b", scale=2, shift=0, gate=4, norm=None, silu=False),
    dict(w="L3_cond_adaln_mlp_w", at=0, b="L3_cond_adaln_mlp_b", scale=2, shift=0, gate=4, norm=None, silu=False),
]
SCALE, SHIFT, GATE = range(3)

ATTN = {
    0: dict(bq="L0_cond_bq", bk="L0_cond_bk", bv="L0_cond_bv", bo="L0_cond_bo",
            b1="L0_cond_b1", b2="L0_cond_b2", gated=False),
    2: dict(bq=None, bk=None, bv=None, bo="L2_cond_bproj", b1="L2_cond_b1", b2="L2_cond_b2", gated=True),
}
MAMBA = {
    1: dict(states=32, conv=True, hidden=3, dirs=("", ""), rank=16),
    3: dict(states=64, conv=False, hidden=4, dirs=("fwd_", "bwd_"), rank=None),
}


class Steps:

    def __init__(self, semaphore, names):
        self.semaphore, self.names, self.next = semaphore, names, 0
        self.place = {n: i + 1 for i, n in enumerate(names)}
        assert len(self.place) == len(names)

    def sem(self, name):
        assert self.names[self.next] == name, (self.names[self.next], name)
        self.next += 1
        return self.semaphore

    def count(self, block, name):
        return block * len(self.names) + (BASE + self.place[name])

    def previous(self, block, name):
        ahead = len(self.names) - self.place[name]
        assert ahead < BASE
        return block * len(self.names) + (BASE - ahead)

    def lead(self, name):
        return self.place[name]

    def before(self, block):
        return block * len(self.names) + BASE


def norm_steps(name):
    return [[f"{name}_mean", f"{name}_var"], [f"{name}_square", f"{name}_rstd"], [f"{name}_centred", f"{name}_h"]]


ACT_NORMS = ["next_square", "next_rstd", "ln2_square0", "ln2_square1", "ln2_rstd"]
DVE_NORMS = ["ln2_centred0", "ln2_centred1", "next_h", "ln2_h0", "ln2_h1"]


def attention_steps():
    pe = ["k0", "k1", "q0", "q1", "v0", "score0", "v1"] + [f"score{p}" for p in range(1, PAIRS)]
    act = ["k0", "k1", "q0", "q1", "v0", "v1", "exp0"]
    dve = ["sub0"]
    pool = [f"kbd{p}" for p in range(PAIRS)] + [f"norm{p}" for p in range(PAIRS)]
    for p in range(PAIRS):
        pe += [f"tr{p}"] + (["next_mean"] if p == PAIRS - 1 else []) + [f"av{p}"]
        act += ([f"exp{p + 1}"] if p + 1 < PAIRS else []) + [f"pt{p}", f"o{p}"]
        dve += ([f"sub{p + 1}"] if p + 1 < PAIRS else []) + [f"inverse{p}"]
    pe += ["proj0", "proj1", "next_var", "ln2_mean", "ln2_var"]
    dve += ["next_centred", "x0", "x1"] + DVE_NORMS
    act += ACT_NORMS
    pe += [f"up{j}" for j in range(MLP // P)] + ["down0", "down1"]
    act += [f"gelu{j}" for j in range(MLP // P)]
    dve += ["end0", "end1"]
    return pe, act, dve, pool


def mamba_steps(cfg):
    pe, act, dve = [], [], []
    for d in range(2):
        if d == 0:
            pe += [f"in{d}_{j}" for j in range(2 * DC)]
        elif not cfg["conv"]:
            pe += [f"in{d}_{j}" for j in range(DC, 2 * DC)]
        if d == 0 or not cfg["conv"]:
            act += [f"in{d}_{j}" for j in range(2 * DC)]
        if cfg["conv"]:
            if d == 0:
                dve += [f"conv{d}_{j}" for j in range(DC)]
            act += [f"xs{d}"]
            pe += [f"rank{d}"]
            act += [f"rank{d}"]
        pe += [f"dt{d}_{j}" for j in range(DC)] + [f"C{d}", f"B{d}", f"dtx{d}"]
        act += [f"soft{d}_0", f"soft{d}_1", f"B{d}", f"dtx{d}"]
        dve += [f"relu{d}_0", f"relu{d}_1", f"dtx{d}_0", f"relu{d}_2", f"relu{d}_3", f"C{d}", f"dtx{d}_1", f"dtxt{d}"]
        dve += [f"y{d}_{j}" for j in Y_ORDER]
        if d == 0 and not cfg["conv"]:
            pe += [f"in1_{j}" for j in range(DC)]
        if d == 1:
            pe += ["next_mean"]
            dve += ["next_centred"]
        if d == 1 or not cfg["conv"]:
            pe += [f"out{d}_{j}" for j in range(KC)]
            dve += [f"x{d}_{j}" for j in range(KC)]
    pe += ["next_var", "ln2_mean", "ln2_var"]
    act += ACT_NORMS
    dve += DVE_NORMS
    for j in range(cfg["hidden"]):
        pe += [f"gate{j}", f"up{j}"]
        act += [f"silu{j}"]
        dve += [f"glu{j}"]
    pe += ["down0", "down1"]
    dve += ["end0", "end1"]
    return pe, act, dve, [f"conv1_{j}" for j in range(DC)] if cfg["conv"] else []


def products(states, run, group, k, j):
    per_pair = 2 * DC - VECTOR_PRODUCTS
    assert k % 2 == 0 or j < 0 or j >= VECTOR_PRODUCTS
    return ((run * (states // 2) + group * (UN // 2)) * per_pair
            + (k // 2 * per_pair + (k % 2) * (DC - VECTOR_PRODUCTS) + (j + 1) + CREDIT))


def build(nc, a, out, c_rows):
    f32, u8 = mybir.dt.float32, mybir.dt.uint8
    ALU, ACT, AX = mybir.AluOpType, mybir.ActivationFunctionType, mybir.AxisListType
    ds = bass.ds
    ctx = ExitStack()
    with ctx:
        def sb(name, shape, dt=f32):
            return ctx.enter_context(nc.sbuf_tensor(name, shape, dt))

        def sem(name):
            return ctx.enter_context(nc.semaphore(name))

        X = sb("x_stream", [P, KC, TOKENS])
        MOD = sb("modulation", [P, len(SITES), 3, KC, BATCH])
        VEC = sb("vectors", [P, NVEC])
        ZERO = sb("zero_col", [P, 1])
        EPSC = sb("eps_col", [P, 1])
        ONEC = sb("one_col", [P, 1])
        COND = sb("cond", [P, KC, BATCH])
        CSILU = sb("cond_silu", [P, KC, BATCH])
        IDENT = sb("ident", [P, P])
        MEAN = sb("mean_weights", [P, P])
        HMASK = sb("head_mask", [P, HPC])
        CAUSAL = sb("causal_add", [P, SEQ])
        KEYADD = sb("key_mask_add", [P, BATCH // 2, SEQ])
        KEYU8 = sb("key_mask", [P, BATCH // 2, SEQ], u8)
        A1 = sb("decay1", [P, DC, 32])
        A3 = sb("decay3", [P, 2, DC, 64])
        WA = sb("weights_a", [P, 6144])
        WC = sb("weights_c", [P, 15360])
        WORK = sb("work", [P, 21504])
        PS = ctx.enter_context(nc.psum_tensor("psum", [P, 8, T], f32))

        def region(base, at, *dims):
            n = int(np.prod(dims))
            v = base[:, at:at + n]
            if len(dims) == 1:
                return v
            names = "abcd"[:len(dims)]
            return v.rearrange(f"p ({' '.join(names)}) -> p {' '.join(names)}",
                               **{k: s for k, s in zip(names[1:], dims[1:])})

        H = H1 = sb("normed1", [P, KC, T])
        H2 = region(WORK, 0, KC, T)
        Q = region(WORK, 1024, KC, T)
        KF = region(WORK, 2048, KC, T)
        KBD = region(WORK, 3072, 2, KC, 2, HPC * SEQ)
        VBD = WORK[:, 7168:9216].rearrange("p (b h r d) -> p b h r d", b=BB, h=HEADS // 2, r=2)
        S = region(WORK, 14336, PAIRS, HEADS, SEQ)
        PT = region(WORK, 11264, 2, HEADS // 2, P)
        AO = region(WORK, 13312, KC, T)
        G = region(WORK, 14336, MLP // P, T)
        XC_A = region(WORK, 18432, KC, T)
        SQ_A = region(WORK, 19456, KC, T)
        RSTD_A = region(WORK, 20480, T)
        LN_A = (XC_A, SQ_A, RSTD_A)
        NEXT_A = (region(WORK, 3072, KC, T), region(WORK, 4096, KC, T), region(WORK, 5120, T))
        TMP_A = region(WORK, 20992, T)
        Z = region(WORK, 1024, DC, T)
        XS = region(WORK, 3072, DC, T)
        DT = region(WORK, 5120, DC, T)
        DTXT = region(WORK, 7168, TT, DI)
        UT = region(WORK, 9216, 2, TT, DI)
        DA = region(WORK, 13312, DC, T)
        HB = region(WORK, 15360, DC, T)
        PR = region(WORK, 17408, DC, T)
        BT = region(WORK, 19456, TT, 64)
        CROW = WORK[0:64, 19712:20224]
        CB = {1: region(WC, 11264 + PAIRED * T, 2, 2, T), 3: region(WA, PAIRED * T, 2, 2, T)}
        XC_M, SQ_M = region(WORK, 9216, KC, T), region(WORK, 10240, KC, T)
        RSTD_M, TMP_M = region(WORK, 11264, T), region(WORK, 11776, T)
        LN_M = (XC_M, SQ_M, RSTD_M)
        NEXT_M = (region(WORK, 7168, KC, T), region(WORK, 8192, KC, T), region(WORK, 12288, T))
        PR2 = {1: region(WC, 11264, PAIRED, T), 3: region(WA, 0, PAIRED, T)}
        SOFT = PR
        SG = region(WORK, 13312, 4, T)
        GLU = region(WORK, 15360, 4, T)
        XPRE = region(WC, 6656, DC, T)
        CONV = region(WC, 11264 + (PAIRED + 4) * T, 2, T)
        YS = region(WC, 8704, DC, T)
        DTR = region(WC, 10752, T)

        mx = sb("row_max", [P, HEADS])
        sm = sb("row_sum", [P, PAIRS, HEADS])
        inverse = sb("row_inverse", [P, PAIRS, HEADS])

        WQKVO = region(WA, 0, KC, 4 * D)
        W1A, W2A = region(WA, 2048, KC, MLP), region(WA, 4096, MLP // P, D)
        W1 = dict(inp=region(WC, 0, KC, 2 * DI), rank=region(WC, 2048, DC, 16), B=region(WC, 2112, DC, 32),
                  C=region(WC, 2240, DC, 32),
                  dt=region(WC, 2624, 1, 512), out=region(WC, 3136, DC, D))
        WM1 = dict(w1=region(WC, 4160, KC, 384), w2=region(WC, 4928, KC, 384), w3=region(WC, 5696, 3, D))
        W3 = [dict(inp=region(WC, o, KC, 2 * DI), dt=region(WC, o + 2048, DC, DI), B=region(WC, o + 4096, DC, 64),
                   C=region(WC, o + 4352, DC, 64),
                   out=region(WC, o + 5120, DC, D)) for o in (0, 6144)]
        WM3 = dict(w1=region(WC, 12288, KC, 512), w2=region(WC, 13312, KC, 512), w3=region(WC, 14336, 4, D))
        ADA, at = {}, 0
        for s in SITES:
            if s["w"] not in ADA:
                n = a[s["w"]].shape[1]
                ADA[s["w"]] = region(WC, at, KC, n)
                at += KC * n

        def vec(name, c):
            return ZERO[:, 0:1] if name is None else VEC[:, VCOL[name] + c:VCOL[name] + c + 1]

        dma_cond, dma_small, dma_x, dma_out = sem("dma_cond"), sem("dma_small"), sem("dma_x"), sem("dma_out")
        dma_ada = {name: sem(f"dma_{name}") for name in ADA}
        dma_w = [sem(f"dma_weights{l}") for l in range(4)]
        const_ready = sem("const_ready")
        cond_silu_ready = sem("cond_silu_ready")
        mods_psum = sem("mods_psum")
        mods_ready = sem("mods_ready")
        decay_exp = sem("decay_exp")
        vbd_zeroed = sem("vbd_zeroed")
        rank_zeroed = sem("rank_zeroed")
        lead = [{e: Steps(sem(f"{e}_lead{l}"), n) for e, n in zip(("pe", "act", "dve"), norm_steps("lead"))}
                for l in range(4)]
        steps = []
        for l in range(4):
            lists = attention_steps() if l in ATTN else mamba_steps(MAMBA[l])
            steps.append({e: Steps(sem(f"{e}_steps{l}"), n)
                          for e, n in zip(("pe", "act", "dve", "pool"), lists)})
        crow_out = {l: sem(f"crow_out{l}") for l in MAMBA}
        c_loaded = {l: [sem(f"c_loaded{l}_slot{s}") for s in range(2)] for l in MAMBA}
        scan_sems = {l: {n: sem(f"{n}{l}") for n in (
            "scaled_act",
            "scaled_dve",
            "input_ready",
            "decay_ready",
            "state_ready",
            "prod_ready",
            "prod_vector",
            "sum_done",
            "pair_added",
            "pair_summed",
        )} for l in MAMBA}
        NSMALL = 7

        block = ctx.enter_context(nc.Block())

        @block.sync
        def _(sp):
            def load(dst, src, s):
                sp.dma_start(dst, src).then_inc(s, 16)

            kp = "(k p) n -> p k n"
            load(COND[:, :, :], a["cond_t"].rearrange(kp, p=P), dma_cond)
            load(VEC[:, :], a["vectors"], dma_cond)
            for name, w in ADA.items():
                load(w, a[name].rearrange(kp, p=P), dma_ada[name])
            load(IDENT[:, :], a["ident"], dma_small)
            load(HMASK[:, :], a["head_mask"], dma_small)
            mask = a["mask"].rearrange("(p r) m -> r p m", r=2)
            for r in range(2):
                load(KEYU8[64 * r:64 * r + 64, :, :],
                     mask[r].unsqueeze(0).broadcast_to([64, BATCH // 2, SEQ]), dma_small)
            load(A1[:, :, :], a["L1_cond_A_log"].rearrange(kp, p=P), dma_small)
            for d, pre in enumerate(("fwd_", "bwd_")):
                load(A3[:, d, :, :], a[f"L3_cond_{pre}A_log"].rearrange(kp, p=P), dma_small)
            for b in range(NBLK):
                load(X[:, :, b * T:(b + 1) * T], a["x_t"].rearrange(kp, p=P)[:, :, b * T:(b + 1) * T], dma_x)
            for i, n in enumerate(("wq", "wk", "wv", "wo")):
                load(WQKVO[:, :, i * D:(i + 1) * D], a[f"L0_cond_{n}"].rearrange(kp, p=P), dma_w[0])
            load(W1A, a["L0_cond_w1"].rearrange(kp, p=P), dma_w[0])
            load(W2A, a["L0_cond_w2"].rearrange(kp, p=P), dma_w[0])

            sp.wait_ge(rank_zeroed, 1)
            xp = a["L1_cond_x_proj_W"].rearrange(kp, p=P)
            load(W1["inp"], a["L1_cond_in_proj_W"].rearrange(kp, p=P), dma_w[1])
            load(W1["rank"], xp[:, :, 0:16], dma_w[1])
            load(W1["B"], xp[:, :, 16:48], dma_w[1])
            load(W1["C"], xp[:, :, 48:80], dma_w[1])
            load(W1["dt"][0:16, 0, :], a["L1_cond_dt_proj_W"], dma_w[1])
            load(W1["out"], a["L1_cond_out_proj_W"].rearrange(kp, p=P), dma_w[1])
            for n in ("w1", "w2", "w3"):
                load(WM1[n], a[f"L1_cond_{n}"].rearrange(kp, p=P), dma_w[1])

            sp.wait_ge(steps[0]["dve"].semaphore, steps[0]["dve"].before(NBLK))
            load(WQKVO[:, :, 0:3 * D], a["L2_cond_Wqkv"].rearrange(kp, p=P), dma_w[2])
            load(WQKVO[:, :, 3 * D:4 * D], a["L2_cond_Wproj"].rearrange(kp, p=P), dma_w[2])
            load(W1A, a["L2_cond_W1"].rearrange(kp, p=P), dma_w[2])
            load(W2A, a["L2_cond_W2"].rearrange(kp, p=P), dma_w[2])

            def spread_c(l, b, d):
                N, ss = MAMBA[l]["states"], scan_sems[l]
                r = b * 2 + d
                sp.wait_ge(steps[l]["dve"].semaphore, steps[l]["dve"].count(b, f"C{d}"))
                sp.dma_start(c_rows[d, 0:N, :], CROW[0:N, :]).then_inc(crow_out[l], 16)
                with sp.Fori(0, N // UN) as i:
                    sp.wait_ge(crow_out[l], r * 16 + 16)
                    for s in range(2):
                        sp.wait_ge(ss["pair_summed"], (r * (N // 2) + i * (UN // 2) + s - 1) * PAIRED + CREDIT)
                        sp.dma_start(CB[l][:, s, :, :],
                                     c_rows[d, ds(i * UN + 2 * s, 2), :].unsqueeze(0).broadcast_to([P, 2, T])
                                     ).then_inc(c_loaded[l][s], 16)

            with sp.Fori(0, NBLK) as b:
                for d in range(2):
                    spread_c(1, b, d)

            sp.wait_ge(steps[1]["dve"].semaphore, steps[1]["dve"].before(NBLK))
            for w, pre in zip(W3, ("fwd_", "bwd_")):
                xp = a[f"L3_cond_{pre}xproj_w"].rearrange(kp, p=P)
                load(w["inp"], a[f"L3_cond_{pre}in_w"].rearrange(kp, p=P), dma_w[3])
                load(w["dt"], xp[:, :, 0:DI], dma_w[3])
                load(w["B"], xp[:, :, DI:DI + 64], dma_w[3])
                load(w["C"], xp[:, :, DI + 64:DI + 128], dma_w[3])
                load(w["out"], a[f"L3_cond_{pre}out_w"].rearrange(kp, p=P), dma_w[3])
            for n in ("w1", "w2", "w3"):
                load(WM3[n], a[f"L3_cond_mlp_{n}"].rearrange(kp, p=P), dma_w[3])

            with sp.Fori(0, NBLK) as b:
                for d in range(2):
                    spread_c(3, b, d)
                sp.wait_ge(steps[3]["dve"].semaphore, steps[3]["dve"].count(b, "end1"))
                sp.dma_start(out.rearrange(kp, p=P)[:, :, ds(b * T, T)], X[:, :, ds(b * T, T)]).then_inc(dma_out, 16)
            sp.wait_ge(dma_out, 16 * NBLK)

        NW = [6, 9, 4, 2 * 5 + 3]

        @block.tensor
        def _(pe):
            pe.wait_ge(dma_cond, 16 * 2)
            pe.wait_ge(cond_silu_ready, 1)
            for i, s in enumerate(SITES):
                pe.wait_ge(dma_ada[s["w"]], 16)
                for kind, first in enumerate((s["scale"], s["shift"], s["gate"])):
                    if first is None:
                        continue
                    for c in range(KC):
                        o = (kind * KC + c) * BATCH
                        for k in range(KC):
                            last = nc.tensor.matmul(
                                PS[:, i, o:o + BATCH], ADA[s["w"]][:, k, (first + c) * P:(first + c + 1) * P],
                                (CSILU if s["silu"] else COND)[:, k, :], start=(k == 0), stop=(k == KC - 1))
                last.then_inc(mods_psum, 1)
            pe.wait_ge(dma_small, 16 * NSMALL)
            pe.wait_ge(const_ready, 3)
            pe.wait_ge(dma_x, 16 * NBLK)

            for l in range(4):
                st = steps[l]
                mine = st["pe"]
                pe.sem_inc(mine.semaphore, BASE)
                if l in MAMBA:
                    for n in ("input_ready", "sum_done", "pair_summed"):
                        pe.sem_inc(scan_sems[l][n], CREDIT)
                pe.wait_ge(dma_w[l], 16 * NW[l])
                if l == 0:
                    pe.wait_ge(mods_ready, 1)
                else:
                    pe.wait_ge(steps[l - 1]["dve"].semaphore, steps[l - 1]["dve"].before(NBLK))

                def average(bank, moving, done, ready=None):
                    for k in range(KC):
                        if ready:
                            ready(k)
                        last = nc.tensor.matmul(PS[:, bank, :], MEAN[:, :], moving[k],
                                                start=(k == 0), stop=(k == KC - 1))
                    last.then_inc(done, 1)

                LN, NEXT = (LN_A, NEXT_A) if l in ATTN else (LN_M, NEXT_M)
                ld = lead[l]
                average(0, [X[:, k, 0:T] for k in range(KC)], ld["pe"].sem("lead_mean"))
                pe.wait_ge(ld["act"].semaphore, ld["act"].lead("lead_square"))
                average(1, [LN[1][:, k, :] for k in range(KC)], ld["pe"].sem("lead_var"))

                with pe.Fori(0, NBLK) as b:
                    def after(engine, name):
                        pe.wait_ge(st[engine].semaphore, st[engine].count(b, name))

                    pe.wait_ge(st["dve"].semaphore, st["dve"].previous(b, "next_h"))

                    def next_mean(bank):
                        nxt = ((b + 1) % NBLK) * T
                        average(bank, [X[:, k, ds(nxt, T)] for k in range(KC)], mine.sem("next_mean"))

                    def norms(bank, next_bank, ready):
                        after("act", "next_square")
                        average(next_bank + 1, [NEXT[1][:, k, :] for k in range(KC)], mine.sem("next_var"))
                        average(bank, [X[:, k, ds(b * T, T)] for k in range(KC)], mine.sem("ln2_mean"),
                                lambda k: after("dve", f"{ready}{k}"))
                        average(bank + 1, [LN[1][:, k, :] for k in range(KC)], mine.sem("ln2_var"),
                                lambda k: after("act", f"ln2_square{k}"))

                    def linear(name, psum, weights, moving, chunks, ready=None):
                        for k in range(chunks):
                            if ready:
                                ready(k)
                            last = nc.tensor.matmul(psum, weights[k], moving[k],
                                                    start=(k == 0), stop=(k == chunks - 1))
                        last.then_inc(mine.sem(name), 1)

                    if l in ATTN:
                        hs = [H1[:, k, :] for k in range(KC)]
                        h2 = [H2[:, k, :] for k in range(KC)]
                        for i, n, bank in ((1, "k", 2), (0, "q", 4)):
                            if n == "q":
                                pe.wait_ge(st["dve"].semaphore, st["dve"].before(b))
                            for c in range(KC):
                                o = i * D + c * P
                                linear(f"{n}{c}", PS[:, bank + c, :],
                                       [WQKVO[:, k, o:o + P] for k in range(KC)], hs, KC)
                        wv = WQKVO[:, :, 2 * D:3 * D].rearrange("p k (h r d) -> p k h r d", r=2, d=HD)
                        def values(half):
                            for j in range(BB // 2):
                                o = (half * BB // 2 + j) * SEQ
                                for r in range(2):
                                    for k in range(KC):
                                        last = nc.tensor.matmul(
                                            PS[64 * r:64 * r + 64, 6 + half, j * P:(j + 1) * P],
                                            H[:, k, o:o + SEQ], wv[:, k, :, r, :],
                                            start=(k == 0), stop=(k == KC - 1))
                            last.then_inc(mine.sem(f"v{half}"), 1)

                        def score(p):
                            after("pool", f"kbd{p}")
                            if p >= 2:
                                after("dve", f"sub{p - 2}")
                            for c in range(KC):
                                for r in range(2):
                                    o = (2 * p + r) * SEQ
                                    last = nc.tensor.matmul(
                                        PS[64 * r:64 * r + 64, 2 * (p % 2) + c, :], Q[:, c, o:o + SEQ],
                                        KBD[:, p % 2, c, r, :], start=True, stop=True)
                            last.then_inc(mine.sem(f"score{p}"), 1)

                        values(0)
                        after("act", "q1")
                        score(0)
                        values(1)
                        for p in range(1, PAIRS):
                            score(p)
                        for p in range(PAIRS):
                            after("pool", f"norm{p}")
                            if p > 0:
                                after("act", f"pt{p - 1}")
                            for h in range(HEADS // 2):
                                last = nc.tensor.transpose(
                                    PS[:, 4 + h // 4, (h % 4) * P:(h % 4 + 1) * P],
                                    S[:, p, 2 * h:2 * h + 2, :].rearrange("p h m -> p (h m)"), IDENT[:, :])
                            last.then_inc(mine.sem(f"tr{p}"), 1)
                            if p == PAIRS - 1:
                                next_mean(2)
                            after("act", f"pt{p}")
                            if p >= 2:
                                after("act", f"o{p - 2}")
                            else:
                                after("act", f"v{p}")
                                after("act", "v1")
                            for h in range(HEADS // 2):
                                q4 = 32 * (h % 4)
                                for r in range(2):
                                    o = (h // 4) * P + r * SEQ
                                    last = nc.tensor.matmul(
                                        PS[q4:q4 + 32, 6 + p % 2, o:o + SEQ],
                                        VBD[:, 2 * p + r, h, :, :].rearrange("p r d -> p (r d)"),
                                        PT[:, p % 2, h, r * SEQ:(r + 1) * SEQ], start=True, stop=True,
                                        tile_position=(0, q4))
                            last.then_inc(mine.sem(f"av{p}"), 1)
                        after("act", f"o{PAIRS - 1}")
                        for c in range(KC):
                            o = 3 * D + c * P
                            linear(f"proj{c}", PS[:, c, :], [WQKVO[:, k, o:o + P] for k in range(KC)],
                                   [AO[:, k, :] for k in range(KC)], KC)
                        norms(6, 2, "x")
                        for j in range(MLP // P):
                            linear(f"up{j}", PS[:, (4 + j) % 8, :],
                                   [W1A[:, k, j * P:(j + 1) * P] for k in range(KC)], h2, KC,
                                   (lambda k: after("dve", f"ln2_h{k}")) if j == 0 else None)
                        last = [None] * KC
                        for k in range(MLP // P):
                            after("act", f"gelu{k}")
                            for c in range(KC):
                                last[c] = nc.tensor.matmul(PS[:, 4 + c, :], W2A[:, k, c * P:(c + 1) * P], G[:, k, :],
                                                           start=(k == 0), stop=(k == MLP // P - 1))
                                if k == 0 and c == 0:
                                    after("act", "gelu1")
                        for c in range(KC):
                            last[c].then_inc(mine.sem(f"down{c}"), 1)
                        continue

                    cfg, ss = MAMBA[l], scan_sems[l]
                    N = cfg["states"]
                    hs = [H1[:, k, :] for k in range(KC)]
                    h2 = [H2[:, k, :] for k in range(KC)]

                    def project_in(d, chunks):
                        for j in chunks:
                            linear(f"in{d}_{j}", PS[:, (4 + j) % 8, :],
                                   [(W1 if l == 1 else W3[d])["inp"][:, k, j * P:(j + 1) * P] for k in range(KC)],
                                   hs, KC)

                    for d in range(2):
                        w = W1 if l == 1 else W3[d]
                        if d == 0:
                            project_in(0, range(DC))
                            pe.wait_ge(st["dve"].semaphore, st["dve"].before(b))
                            project_in(0, range(DC, 2 * DC))
                        elif not cfg["conv"]:
                            project_in(1, (DC, DC + 1))
                            after("dve", "x0_1")
                            project_in(1, (DC + 2, DC + 3))
                        xs = [XS[:, k, :] for k in range(DC)]
                        if cfg["conv"]:
                            after("act", f"xs{d}")
                            if d == 0:
                                after("act", f"in{d}_{2 * DC - 1}")
                            else:
                                after("dve", f"y0_{Y_ORDER[-1]}")
                            linear(f"rank{d}", PS[0:16, 3, :], [w["rank"][:, k, :] for k in range(DC)], xs, DC)
                            after("act", f"rank{d}")
                            for j in range(DC):
                                nc.tensor.matmul(PS[:, 4 + j, :], w["dt"][:, 0, j * P:(j + 1) * P], DTR,
                                                 start=True, stop=True).then_inc(mine.sem(f"dt{d}_{j}"), 1)
                        else:
                            after("act", f"in{d}_{DC - 1}")
                            for j in range(DC):
                                linear(f"dt{d}_{j}", PS[:, 4 + j, :],
                                       [w["dt"][:, k, j * P:(j + 1) * P] for k in range(DC)], xs, DC)
                            after("act", f"in{d}_{2 * DC - 1}")
                        linear(f"C{d}", PS[0:N, 1, :], [w["C"][:, k, :] for k in range(DC)], xs, DC)
                        for t in range(TT):
                            for k in range(DC):
                                last = nc.tensor.matmul(PS[:, 0, t * N:(t + 1) * N],
                                                        XS[:, k, t * P:(t + 1) * P], w["B"][:, k, :],
                                                        start=(k == 0), stop=(k == DC - 1))
                        last.then_inc(mine.sem(f"B{d}"), 1)
                        after("act", f"B{d}")
                        after("dve", f"C{d}")
                        for j in range(DC):
                            if j % 2 == 0:
                                after("dve", f"dtx{d}_{j // 2}")
                            for t in range(TT):
                                last = nc.tensor.transpose(PS[:, t, j * P:(j + 1) * P],
                                                           HB[:, j, t * P:(t + 1) * P], IDENT[:, :])
                        last.then_inc(mine.sem(f"dtx{d}"), 1)

                        runc = (b * 2 + d) * (N * DC) + CREDIT
                        run_act = (b * 2 + d) * (N * ACT_TILES) + CREDIT
                        run_dve = (b * 2 + d) * (N * (TT - ACT_TILES)) + CREDIT
                        run_pair = (b * 2 + d) * (N // 2 * PAIRED) + CREDIT

                        def transpose_input(n, j, parity):
                            if j == 0:
                                pe.wait_ge(ss["scaled_act"], run_act + (n + 1) * ACT_TILES)
                                pe.wait_ge(ss["scaled_dve"], run_dve + (n + 1) * (TT - ACT_TILES))
                            pe.wait_ge(ss["state_ready"], runc + n * DC + (j + 1 - DC))
                            for t in range(TT):
                                last = nc.tensor.transpose(PS[:, 4 + j, t * P:(t + 1) * P],
                                                           UT[:, parity, t, j * P:(j + 1) * P], IDENT[:, :])
                            last.then_inc(ss["input_ready"], 1)

                        def add_up(i, k, j, first, final):
                            pe.wait_ge(ss["prod_ready"], products(N, b * 2 + d, i, k, j))
                            nc.tensor.matmul(PS[:, j, :], IDENT[:, :], PR[:, j, :], start=first,
                                             stop=final).then_inc(ss["sum_done"], 1)

                        def add_up_pair(pair, j, first, final):
                            pe.wait_ge(ss["pair_added"], run_pair + pair * PAIRED + (j + 1))
                            nc.tensor.matmul(PS[:, j, :], IDENT[:, :], PR2[l][:, j, :], start=first,
                                             stop=final).then_inc(ss["pair_summed"], 1)

                        for j in range(DC):
                            transpose_input(0, j, 0)
                        after("act", f"dtx{d}")
                        after("dve", f"dtxt{d}")

                        def states(i, first, final):
                            for k in range(UN):
                                n = i * UN + k
                                more = not (final and k == UN - 1)
                                for j in range(DC):
                                    if more:
                                        transpose_input(n + 1, j, (k + 1) % 2)
                                    if j == PAIRED - 1 and k % 2 == 0 and not (first and k == 0):
                                        for c in range(PAIRED):
                                            add_up_pair(i * (UN // 2) + (k // 2 - 1), c, first and k == 2, False)
                                    if j >= PAIRED:
                                        add_up(i, k, j, first and k == 0, not more)
                            if final:
                                for c in range(PAIRED):
                                    add_up_pair(N // 2 - 1, c, False, True)

                        states(0, True, False)
                        with pe.Fori(1, N // UN - 1) as i:
                            states(i, False, False)
                        states(N // UN - 1, False, True)
                        pe.wait_ge(ss["state_ready"], runc + N * DC)
                        if d == 1:
                            next_mean(6)
                        elif not cfg["conv"]:
                            project_in(1, range(DC))
                        if d == 1 or not cfg["conv"]:
                            last = [None] * KC
                            for k in Y_ORDER:
                                after("dve", f"y{d}_{k}")
                                for c in range(KC):
                                    last[c] = nc.tensor.matmul(PS[:, 2 + 2 * d + c, :], w["out"][:, k, c * P:(c + 1) * P],
                                                               HB[:, k, :], start=(k == Y_ORDER[0]),
                                                               stop=(k == Y_ORDER[-1]))
                            for c in range(KC):
                                last[c].then_inc(mine.sem(f"out{d}_{c}"), 1)

                    m = WM1 if l == 1 else WM3
                    norms(0, 6, "x1_")
                    for j in range(cfg["hidden"]):
                        if j == 3:
                            after("act", "next_rstd")
                        for n, key, o in (("gate", "w1", 0), ("up", "w2", 1)):
                            linear(f"{n}{j}", PS[:, 2 * j + o, :],
                                   [m[key][:, k, j * P:(j + 1) * P] for k in range(KC)], h2, KC,
                                   (lambda k: after("dve", f"ln2_h{k}")) if j == 0 and n == "gate" else None)
                    after("dve", f"glu{cfg['hidden'] - 1}")
                    for c in range(KC):
                        linear(f"down{c}", PS[:, c, :],
                               [m["w3"][:, k, c * P:(c + 1) * P] for k in range(cfg["hidden"])],
                               [GLU[:, k, :] for k in range(cfg["hidden"])], cfg["hidden"])

        @block.scalar
        def _(act):
            f = nc.scalar.activation
            EXP_LN, GELU, SILU = 6, 10, 18

            def tables(which):
                act.add_instruction(mybir.InstLoadActFuncSet(
                    name=nc.get_next_instruction_name(), engine=act.engine, act_func_set_id=which, ins=[], outs=[]))

            act.wait_ge(dma_cond, 16 * 2)
            f(CSILU[:, :, :], COND[:, :, :], ACT.Silu).then_inc(cond_silu_ready, 1)
            tables(EXP_LN)
            act.wait_ge(const_ready, 3)
            act.wait_ge(dma_small, 16 * NSMALL)
            f(A1[:, :, :], A1[:, :, :], ACT.Exp)
            f(A3[:, :, :, :], A3[:, :, :, :], ACT.Exp).then_inc(decay_exp, 1)
            act.wait_ge(mods_ready, 1)

            for l in range(4):
                st = steps[l]
                mine = st["act"]
                act.sem_inc(mine.semaphore, BASE)
                if l in MAMBA:
                    ss = scan_sems[l]
                    for n in ("scaled_act", "decay_ready"):
                        act.sem_inc(ss[n], CREDIT)
                def square(xc, sq, done):
                    f(sq, xc, ACT.Square).then_inc(done, 1)

                def rsqrt(bank, rstd, done):
                    f(rstd, PS[:, bank, :], ACT.Ln, bias=EPSC[:, 0:1])
                    act.drain()
                    f(rstd, rstd, ACT.Exp, scale=-0.5).then_inc(done, 1)

                LN, NEXT = (LN_A, NEXT_A) if l in ATTN else (LN_M, NEXT_M)
                ld = lead[l]
                tables(EXP_LN)
                act.wait_ge(ld["dve"].semaphore, ld["dve"].lead("lead_centred"))
                square(LN[0], LN[1], ld["act"].sem("lead_square"))
                act.wait_ge(ld["pe"].semaphore, ld["pe"].lead("lead_var"))
                rsqrt(1, LN[2], ld["act"].sem("lead_rstd"))
                if l in MAMBA:
                    tables(SILU)

                with act.Fori(0, NBLK) as b:
                    def after(engine, name):
                        act.wait_ge(st[engine].semaphore, st[engine].count(b, name))

                    def norms(bank, next_bank):
                        after("dve", "next_centred")
                        square(NEXT[0], NEXT[1], mine.sem("next_square"))
                        after("pe", "next_var")
                        rsqrt(next_bank + 1, NEXT[2], mine.sem("next_rstd"))
                        for c in range(KC):
                            after("dve", f"ln2_centred{c}")
                            square(LN[0][:, c, :], LN[1][:, c, :], mine.sem(f"ln2_square{c}"))
                        after("pe", "ln2_var")
                        rsqrt(bank + 1, LN[2], mine.sem("ln2_rstd"))

                    if l in ATTN:
                        cfg = ATTN[l]
                        tables(EXP_LN)
                        for n, dst, bank in (("k", KF, 2), ("q", Q, 4)):
                            for c in range(KC):
                                after("pe", f"{n}{c}")
                                f(dst[:, c, :], PS[:, bank + c, :], ACT.Identity,
                                  bias=vec(cfg["b" + n], c)).then_inc(mine.sem(f"{n}{c}"), 1)
                        act.wait_ge(vbd_zeroed, 1 + l // 2)
                        for half in range(2):
                            after("pe", f"v{half}")
                            for r in range(2):
                                last = f(VBD[64 * r:64 * r + 64, half * 4:half * 4 + 4, :, r, :],
                                         PS[64 * r:64 * r + 64, 6 + half, :].rearrange(
                                             "p (b h d) -> p b h d", b=4, h=HEADS // 2), ACT.Copy)
                            last.then_inc(mine.sem(f"v{half}"), 1)

                        def exps(p):
                            after("dve", f"sub{p}")
                            f(S[:, p, :, :], S[:, p, :, :], ACT.Exp).then_inc(mine.sem(f"exp{p}"), 1)

                        exps(0)
                        for p in range(PAIRS):
                            if p + 1 < PAIRS:
                                exps(p + 1)
                            after("pe", f"tr{p}")
                            if p >= 2:
                                after("pe", f"av{p - 2}")
                            f(PT[:, p % 2, :, :], PS[:, 4:6, :].rearrange("p a (h n) -> p (a h) n", n=P),
                              ACT.Copy).then_inc(mine.sem(f"pt{p}"), 1)
                            after("pe", f"av{p}")
                            for c in range(KC):
                                last = f(AO[:, c, p * P:(p + 1) * P], PS[:, 6 + p % 2, c * P:(c + 1) * P],
                                         ACT.Identity, bias=vec(cfg["bv"], c))
                            last.then_inc(mine.sem(f"o{p}"), 1)
                        norms(6, 2)
                        tables(GELU)
                        for j in range(MLP // P):
                            after("pe", f"up{j}")
                            f(G[:, j, :], PS[:, (4 + j) % 8, :], ACT.Gelu,
                              bias=vec(cfg["b1"], j)).then_inc(mine.sem(f"gelu{j}"), 1)
                        continue

                    cfg, ss = MAMBA[l], scan_sems[l]
                    N = cfg["states"]
                    for d in range(2):
                        if d == 1:
                            tables(SILU)
                        decay = A1 if l == 1 else A3[:, d, :, :]
                        dt_bias = "L1_cond_dt_proj_b" if l == 1 else f"L3_cond_{cfg['dirs'][d]}dt_bias"
                        if d == 0 or not cfg["conv"]:
                            if d == 1:
                                after("dve", f"y0_{Y_ORDER[-1]}")
                            for j in range(2 * DC):
                                after("pe", f"in{d}_{j}")
                                if j >= DC:
                                    f(Z[:, j - DC, :], PS[:, j - DC, :], ACT.Silu).then_inc(mine.sem(f"in{d}_{j}"), 1)
                                elif cfg["conv"]:
                                    f(XPRE[:, j, :], PS[:, 4 + j, :], ACT.Copy).then_inc(mine.sem(f"in{d}_{j}"), 1)
                                else:
                                    f(XS[:, j, :], PS[:, 4 + j, :], ACT.Silu).then_inc(mine.sem(f"in{d}_{j}"), 1)
                        if cfg["conv"]:
                            if d == 1:
                                after("dve", f"y0_{Y_ORDER[-1]}")
                            for j in range(DC):
                                after("pool" if d else "dve", f"conv{d}_{j}")
                                last = f(XS[:, j, :], (XPRE if d else HB)[:, j, :], ACT.Silu, bias=vec("L1_cond_conv_b", j))
                            last.then_inc(mine.sem(f"xs{d}"), 1)
                            after("pe", f"rank{d}")
                            f(DTR[0:16, :], PS[0:16, 3, :], ACT.Copy).then_inc(mine.sem(f"rank{d}"), 1)
                        tables(EXP_LN)
                        for h in range(2):
                            two = slice(2 * h, 2 * h + 2)
                            for j in (2 * h, 2 * h + 1):
                                after("dve", f"relu{d}_{j}")
                                f(SOFT[:, j, :], PS[:, 4 + j, :], ACT.Abs, bias=vec(dt_bias, j))
                            act.drain()
                            f(SOFT[:, two, :], SOFT[:, two, :], ACT.Exp, scale=-1.0)
                            act.drain()
                            f(SOFT[:, two, :], SOFT[:, two, :], ACT.Ln,
                              bias=ONEC[:, 0:1]).then_inc(mine.sem(f"soft{d}_{h}"), 1)
                        after("pe", f"B{d}")
                        f(BT[:, :, 0:N], PS[:, 0, 0:TT * N].rearrange("p (t n) -> p t n", t=TT),
                          ACT.Copy).then_inc(mine.sem(f"B{d}"), 1)
                        runc = (b * 2 + d) * (N * DC) + CREDIT
                        lo = 1 - d

                        def decay_of(n, j):
                            act.wait_ge(ss["state_ready"], runc + n * DC + (j + 1 - DC))
                            seqs = DA[:, j, :].rearrange("p (b s) -> p b s", s=SEQ)
                            dts = DT[:, j, :].rearrange("p (b s) -> p b s", s=SEQ)
                            f(seqs[:, :, lo:lo + SEQ - 1], dts[:, :, lo:lo + SEQ - 1], ACT.Exp,
                              scale=decay[:, j, ds(n, 1)]).then_inc(ss["decay_ready"], 1)

                        def scale_input(n, parity, t):
                            act.wait_ge(ss["input_ready"], runc + n * DC - DC)
                            f(UT[:, parity, t, :], DTXT[:, t, :], ACT.Copy,
                              scale=BT[:, t, ds(n, 1)]).then_inc(ss["scaled_act"], 1)

                        for j in range(DC):
                            after("dve", f"dtx{d}_{j // 2}")
                            decay_of(0, j)
                        after("pe", f"dtx{d}")
                        for t in range(ACT_TILES):
                            f(UT[:, 0, t, :], PS[:, t, :], ACT.Copy,
                              scale=BT[:, t, 0:1]).then_inc(ss["scaled_act"], 1)
                        for t in range(ACT_TILES):
                            last = f(DTXT[:, t, :], PS[:, t, :], ACT.Copy)
                        last.then_inc(mine.sem(f"dtx{d}"), 1)
                        act.drain()

                        def decays(i, first, final):
                            for k in range(UN):
                                n = i * UN + k
                                for j in range(DC):
                                    if not (first and k == 0):
                                        decay_of(n, j)
                                    if j < ACT_TILES and not (final and k == UN - 1):
                                        scale_input(n + 1, (k + 1) % 2, j)

                        decays(0, True, False)
                        with act.Fori(1, N // UN - 1) as i:
                            decays(i, False, False)
                        decays(N // UN - 1, False, True)
                    norms(0, 6)
                    tables(SILU)
                    for j in range(cfg["hidden"]):
                        after("pe", f"gate{j}")
                        f(SG[:, j, :], PS[:, 2 * j, :], ACT.Silu).then_inc(mine.sem(f"silu{j}"), 1)

        @block.vector
        def _(dve):
            v = nc.vector
            v.memset(ZERO[:, :], 0.0)
            v.memset(EPSC[:, :], EPS)
            v.memset(ONEC[:, :], 1.0)
            v.memset(MEAN[:, :], 1.0 / D).then_inc(const_ready, 1)
            for i, s in enumerate(SITES):
                dve.wait_ge(mods_psum, i + 1)
                for kind, first in ((SHIFT, s["shift"]), (GATE, s["gate"]), (SCALE, s["scale"])):
                    if first is None:
                        continue
                    c = VCOL[s["b"]] + first
                    v.tensor_tensor(MOD[:, i, kind, :, :],
                                    PS[:, i, kind * KC * BATCH:(kind + 1) * KC * BATCH].rearrange(
                                        "p (c n) -> p c n", c=KC),
                                    VEC[:, c:c + KC].unsqueeze(2).broadcast_to([P, KC, BATCH]), ALU.add)
                dve.drain()
                v.tensor_scalar(MOD[:, i, SCALE, :, :], MOD[:, i, SCALE, :, :], 1.0, None, ALU.add)
                dve.drain()
                if s["norm"]:
                    wcol, bcol = (VEC[:, VCOL[n]:VCOL[n] + KC].unsqueeze(2).broadcast_to([P, KC, BATCH])
                                  for n in s["norm"])
                    product = TMP_A[:, 0:KC * BATCH].rearrange("p (c n) -> p c n", c=KC)
                    v.tensor_tensor(product, MOD[:, i, SCALE, :, :], bcol, ALU.mult)
                    dve.drain()
                    v.tensor_tensor(MOD[:, i, SHIFT, :, :], MOD[:, i, SHIFT, :, :], product, ALU.add)
                    v.tensor_tensor(MOD[:, i, SCALE, :, :], MOD[:, i, SCALE, :, :], wcol, ALU.mult)
                    dve.drain()
            dve.wait_ge(dma_small, 16 * NSMALL)
            v.tensor_scalar(KEYADD[:, :, :], KEYU8[:, :, :], -3e38, 10.0, ALU.mult, ALU.mult).then_inc(const_ready, 1)
            dve.wait_ge(decay_exp, 1)
            v.tensor_scalar(A1[:, :, :], A1[:, :, :], -1.0, None, ALU.mult)
            v.tensor_scalar(A3[:, :, :, :], A3[:, :, :, :], -1.0, None, ALU.mult)
            v.tensor_copy(ZERO[:, :], ZERO[:, :]).then_inc(mods_ready, 1)

            for l in range(4):
                st = steps[l]
                mine = st["dve"]
                if l in MAMBA:
                    for n in ("scaled_dve", "state_ready", "prod_vector", "pair_added"):
                        dve.sem_inc(scan_sems[l][n], CREDIT)
                if l == 0:
                    dve.wait_ge(dma_x, 16 * NBLK)

                def seqs(ap):
                    return ap.rearrange("p (b s) -> p b s", s=SEQ)

                def modulation(site, kind, c, b):
                    return MOD[:, site, kind, c, ds(b * BB, BB)].unsqueeze(2).broadcast_to([P, BB, SEQ])

                def centre(bank, xc, b, done):
                    for c in range(KC):
                        last = v.tensor_tensor(xc[:, c, :], X[:, c, ds(b * T, T)], PS[:, bank, :], ALU.subtract)
                        signal = done(c)
                        if signal is not None:
                            last.then_inc(signal, 1)

                def at_end(steps, name):
                    return lambda c: steps.sem(name) if c == KC - 1 else None

                def scale_norm(site, xc, h, b):
                    for c in range(KC):
                        v.tensor_tensor(seqs(h[:, c, :]), seqs(xc[:, c, :]), modulation(site, SCALE, c, b), ALU.mult)

                def modulate(site, rstd, h, b, done):
                    for c in range(KC):
                        v.tensor_tensor(h[:, c, :], h[:, c, :], rstd, ALU.mult)
                    dve.drain()
                    for c in range(KC):
                        last = v.tensor_tensor(seqs(h[:, c, :]), seqs(h[:, c, :]), modulation(site, SHIFT, c, b),
                                               ALU.add)
                        signal = done(c)
                        if signal is not None:
                            last.then_inc(signal, 1)

                LN, NEXT = (LN_A, NEXT_A) if l in ATTN else (LN_M, NEXT_M)
                ld = lead[l]
                dve.drain()
                dve.wait_ge(ld["pe"].semaphore, ld["pe"].lead("lead_mean"))
                centre(0, LN[0], 0, at_end(ld["dve"], "lead_centred"))
                dve.drain()
                scale_norm(2 * l, LN[0], H1, 0)
                dve.drain()
                dve.wait_ge(ld["act"].semaphore, ld["act"].lead("lead_rstd"))
                modulate(2 * l, LN[2], H1, 0, at_end(ld["dve"], "lead_h"))
                dve.drain()
                dve.sem_inc(mine.semaphore, BASE)
                with dve.Fori(0, NBLK) as b:
                    def after(engine, name):
                        dve.wait_ge(st[engine].semaphore, st[engine].count(b, name))

                    def xblk(c):
                        return X[:, c, ds(b * T, T)]

                    def mod(site, kind, c):
                        return modulation(site, kind, c, b)

                    nxt = (b + 1) % NBLK

                    def next_centre(bank):
                        after("pe", "next_mean")
                        centre(bank, NEXT[0], nxt, at_end(mine, "next_centred"))
                        dve.drain()
                        scale_norm(2 * l, NEXT[0], H1, nxt)

                    def norms(bank):
                        after("pe", "ln2_mean")
                        centre(bank, LN[0], b, lambda c: mine.sem(f"ln2_centred{c}"))
                        dve.drain()
                        scale_norm(2 * l + 1, LN[0], H2, b)
                        after("act", "next_rstd")
                        modulate(2 * l, NEXT[2], H1, nxt, at_end(mine, "next_h"))
                        after("act", "ln2_rstd")
                        modulate(2 * l + 1, LN[2], H2, b, lambda c: mine.sem(f"ln2_h{c}"))

                    def residual(name, c, bank, bias, site, tmp):
                        if site is None:
                            v.scalar_tensor_tensor(out=xblk(c), in0=PS[:, bank, :], scalar=bias, in1=xblk(c),
                                                   op0=ALU.add, op1=ALU.add).then_inc(mine.sem(name), 1)
                            return
                        v.scalar_tensor_tensor(out=seqs(tmp), in0=seqs(PS[:, bank, :]), scalar=bias,
                                               in1=mod(site, GATE, c), op0=ALU.add, op1=ALU.mult)
                        dve.drain()
                        v.tensor_tensor(xblk(c), xblk(c), tmp, ALU.add).then_inc(mine.sem(name), 1)
                        dve.drain()

                    if l in ATTN:
                        cfg = ATTN[l]
                        site = lambda i: 2 * l + i if cfg["gated"] else None
                        def sub(p):
                            after("pe", f"score{p}")
                            add = KEYADD[:, ds(b * PAIRS + p, 1), :] if l == 0 else CAUSAL[:, :].unsqueeze(1)
                            s = S[:, p, :, :]
                            v.scalar_tensor_tensor(
                                out=s, in0=PS[:, 2 * (p % 2):2 * (p % 2) + 2, :].rearrange("p c (h m) -> p (c h) m", m=SEQ),
                                scalar=float(HD) ** -0.5, in1=add.broadcast_to([P, HEADS, SEQ]),
                                op0=ALU.mult, op1=ALU.add)
                            dve.drain()
                            v.reduce_max(mx[:, :], s, AX.X)
                            dve.drain()
                            v.tensor_tensor(s, s, mx[:, :].unsqueeze(2).broadcast_to([P, HEADS, SEQ]),
                                            ALU.subtract).then_inc(mine.sem(f"sub{p}"), 1)

                        def normalise(p):
                            s = S[:, p, :, :]
                            after("act", f"exp{p}")
                            v.reduce_sum(sm[:, p, :], s, AX.X)
                            dve.drain()
                            v.reciprocal(inverse[:, p, :], sm[:, p, :]).then_inc(mine.sem(f"inverse{p}"), 1)

                        dve.drain()
                        sub(0)
                        for p in range(PAIRS):
                            if p + 1 < PAIRS:
                                sub(p + 1)
                            normalise(p)
                        next_centre(2)
                        for c in range(KC):
                            after("pe", f"proj{c}")
                            residual(f"x{c}", c, c, vec(cfg["bo"], c), site(0), TMP_A)
                        norms(6)
                        for c in range(KC):
                            after("pe", f"down{c}")
                            residual(f"end{c}", c, 4 + c, vec(cfg["b2"], c), site(1), TMP_A)
                        dve.drain()
                        continue

                    cfg, ss = MAMBA[l], scan_sems[l]
                    N = cfg["states"]
                    for d in range(2):
                        pre = cfg["dirs"][d]
                        dt_bias = "L1_cond_dt_proj_b" if l == 1 else f"L3_cond_{pre}dt_bias"
                        skip = "L1_cond_Dp" if l == 1 else f"L3_cond_{pre}D"
                        if cfg["conv"] and d == 0:
                            for tap in range(3, -1, -1):
                                shift = 3 - tap
                                for j in range(DC):
                                    col = VCONV + j * 4 + tap
                                    wt = VEC[:, col:col + 1]
                                    src, dst = seqs(XPRE[:, j, :]), seqs(HB[:, j, :])
                                    if shift == 0:
                                        after("act", f"in0_{j}")
                                        v.tensor_scalar(HB[:, j, :], XPRE[:, j, :], wt, None, ALU.mult)
                                        continue
                                    last = v.scalar_tensor_tensor(
                                        out=dst[:, :, shift:SEQ], in0=src[:, :, 0:SEQ - shift], scalar=wt,
                                        in1=dst[:, :, shift:SEQ], op0=ALU.mult, op1=ALU.add)
                                    if shift == 3:
                                        last.then_inc(mine.sem(f"conv{d}_{j}"), 1)
                                if shift < 3:
                                    dve.drain()
                        for h in range(2):
                            two = slice(2 * h, 2 * h + 2)
                            for j in (2 * h, 2 * h + 1):
                                after("pe", f"dt{d}_{j}")
                                v.tensor_scalar(DT[:, j, :], PS[:, 4 + j, :], vec(dt_bias, j), 0.0,
                                                ALU.add, ALU.max).then_inc(mine.sem(f"relu{d}_{j}"), 1)
                            dve.drain()
                            if h == 1:
                                after("pe", f"C{d}")
                                v.tensor_copy(CROW[0:N, :], PS[0:N, 1, :]).then_inc(mine.sem(f"C{d}"), 1)
                            after("act", f"soft{d}_{h}")
                            v.tensor_tensor(DT[:, two, :], DT[:, two, :], SOFT[:, two, :], ALU.add)
                            dve.drain()
                            v.tensor_tensor(HB[:, two, :], DT[:, two, :], XS[:, two, :],
                                            ALU.mult).then_inc(mine.sem(f"dtx{d}_{h}"), 1)
                        first = 0 if d == 0 else SEQ - 1
                        v.memset(DA.rearrange("p j (b s) -> p (j b) s", s=SEQ)[:, :, first:first + 1], 0.0)
                        dve.drain()
                        after("act", f"B{d}")
                        after("pe", f"dtx{d}")
                        for t in range(ACT_TILES, TT):
                            v.tensor_scalar(UT[:, 0, t, :], PS[:, t, :], BT[:, t, 0:1], None,
                                            ALU.mult).then_inc(ss["scaled_dve"], 1)
                        for t in range(ACT_TILES, TT):
                            last = v.tensor_copy(DTXT[:, t, :], PS[:, t, :])
                        last.then_inc(mine.sem(f"dtxt{d}"), 1)
                        dve.drain()

                        runc = (b * 2 + d) * (N * DC) + CREDIT

                        run_vector = (b * 2 + d) * (N // 2 * VECTOR_PRODUCTS) + CREDIT

                        def scale_input(n, parity):
                            dve.wait_ge(ss["input_ready"], runc + n * DC - DC)
                            for t in range(ACT_TILES, TT):
                                v.tensor_scalar(UT[:, parity, t, :], DTXT[:, t, :], BT[:, t, ds(n, 1)], None,
                                                ALU.mult).then_inc(ss["scaled_dve"], 1)

                        def states(i, final):
                            for k in range(UN):
                                n = i * UN + k
                                for j in range(DC):
                                    dve.wait_ge(ss["input_ready"], runc + n * DC + (j + 1))
                                    dve.wait_ge(ss["decay_ready"], runc + n * DC + (j + 1))
                                    if k % 2 or j >= VECTOR_PRODUCTS:
                                        dve.wait_ge(ss["prod_ready"], products(N, b * 2 + d, i, k - 1, j))
                                    else:
                                        dve.wait_ge(ss["prod_vector"], run_vector
                                                    + (i * (UN // 2) + k // 2) * VECTOR_PRODUCTS
                                                    + (j + 1 - VECTOR_PRODUCTS))
                                    step = slice(None, None, -1) if d else slice(None)
                                    v.tensor_tensor_scan(HB[:, j, step], DA[:, j, step], PS[:, 4 + j, step],
                                                         0.0, ALU.mult, ALU.add).then_inc(ss["state_ready"], 1)
                                    if j == 0 and not (final and k == UN - 1):
                                        scale_input(n + 1, (k + 1) % 2)
                                    if k % 2 and j == max(VECTOR_PRODUCTS, 1):
                                        for c in range(VECTOR_PRODUCTS):
                                            multiply_odd(i, k, c)
                                    if k % 2 and 0 <= j - (DC - PAIRED) < PAIRED:
                                        add_pair(i, k, j - (DC - PAIRED))

                        def multiply_odd(i, k, j):
                            dve.wait_ge(ss["state_ready"], runc + (i * UN + k) * DC + (j + 1))
                            dve.wait_ge(c_loaded[l][k // 2], (b * 2 + d) * (N // UN * 16) + i * 16 + 16)
                            dve.wait_ge(ss["pair_summed"], (b * 2 + d) * (N // 2 * PAIRED)
                                        + (i * (UN // 2) + k // 2) * PAIRED + (CREDIT + j + 1 - PAIRED))
                            v.tensor_tensor(PR2[l][:, j, :], HB[:, j, :], CB[l][:, k // 2, 1, :],
                                            ALU.mult).then_inc(ss["prod_vector"], 1)

                        def add_pair(i, k, j):
                            q = k
                            if j < VECTOR_PRODUCTS:
                                q = k - 1
                                dve.wait_ge(ss["prod_vector"], run_vector
                                            + (i * (UN // 2) + k // 2) * VECTOR_PRODUCTS + (j + 1))
                            dve.wait_ge(ss["prod_ready"], products(N, b * 2 + d, i, q, j))
                            v.tensor_tensor(PR2[l][:, j, :], PR2[l][:, j, :], PR[:, j, :],
                                            ALU.add).then_inc(ss["pair_added"], 1)

                        with dve.Fori(0, N // UN - 1) as i:
                            states(i, False)
                        states(N // UN - 1, True)

                        into = YS if l == 1 and d == 0 else HB
                        dve.drain()
                        for j in Y_ORDER:
                            if j == PAIRED:
                                dve.wait_ge(ss["sum_done"], (b * 2 + d) * (N * SINGLE) + (CREDIT + N * SINGLE))
                            elif j == 0:
                                dve.wait_ge(ss["pair_summed"],
                                            (b * 2 + d) * (N // 2 * PAIRED) + (CREDIT + N // 2 * PAIRED))
                            last = v.scalar_tensor_tensor(out=into[:, j, :], in0=XS[:, j, :], scalar=vec(skip, j),
                                                          in1=PS[:, j, :], op0=ALU.mult, op1=ALU.add)
                            if l == 1 and d == 0:
                                last.then_inc(mine.sem(f"y{d}_{j}"), 1)
                        dve.drain()
                        if l == 1 and d == 0:
                            continue
                        if l == 1:
                            for j in range(DC):
                                v.tensor_tensor(HB[:, j, :], HB[:, j, :], YS[:, j, :], ALU.add)
                            dve.drain()
                        for j in Y_ORDER:
                            v.tensor_tensor(HB[:, j, :], HB[:, j, :], Z[:, j, :],
                                            ALU.mult).then_inc(mine.sem(f"y{d}_{j}"), 1)
                        if d == 1:
                            next_centre(6)
                        for c in range(KC):
                            after("pe", f"out{d}_{c}")
                            residual(f"x{d}_{c}", c, 2 + 2 * d + c, ZERO[:, 0:1], 2 * l, TMP_M)
                    norms(0)
                    for j in range(cfg["hidden"]):
                        after("pe", f"up{j}")
                        after("act", f"silu{j}")
                        v.tensor_tensor(GLU[:, j, :], SG[:, j, :], PS[:, 2 * j + 1, :],
                                        ALU.mult).then_inc(mine.sem(f"glu{j}"), 1)
                    for c in range(KC):
                        after("pe", f"down{c}")
                        residual(f"end{c}", c, c, ZERO[:, 0:1], 2 * l + 1, TMP_M)
                    dve.drain()

        @block.gpsimd
        def _(pool):
            g = nc.gpsimd
            g.memset(CAUSAL[:, :], 0.0)
            pool.drain()
            for r in range(2):
                g.affine_select(out=CAUSAL[64 * r:64 * r + 64, :], in_=CAUSAL[64 * r:64 * r + 64, :],
                                compare_op=ALU.is_ge, fill=-1e30, base=0, pattern=[[-1, SEQ]], channel_multiplier=1)
            pool.drain()
            g.memset(VBD, 0.0).then_inc(vbd_zeroed, 1)
            pool.sem_inc(const_ready, 1)

            pool.wait_ge(mods_psum, len(SITES))
            g.memset(W1["dt"], 0.0)
            g.memset(DTR, 0.0)
            pool.drain()
            pool.sem_inc(rank_zeroed, 1)

            for l in range(4):
                st = steps[l]
                mine = st["pool"]
                pool.sem_inc(mine.semaphore, BASE)
                if l == 2:
                    pool.wait_ge(steps[1]["dve"].semaphore, steps[1]["dve"].before(NBLK))
                    g.memset(VBD, 0.0).then_inc(vbd_zeroed, 1)
                if l in MAMBA:
                    pool.sem_inc(scan_sems[l]["prod_ready"], CREDIT)
                with pool.Fori(0, NBLK) as b:
                    if l in ATTN:
                        for p in range(PAIRS):
                            if p >= 2:
                                pool.wait_ge(st["pe"].semaphore, st["pe"].count(b, f"score{p - 2}"))
                            for c in range(KC):
                                if p == 0:
                                    pool.wait_ge(st["act"].semaphore, st["act"].count(b, f"k{c}"))
                                for r in range(2):
                                    o = (2 * p + r) * SEQ
                                    last = g.tensor_tensor(
                                        KBD[:, p % 2, c, r, :].rearrange("p (h m) -> p h m", m=SEQ),
                                        KF[:, c, o:o + SEQ].unsqueeze(1).broadcast_to([P, HPC, SEQ]),
                                        HMASK[:, :].unsqueeze(2).broadcast_to([P, HPC, SEQ]), ALU.mult)
                            last.then_inc(mine.sem(f"kbd{p}"), 1)
                        for p in range(PAIRS):
                            pool.wait_ge(st["dve"].semaphore, st["dve"].count(b, f"inverse{p}"))
                            g.tensor_tensor(S[:, p, :, :], S[:, p, :, :],
                                            inverse[:, p, :].unsqueeze(2).broadcast_to([P, HEADS, SEQ]),
                                            ALU.mult).then_inc(mine.sem(f"norm{p}"), 1)
                        continue
                    cfg, ss = MAMBA[l], scan_sems[l]
                    N = cfg["states"]
                    if cfg["conv"]:
                        for j in range(DC):
                            pool.wait_ge(st["act"].semaphore, st["act"].count(b, f"in0_{j}"))
                            total, part = CONV[:, 0, :], CONV[:, 1, :]

                            def weight(tap, count):
                                col = VCONV + j * 4 + tap
                                return VEC[:, col:col + 1].unsqueeze(2).broadcast_to([P, BB, count])

                            def by_sequence(ap, first, count):
                                return ap.rearrange("p (b s) -> p b s", s=SEQ)[:, :, first:first + count]

                            g.tensor_tensor(by_sequence(total, 0, SEQ), by_sequence(XPRE[:, j, :], 0, SEQ),
                                            weight(3, SEQ), ALU.mult)
                            for shift in (1, 2, 3):
                                count = SEQ - shift
                                g.tensor_tensor(by_sequence(part, 0, count),
                                                by_sequence(XPRE[:, j, :], shift, count),
                                                weight(3 - shift, count), ALU.mult)
                                pool.drain()
                                into = total
                                if shift == 3:
                                    pool.wait_ge(st["dve"].semaphore, st["dve"].count(b, f"conv0_{j}"))
                                    into = XPRE[:, j, :]
                                last = g.tensor_tensor(by_sequence(into, 0, count), by_sequence(total, 0, count),
                                                       by_sequence(part, 0, count), ALU.add)
                                if shift < 3:
                                    pool.drain()
                            last = g.tensor_copy(by_sequence(XPRE[:, j, :], SEQ - 3, 3),
                                                 by_sequence(total, SEQ - 3, 3))
                            last.then_inc(mine.sem(f"conv1_{j}"), 1)
                            pool.drain()
                    for d in range(2):
                        run_c = (b * 2 + d) * (N // UN * 16) + 16
                        runc = (b * 2 + d) * (N * DC) + CREDIT
                        run_single = (b * 2 + d) * (N * SINGLE) + CREDIT
                        run_pair = (b * 2 + d) * (N // 2 * PAIRED) + CREDIT
                        with pool.Fori(0, N // UN) as i:
                            for k in range(UN):
                                n = i * UN + k
                                if k % 2 == 0:
                                    pool.wait_ge(c_loaded[l][k // 2], run_c + i * 16)
                                for j in range(DC):
                                    pool.wait_ge(ss["state_ready"], runc + n * DC + (j + 1))
                                    if k % 2 and j < VECTOR_PRODUCTS:
                                        continue
                                    into = PR[:, j, :]
                                    if j >= PAIRED:
                                        pool.wait_ge(ss["sum_done"], run_single + n * SINGLE + (j + 1 - DC))
                                    elif k % 2 == 0:
                                        pool.wait_ge(ss["pair_added"],
                                                     run_pair + (i * (UN // 2) + k // 2) * PAIRED + (j + 1 - PAIRED))
                                    else:
                                        pool.wait_ge(ss["pair_summed"],
                                                     run_pair + (i * (UN // 2) + k // 2) * PAIRED + (j + 1 - PAIRED))
                                        into = PR2[l][:, j, :]
                                    g.tensor_tensor(into, HB[:, j, :], CB[l][:, k // 2, k % 2, :],
                                                    ALU.mult).then_inc(ss["prod_ready"], 1)


_TRANSPOSED = ("L0_cond_w_adaln1", "L0_cond_w_adaln2", "L0_cond_wq", "L0_cond_wk", "L0_cond_wv",
               "L0_cond_wo", "L0_cond_w1", "L0_cond_w2")
_PLAIN = ("L1_cond_adaln1_W", "L1_cond_adaln2_W", "L1_cond_in_proj_W", "L1_cond_x_proj_W", "L1_cond_dt_proj_W",
          "L1_cond_A_log", "L1_cond_out_proj_W", "L1_cond_w1", "L1_cond_w2", "L1_cond_w3", "L2_cond_Wqkv",
          "L2_cond_Wproj", "L2_cond_W1", "L2_cond_W2", "L2_cond_Wada", "L3_cond_adaln_mamba_w",
          "L3_cond_adaln_mlp_w", "L3_cond_mlp_w1", "L3_cond_mlp_w2", "L3_cond_mlp_w3", "L3_cond_fwd_in_w",
          "L3_cond_fwd_xproj_w", "L3_cond_fwd_A_log", "L3_cond_fwd_out_w", "L3_cond_bwd_in_w",
          "L3_cond_bwd_xproj_w", "L3_cond_bwd_A_log", "L3_cond_bwd_out_w")


def kernel(**inputs):
    import concourse.bacc as bacc
    from concourse.bass_utils import run_bass_kernel_spmd

    arrays = {k: np.asarray(v) for k, v in inputs.items()}
    laid = {k: arrays[k].T for k in _TRANSPOSED}
    laid |= {k: arrays[k] for k in _PLAIN}
    laid["x_t"] = arrays["x"].reshape(TOKENS, D).T
    laid["cond_t"] = arrays["cond_1024"].T
    laid["mask"] = arrays["mask_BxS_bf0"]
    columns = [arrays[n].reshape(c, P).T for n, c in VECTORS]
    columns.append(arrays["L1_cond_conv_w"].reshape(DC, P, 4).transpose(1, 0, 2).reshape(P, DC * 4))
    laid["vectors"] = np.concatenate(columns, axis=1)
    laid["ident"] = np.eye(P, dtype=np.float32)
    laid["head_mask"] = np.kron(np.eye(HPC), np.ones((HD, 1))).astype(np.float32)

    nc = bacc.Bacc("TRN2", target_bir_lowering=False, num_devices=1)
    feeds, aps = {}, {}
    for name, value in laid.items():
        value = np.ascontiguousarray(value)
        feeds[f"in_{name}"] = value
        aps[name] = nc.dram_tensor(f"in_{name}", value.shape, mybir.dt.from_np(value.dtype), kind="ExternalInput").ap()
    out = nc.dram_tensor("out_t", (D, TOKENS), mybir.dt.float32, kind="ExternalOutput").ap()
    c_rows = nc.dram_tensor("c_rows", (2, 64, T), mybir.dt.float32, kind="Internal").ap()
    build(nc, aps, out, c_rows)
    r = run_bass_kernel_spmd(nc, [feeds], core_ids=[0])
    return np.ascontiguousarray(r.results[0]["out_t"].T).reshape(BATCH, SEQ, D)
```
